# Optimizing a Trainium2 kernel written in Bass

```python
import numpy as np
import jax
import jax.numpy as jnp

def _softmax(x, axis=-1):
    return jax.nn.softmax(x, axis=axis)

def _gelu(x):
    return jax.nn.gelu(x, approximate=True)

def _silu(x):
    return jax.nn.silu(x)

def _sigmoid(x):
    return jax.nn.sigmoid(x)

def _layernorm(x, axis=-1, eps=1e-05):
    m = jnp.mean(x, axis=axis, keepdims=True)
    v = jnp.var(x, axis=axis, keepdims=True)
    return (x - m) / jnp.sqrt(v + eps)

def _scatter_add(tgt, idx, src, axis=0):
    return tgt.at[idx].add(src)

def _segment_sum(src, seg, n):
    return jax.ops.segment_sum(src, seg, n)
kernel_name = 'mk_gnn_resnorm_d2_gnn_r16_ec6294'

def setup_inputs(seed: int=0):
    np.random.seed(seed)
    _w = jnp.asarray

    def _rec_inputs():
        import jax
        import jax.numpy as jnp
        _gk = jax.random.key(seed)
        x = -8.776e-05 + 1 * jax.random.normal(jax.random.fold_in(_gk, 1), (6250, 256), jnp.float32)
        src = jax.random.randint(jax.random.fold_in(_gk, 2), (100000,), 0, 6250, jnp.int32)
        dst = jnp.minimum((6250 * jax.random.uniform(jax.random.fold_in(_gk, 3), (100000,)) ** 2.0).astype(jnp.int32), 99999)
        _o = jnp.argsort(dst, stable=True)
        src = src[_o]
        dst = dst[_o]
        edge_type_200 = jax.random.randint(jax.random.fold_in(_gk, 13), (100000,), 0, 200, jnp.int32)
        return (x, src, dst, edge_type_200)
    x, src, dst, edge_type_200 = _rec_inputs()

    def _L0_gnn_setup():
        import jax, jax.numpy as jnp
        import numpy as np
        N = 1250
        E = 20000
        D_IN = 256
        HID = 64
        HEADS = 4
        D_OUT = 256
        EPS = 1e-05
        SLOPE = 0.2

        def _gat(x, src, dst, W, a_src, a_dst, b, heads, ch, concat):
            n = x.shape[0]
            h = (x @ W).reshape(n, heads, ch)
            es = (h * a_src).sum(-1)
            ed = (h * a_dst).sum(-1)
            e = jax.nn.leaky_relu(es[src] + ed[dst], SLOPE)
            m = jax.ops.segment_max(e, dst, num_segments=n)
            w = jnp.exp(e - m[dst])
            den = jax.ops.segment_sum(w, dst, num_segments=n)
            alpha = w / den[dst]
            msg = h[src] * alpha[:, :, None]
            out = jax.ops.segment_sum(msg, dst, num_segments=n)
            out = out.reshape(n, heads * ch) if concat else out.mean(axis=1)
            return out + b

        def _layernorm(x, g, b):
            mu = x.mean(-1, keepdims=True)
            v = ((x - mu) ** 2).mean(-1, keepdims=True)
            return (x - mu) * jax.lax.rsqrt(v + EPS) * g + b
        key = jax.random.key(seed)
        ks = jax.random.split(key, 10)

        def glorot(k, shape):
            fan_in, fan_out = (shape[0], int(np.prod(shape[1:])))
            s = np.sqrt(2.0 / (fan_in + fan_out)).astype(np.float32)
            return jax.random.normal(k, shape, dtype=jnp.float32) * s
        x = jax.random.normal(ks[0], (N, D_IN), dtype=jnp.float32)
        edge_index = jax.random.randint(ks[1], (2, E), 0, N, dtype=jnp.int64)
        return {'x': x, 'edge_index': edge_index, 'W1': glorot(ks[2], (D_IN, HEADS * HID)), 'a1_src': glorot(ks[3], (HEADS, HID)), 'a1_dst': glorot(ks[4], (HEADS, HID)), 'b1': jnp.zeros((HEADS * HID,), jnp.float32), 'ln_g': jnp.ones((HEADS * HID,), jnp.float32), 'ln_b': jnp.zeros((HEADS * HID,), jnp.float32), 'W2': glorot(ks[5], (HEADS * HID, D_OUT)), 'a2_src': glorot(ks[6], (1, D_OUT)), 'a2_dst': glorot(ks[7], (1, D_OUT)), 'b2': jnp.zeros((D_OUT,), jnp.float32)}
    _L0_gnn_all = _L0_gnn_setup()
    _L0_gnn_in = {k: v for k, v in _L0_gnn_all.items() if k in ('W1', 'a1_src', 'a1_dst', 'b1', 'ln_g', 'ln_b', 'W2', 'a2_src', 'a2_dst', 'b2')}
    del _L0_gnn_all

    def _L1_gnn_setup():
        import jax, jax.numpy as jnp
        import numpy as np
        N, D, E, R = (3125, 256, 40000, 200)
        if __name__ == '__main__':
            out = reference(**setup_inputs())
            print(out.shape, out.dtype)
        key = jax.random.key(seed)
        ks = jax.random.split(key, 12)

        def xavier(k, shape, gain=np.sqrt(2.0)):
            fan_in, fan_out = (shape[0], shape[1])
            bound = gain * np.sqrt(6.0 / (fan_in + fan_out))
            return jax.random.uniform(k, shape, jnp.float32, -bound, bound)
        return {'h': jax.random.normal(ks[0], (N, D), jnp.float32), 'rel_emb': jax.random.normal(ks[1], (R, D), jnp.float32) * 0.1, 'weight_neighbor': xavier(ks[2], (D, D)), 'a': xavier(ks[3], (3 * D, 1)), 'W3': xavier(ks[4], (3 * D, 3 * D)), 'loop_weight': xavier(ks[5], (D, D)), 'evolve_loop_weight': xavier(ks[6], (D, D)), 'src': jax.random.randint(ks[7], (E,), 0, N, jnp.int32), 'dst': jax.random.randint(ks[8], (E,), 0, N, jnp.int32), 'etype': jax.random.randint(ks[9], (E,), 0, R, jnp.int32)}
    _L1_gnn_all = _L1_gnn_setup()
    _L1_gnn_in = {k: v for k, v in _L1_gnn_all.items() if k in ('rel_emb', 'weight_neighbor', 'a', 'W3', 'loop_weight', 'evolve_loop_weight')}
    del _L1_gnn_all
    return {'x': x, 'src': src, 'dst': dst, 'edge_type_200': edge_type_200, 'L0_gnn_W1': _L0_gnn_in['W1'], 'L0_gnn_a1_src': _L0_gnn_in['a1_src'], 'L0_gnn_a1_dst': _L0_gnn_in['a1_dst'], 'L0_gnn_b1': _L0_gnn_in['b1'], 'L0_gnn_ln_g': _L0_gnn_in['ln_g'], 'L0_gnn_ln_b': _L0_gnn_in['ln_b'], 'L0_gnn_W2': _L0_gnn_in['W2'], 'L0_gnn_a2_src': _L0_gnn_in['a2_src'], 'L0_gnn_a2_dst': _L0_gnn_in['a2_dst'], 'L0_gnn_b2': _L0_gnn_in['b2'], 'L1_gnn_rel_emb': _L1_gnn_in['rel_emb'], 'L1_gnn_weight_neighbor': _L1_gnn_in['weight_neighbor'], 'L1_gnn_a': _L1_gnn_in['a'], 'L1_gnn_W3': _L1_gnn_in['W3'], 'L1_gnn_loop_weight': _L1_gnn_in['loop_weight'], 'L1_gnn_evolve_loop_weight': _L1_gnn_in['evolve_loop_weight']}

def reference(x, src, dst, edge_type_200, L0_gnn_W1, L0_gnn_a1_src, L0_gnn_a1_dst, L0_gnn_b1, L0_gnn_ln_g, L0_gnn_ln_b, L0_gnn_W2, L0_gnn_a2_src, L0_gnn_a2_dst, L0_gnn_b2, L1_gnn_rel_emb, L1_gnn_weight_neighbor, L1_gnn_a, L1_gnn_W3, L1_gnn_loop_weight, L1_gnn_evolve_loop_weight):
    import jax
    import jax.numpy as jnp

    def _L0_gnn_ref(x, edge_index, W1, a1_src, a1_dst, b1, ln_g, ln_b, W2, a2_src, a2_dst, b2):
        import jax, jax.numpy as jnp
        import numpy as np
        N = 1250
        E = 20000
        D_IN = 256
        HID = 64
        HEADS = 4
        D_OUT = 256
        EPS = 1e-05
        SLOPE = 0.2

        def _gat(x, src, dst, W, a_src, a_dst, b, heads, ch, concat):
            n = x.shape[0]
            h = (x @ W).reshape(n, heads, ch)
            es = (h * a_src).sum(-1)
            ed = (h * a_dst).sum(-1)
            e = jax.nn.leaky_relu(es[src] + ed[dst], SLOPE)
            m = jax.ops.segment_max(e, dst, num_segments=n)
            w = jnp.exp(e - m[dst])
            den = jax.ops.segment_sum(w, dst, num_segments=n)
            alpha = w / den[dst]
            msg = h[src] * alpha[:, :, None]
            out = jax.ops.segment_sum(msg, dst, num_segments=n)
            out = out.reshape(n, heads * ch) if concat else out.mean(axis=1)
            return out + b

        def _layernorm(x, g, b):
            mu = x.mean(-1, keepdims=True)
            v = ((x - mu) ** 2).mean(-1, keepdims=True)
            return (x - mu) * jax.lax.rsqrt(v + EPS) * g + b
        loops = jnp.arange(N, dtype=edge_index.dtype)
        src = jnp.concatenate([edge_index[0], loops])
        dst = jnp.concatenate([edge_index[1], loops])
        h = _gat(x, src, dst, W1, a1_src, a1_dst, b1, HEADS, HID, True)
        h = jax.nn.relu(_layernorm(h, ln_g, ln_b))
        out = _gat(h, src, dst, W2, a2_src, a2_dst, b2, 1, D_OUT, False)
        return out

    def _L1_gnn_ref(h, rel_emb, weight_neighbor, a, W3, loop_weight, evolve_loop_weight, src, dst, etype):
        import jax, jax.numpy as jnp
        import numpy as np
        N, D, E, R = (3125, 256, 40000, 200)
        if __name__ == '__main__':
            out = reference(**setup_inputs())
            print(out.shape, out.dtype)
        n, d = h.shape
        e = src.shape[0]
        in_deg = jax.ops.segment_sum(jnp.ones((e,), h.dtype), dst, num_segments=n)
        loop_message = jnp.where((in_deg > 0)[:, None], h @ loop_weight, h @ evolve_loop_weight)
        W = (W3 @ a)[:, 0]
        w_src, w_dst, w_rel = (W[:d], W[d:2 * d], W[2 * d:])
        rel_e = rel_emb[etype]
        score = h[src] @ w_src + h[dst] @ w_dst + rel_e @ w_rel
        alpha = jnp.exp(jax.nn.leaky_relu(score))[:, None]
        alpha = alpha / jnp.sum(alpha, axis=1, keepdims=True)
        msg = (h[src] + rel_e) @ weight_neighbor * alpha
        agg = jax.ops.segment_sum(msg, dst, num_segments=n)
        node_repr = jax.nn.relu(agg) + loop_message
        return node_repr
    edge_index = jnp.stack([src, dst])
    x = _layernorm(x + _L0_gnn_ref(x, edge_index, L0_gnn_W1, L0_gnn_a1_src, L0_gnn_a1_dst, L0_gnn_b1, L0_gnn_ln_g, L0_gnn_ln_b, L0_gnn_W2, L0_gnn_a2_src, L0_gnn_a2_dst, L0_gnn_b2), axis=-1)
    x = _layernorm(x + _L1_gnn_ref(x, L1_gnn_rel_emb, L1_gnn_weight_neighbor, L1_gnn_a, L1_gnn_W3, L1_gnn_loop_weight, L1_gnn_evolve_loop_weight, src, dst, edge_type_200), axis=-1)
    return x

_drawn_inputs = setup_inputs


def setup_inputs(seed=0):
    import zlib

    import numpy as np

    out = dict(_drawn_inputs(seed))
    spreads = {'L0_gnn_b1': (0.0, 0.1),
     'L0_gnn_ln_g': (1.0, 0.2),
     'L0_gnn_ln_b': (0.0, 0.1),
     'L0_gnn_b2': (0.0, 0.1)}
    factors = {}
    for name, (base, spread) in spreads.items():
        noise = np.random.default_rng([zlib.crc32(name.encode()), seed]).standard_normal(out[name].shape)
        drawn = base * np.exp(spread * noise) if base else spread * noise
        out[name] = jnp.asarray(drawn.astype(out[name].dtype))
    for name, factor in factors.items():
        out[name] = (out[name] * factor).astype(out[name].dtype)
    return out
```

```python
from contextlib import ExitStack

import concourse.bass as bass
from concourse import mybir

F32 = mybir.dt.float32
BF16 = mybir.dt.bfloat16
I32 = mybir.dt.int32
ALU = mybir.AluOpType
ACT = mybir.ActivationFunctionType
AX_X = mybir.AxisListType.X

P = 128
N, D, E = 6250, 256, 100000
NB = -(-N // P)
NFULL, NLAST = N // P, N % P
TILES = -(-E // P)
TPR = 7
RW = TPR * P
ROWS = -(-TILES // TPR)
EFULL, ELAST = E // RW, E % RW
STEPS = TILES + NB - 1
U = 10
TURNS = STEPS // U
HALF = STEPS // 2
NCH = -(-STEPS // P)
SELF = 1250
SELFB = -(-SELF // P)
HEADS, HID = 4, 64
REL = 200
LC = 8
BIG = 1e30
PAD_DST = 8191
NODE_U = 7
NODE_TURNS = NB // NODE_U
EPS = 1e-5
assert TURNS * U == STEPS and HALF * 2 == STEPS and HALF <= 512
assert NODE_TURNS * NODE_U == NB and EFULL == ROWS - 1 and ROWS * TPR >= TILES
assert RW % LC == 0 and (RW // LC) % 2 == 0


class Chain:

    def __init__(self, eng, sem, base=0):
        self.eng, self.sem, self.base, self.n = eng, sem, base, 0

    def __call__(self, ins):
        ins.then_inc(self.sem, 1)
        self.n += 1
        self.eng.wait_ge(self.sem, self.base + self.n)


def after(eng, sem, value):
    if not (isinstance(value, int) and value <= 0):
        eng.wait_ge(sem, value)


def settled(eng, passed):
    eng.sem_inc(passed, 1)


def turns(eng, n, body):
    body(0)
    with eng.Fori(1, n - 1) as i:
        body(i)
    body(n - 1)


def program(nc, a, out):
    with ExitStack() as top:
        k = Kernel(nc, a, out, top)
        edge_structure(k)
        first_projection(k)
        with ExitStack() as ctx:
            acc = gat_layer(k, ctx, HEADS, k.h1_d)
            gat_epilogue_1(k, acc)
        with ExitStack() as ctx:
            acc = gat_layer(k, ctx, 1, k.h2_d)
            gat_epilogue_2(k, acc)
        with ExitStack() as ctx:
            acc = relation_layer(k, ctx)
            relation_epilogue(k, acc)


class Kernel:

    def __init__(self, nc, a, out, ctx):
        self.nc, self.a, self.out, self.ctx = nc, a, out, ctx
        self.names = 0
        self.sems = []
        self.passed = ctx.enter_context(nc.semaphore("waits_passed"))
        sb = self.sb
        self.h1_d = nc.dram_tensor("h1_rows", (NB * P, D), F32, kind="Internal").ap()
        self.h2_d = nc.dram_tensor("h2_rows", (NB * P, D), F32, kind="Internal").ap()
        self.x1_d = nc.dram_tensor("x1_rows", (NB * P, D), F32, kind="Internal").ap()
        self.dlo_d = nc.dram_tensor("dst_local_by_step", (NCH * P, P), BF16, kind="Internal").ap()
        self.elo_d = nc.dram_tensor("relation_by_step", (NCH * P, P), BF16, kind="Internal").ap()
        self.slo_d = nc.dram_tensor("src_low_by_column", (RW, ROWS), BF16, kind="Internal").ap()
        self.iota_row = sb(ctx, "iota_row", [P, RW])
        self.iota_part = sb(ctx, "iota_part", [P, 1])
        self.tile_no = sb(ctx, "tile_no", [P, TPR])
        self.iota_nb = sb(ctx, "iota_nb", [P, NB], BF16)
        self.ident = sb(ctx, "ident", [P, P])
        self.steptile = sb(ctx, "steptile", [ROWS, TPR, STEPS])
        self.src_step = sb(ctx, "src_step", [P, STEPS], I32)
        self.dst_step = sb(ctx, "dst_step", [P, STEPS])
        self.et_step = sb(ctx, "et_step", [P, STEPS])
        self.first_step = sb(ctx, "first_step", [P, STEPS])
        self.block_of = sb(ctx, "block_of", [1, STEPS], I32)
        self.src_hi = sb(ctx, "src_hi", [ROWS, RW], BF16)
        self.first_row = sb(ctx, "first_row", [ROWS, RW], BF16)
        self.last_row = sb(ctx, "last_row", [ROWS, RW], BF16)
        self.srel = sb(ctx, "srel", [P, 2])
        self.node_s = sb(ctx, "node_s", [P, 2 * HEADS, NB])

    def sb(self, ctx, name, shape, dt=F32):
        return ctx.enter_context(self.nc.sbuf_tensor(self.fresh(name), shape, dt))

    def psum(self, ctx, name, shape, dt=F32):
        return ctx.enter_context(self.nc.psum_tensor(self.fresh(name), shape, dt))

    def sem(self, name):
        self.sems.append(self.nc.alloc_semaphore(name=self.fresh(name)))
        return self.sems[-1]

    def phase(self):
        if self.sems:
            self.nc.clear_and_free_semaphores(self.sems)
            self.nc.all_engine_barrier()
        self.sems = []

    def fresh(self, name):
        self.names += 1
        return f"{name}_{self.names}"


def edge_structure(k):
    k.phase()
    nc, sb, sem = k.nc, k.sb, k.sem
    with ExitStack() as ctx:
        ints = {n: sb(ctx, f"{n}_int", [ROWS, RW], I32) for n in ("src", "dst", "et")}
        flt = {n: sb(ctx, f"{n}_flt", [ROWS, RW]) for n in ("src", "dst", "et")}
        low_i = sb(ctx, "low_i", [ROWS, RW], I32)
        low_f = sb(ctx, "low_f", [ROWS, RW])
        first_f = sb(ctx, "first_f", [ROWS, RW])
        prev_i = sb(ctx, "prev_i", [ROWS, 1], I32)
        next_i = sb(ctx, "next_i", [ROWS, 1], I32)
        prev_f = sb(ctx, "prev_f", [ROWS, 1])
        next_f = sb(ctx, "next_f", [ROWS, 1])
        hi_i = sb(ctx, "hi_i", [ROWS, TPR], I32)
        first_of_tile = sb(ctx, "first_of_tile", [ROWS, TPR])
        begun = sb(ctx, "begun", [ROWS, TPR, STEPS], BF16)
        ones = sb(ctx, "ones_bf", [ROWS, P], BF16)
        tile_of = sb(ctx, "tile_of", [P, STEPS])
        block_f = sb(ctx, "block_f", [P, STEPS])
        low_t = sb(ctx, "low_t", [P, TPR, ROWS], BF16)
        dst_t = sb(ctx, "dst_t", [P, NCH, P], BF16)
        et_t = sb(ctx, "et_t", [P, NCH, P], BF16)
        pair = [k.psum(ctx, f"pair{i}", [P, 2, 512]) for i in range(3)]
        tps = [k.psum(ctx, f"tps{i}", [P, P]) for i in range(2)]
        s_fill, s_in, s_iota = sem("filled"), sem("edges_in"), sem("iotas")
        s_dve, s_ge, s_one = sem("dve"), sem("begun"), sem("ones")
        s_cnt, s_sel, s_exp, s_evac = sem("counted"), sem("steptile"), sem("expanded"), sem("evacuated")
        s_dst = sem("dst_local")
        s_dstf, s_low, s_tp, s_tc, s_lowd = sem("dst_step"), sem("low"), sem("turned"), sem("turned_out"), sem("low_out")
        names = ("src", "dst", "et")
        with nc.Block() as block:

            @block.gpsimd
            def _(pool):
                nc.gpsimd.memset(ints["src"][:, :], 0).then_inc(s_fill, 1)
                nc.gpsimd.memset(ints["et"][:, :], 0).then_inc(s_fill, 1)
                nc.gpsimd.memset(ints["dst"][:, :], PAD_DST).then_inc(s_fill, 1)
                nc.gpsimd.memset(prev_i[:, :], -1).then_inc(s_fill, 1)
                nc.gpsimd.memset(next_i[:, :], PAD_DST + 1).then_inc(s_fill, 1)
                nc.gpsimd.memset(dst_t[:, :, :], 0.0).then_inc(s_fill, 1)
                nc.gpsimd.memset(et_t[:, :, :], 0.0).then_inc(s_fill, 1)
                io = dict(allow_small_or_imprecise_dtypes=True)
                nc.gpsimd.iota(k.iota_row[:, :], pattern=[[1, RW]], base=0, channel_multiplier=0, **io).then_inc(s_iota, 1)
                nc.gpsimd.iota(k.iota_part[:, :], pattern=[[0, 1]], base=0, channel_multiplier=1, **io).then_inc(s_iota, 1)
                nc.gpsimd.iota(k.tile_no[:, :], pattern=[[1, TPR]], base=0, channel_multiplier=TPR, **io).then_inc(s_iota, 1)
                nc.gpsimd.iota(k.iota_nb[:, :], pattern=[[1, NB]], base=0, channel_multiplier=0, **io).then_inc(s_iota, 1)

            @block.sync
            def _(sp):
                sp.wait_ge(s_fill, 5)
                for n, src in (("dst", k.a["dst"]), ("src", k.a["src"]), ("et", k.a["edge_type_200"])):
                    sp.dma_start(ints[n][0:EFULL, :], src[0:EFULL * RW].rearrange("(p j) -> p j", j=RW)).then_inc(s_in, 16)
                    sp.dma_start(ints[n][EFULL:ROWS, 0:ELAST],
                                 src[EFULL * RW:E].rearrange("(p j) -> p j", p=1)).then_inc(s_in, 16)
                dst_rows = k.a["dst"][0:EFULL * RW].rearrange("(p j) -> p j", j=RW)
                with nc.allow_non_contiguous_dma(reason="one element of each partition"):
                    sp.dma_start(prev_i[1:ROWS, :], dst_rows[:, RW - 1:RW]).then_inc(s_in, 16)
                    sp.dma_start(next_i[0:EFULL - 1, :], dst_rows[1:EFULL, 0:1]).then_inc(s_in, 16)
                    sp.dma_start(next_i[EFULL - 1:EFULL, :],
                                 k.a["dst"][EFULL * RW:EFULL * RW + 1].rearrange("(p j) -> p j", p=1)).then_inc(s_in, 16)
                sp.wait_ge(s_tc, TPR)
                sp.dma_start(k.slo_d.rearrange("(g p) r -> p g r", p=P), low_t[:, :, :]).then_inc(s_lowd, 16)
                sp.wait_ge(s_tc, TPR + NCH)
                sp.dma_start(k.dlo_d.rearrange("(c p) e -> p c e", p=P), dst_t[:, :, :]).then_inc(s_lowd, 16)
                sp.wait_ge(s_tc, TPR + 2 * NCH)
                sp.dma_start(k.elo_d.rearrange("(c p) e -> p c e", p=P), et_t[:, :, :]).then_inc(s_lowd, 16)
                sp.wait_ge(s_lowd, 48)

            @block.vector
            def _(dve):
                link = Chain(dve, s_dve)
                dve.wait_ge(s_iota, 4)
                nc.vector.memset(ones[:, :], 1.0).then_inc(s_one, 1)
                nc.vector.tensor_scalar(k.ident[:, :], k.iota_row[:, 0:P], k.iota_part[:, 0:1], None,
                                        ALU.is_equal).then_inc(s_one, 1)
                dve.wait_ge(s_in, 16 * 9)
                link(nc.vector.tensor_scalar(hi_i[:, :], ints["dst"][:, 0:RW:P], 7, None, ALU.logical_shift_right))
                link(nc.vector.tensor_tensor(first_of_tile[:, :], hi_i[:, :], k.tile_no[0:ROWS, :], ALU.add))
                for g in range(TPR):
                    nc.vector.tensor_scalar(begun[:, g, :], k.iota_row[0:ROWS, 0:STEPS], first_of_tile[:, g:g + 1],
                                            None, ALU.is_ge).then_inc(s_ge, 1)
                link(nc.vector.tensor_scalar(low_i[:, :], ints["src"][:, :], P - 1, None, ALU.bitwise_and))
                nc.vector.tensor_copy(low_f[:, :], low_i[:, :]).then_inc(s_low, 1)
                dve.wait_ge(s_low, 1)
                link(nc.vector.tensor_scalar(low_i[:, :], ints["src"][:, :], 7, None, ALU.logical_shift_right))
                link(nc.vector.tensor_copy(k.src_hi[:, :], low_i[:, :]))
                for n in names:
                    nc.vector.tensor_copy(flt[n][:, :], ints[n][:, :]).then_inc(s_dstf, 1)
                link(nc.vector.tensor_copy(prev_f[:, :], prev_i[:, :]))
                link(nc.vector.tensor_copy(next_f[:, :], next_i[:, :]))
                dve.wait_ge(s_dstf, 3)
                df = flt["dst"]
                link(nc.vector.tensor_tensor(first_f[:, 1:RW], df[:, 1:RW], df[:, 0:RW - 1], ALU.not_equal))
                nc.vector.tensor_tensor(first_f[:, 0:1], df[:, 0:1], prev_f[:, :], ALU.not_equal).then_inc(s_dstf, 1)
                dve.wait_ge(s_dstf, 4)
                link(nc.vector.tensor_copy(k.first_row[:, :], first_f[:, :]))
                link(nc.vector.tensor_copy(k.last_row[:, 0:RW - 1], first_f[:, 1:RW]))
                link(nc.vector.tensor_tensor(k.last_row[:, RW - 1:RW], df[:, RW - 1:RW], next_f[:, :], ALU.not_equal))
                dve.wait_ge(s_cnt, 1)
                link(nc.vector.tensor_scalar(tile_of[:, :].rearrange("p (a s) -> p a s", a=2), pair[0][:, :, 0:HALF],
                                             -1.0, 0.0, ALU.add, ALU.max))
                link(nc.vector.tensor_tensor(block_f[:, :], k.iota_row[:, 0:STEPS], tile_of[:, :], ALU.subtract))
                link(nc.vector.tensor_copy(k.block_of[:, :], block_f[0:1, :]))
                for g in range(TPR):
                    nc.vector.tensor_scalar(k.steptile[:, g, :], tile_of[0:ROWS, :], k.tile_no[0:ROWS, g:g + 1], None,
                                            ALU.is_equal).then_inc(s_sel, 1)
                dve.wait_ge(s_exp, 1)
                nc.vector.scalar_tensor_tensor(
                    out=k.dst_step[:, :].rearrange("p (a s) -> p a s", a=2),
                    in0=block_f[:, :].rearrange("p (a s) -> p a s", a=2), scalar=-float(P),
                    in1=pair[1][:, :, 0:HALF], op0=ALU.mult, op1=ALU.add).then_inc(s_dst, 1)

            @block.tensor
            def _(pe):
                pe.wait_ge(s_one, 2)
                for g in range(TPR):
                    pe.wait_ge(s_ge, g + 1)
                    for h in range(2):
                        last = nc.tensor.matmul(pair[0][:, h, 0:HALF], ones[:, :],
                                                begun[:, g, h * HALF:(h + 1) * HALF],
                                                start=(g == 0), stop=(g == TPR - 1))
                last.then_inc(s_cnt, 1)
                pe.wait_ge(s_low, 1)
                for g in range(TPR):
                    if g >= 2:
                        pe.wait_ge(s_tc, g - 1)
                    nc.tensor.transpose(tps[g % 2][:, 0:ROWS], low_f[:, g * P:(g + 1) * P],
                                        k.ident[0:ROWS, 0:ROWS]).then_inc(s_tp, 1)
                pe.wait_ge(s_dstf, 4)
                pe.wait_ge(s_sel, TPR)
                for q, x in enumerate((flt["dst"], flt["src"], flt["et"], first_f)):
                    if q == 3:
                        pe.wait_ge(s_dst, 1)
                    for g in range(TPR):
                        for h in range(2):
                            last = nc.tensor.matmul(pair[(q + 1) % 3][:, h, 0:HALF], x[:, g * P:(g + 1) * P],
                                                    k.steptile[:, g, h * HALF:(h + 1) * HALF],
                                                    start=(g == 0), stop=(g == TPR - 1))
                    last.then_inc(s_exp, 1)
                pe.wait_ge(s_evac, 2)
                for m, x in enumerate((k.dst_step, k.et_step)):
                    for c in range(NCH):
                        n, at = min(P, STEPS - c * P), TPR + m * NCH + c
                        pe.wait_ge(s_tc, at - 1)
                        nc.tensor.transpose(tps[at % 2][0:n, :], x[:, c * P:c * P + n],
                                            k.ident[:, :]).then_inc(s_tp, 1)

            @block.scalar
            def _(act):
                for g in range(TPR):
                    act.wait_ge(s_tp, g + 1)
                    nc.scalar.activation(low_t[:, g, :], tps[g % 2][:, 0:ROWS], ACT.Copy).then_inc(s_tc, 1)
                for q, y in enumerate((None, k.src_step, k.et_step, k.first_step)):
                    if y is None:
                        continue
                    act.wait_ge(s_exp, q + 1)
                    nc.scalar.activation(y[:, :].rearrange("p (a s) -> p a s", a=2),
                                         pair[(q + 1) % 3][:, :, 0:HALF], ACT.Copy).then_inc(s_evac, 1)
                act.wait_ge(s_fill, 7)
                for m, y in enumerate((dst_t, et_t)):
                    for c in range(NCH):
                        n, at = min(P, STEPS - c * P), TPR + m * NCH + c
                        act.wait_ge(s_tp, at + 1)
                        nc.scalar.activation(y[0:n, c, :], tps[at % 2][0:n, :], ACT.Copy).then_inc(s_tc, 1)



def pe_project(k, pe, xin, slots, s_x, tps, s_tp, s_xt, xt, w, ops, s_mm, s_out, chunks, per=1):
    nc = k.nc

    def body(i):
        def turn_block(u):
            n = i * NODE_U + u
            s_x(pe, i, u)
            after(pe, s_xt, n - 1 if u else n)
            for c, (lo, wd) in enumerate(chunks):
                last = nc.tensor.transpose(tps[u % 2][0:wd, c, :], xin[:, u % slots, lo:lo + wd], k.ident[:, :])
            last.then_inc(s_tp, 1)

        def multiply(u):
            n = i * NODE_U + u
            pe.wait_ge(s_xt, n + 1)
            after(pe, s_out, per * (n - 1 if u else n))
            for group in w:
                o, cs = group
                for m, (c, wt) in enumerate(cs):
                    wd = chunks[c][1]
                    last = nc.tensor.matmul(ops[u % 2][:, o:o + wt.shape[-1]], xt[u % 2][0:wd, c, :], wt,
                                            start=(m == 0), stop=(m == len(cs) - 1))
            last.then_inc(s_mm, 1)

        for u in range(NODE_U):
            turn_block(u)
            if u:
                multiply(u - 1)
        multiply(NODE_U - 1)

    turns(pe, NODE_TURNS, body)


def rows_of(dram, n):
    return dram[bass.ds(n * P, P), :] if not isinstance(n, int) else dram[n * P:(n + 1) * P, :]


def first_projection(k):
    k.phase()
    nc, sb, sem = k.nc, k.sb, k.sem
    W = D + 2 * HEADS
    with ExitStack() as ctx:
        w = sb(ctx, "w1x", [P, 2, W])
        av = sb(ctx, "a_rows", [P, 2, D])
        wa = sb(ctx, "w1_times_a", [P, 2, D])
        xin = sb(ctx, "xin", [P, NODE_U, D])
        hout = sb(ctx, "hout", [P, NODE_U, D])
        xt = [sb(ctx, f"xt{i}", [P, 2, P]) for i in range(2)]
        tps = [k.psum(ctx, f"tps{i}", [P, 2, P]) for i in range(2)]
        ops = [k.psum(ctx, f"ops{i}", [P, 512]) for i in range(2)]
        s_w, s_wx, s_dve, s_last = sem("weights_in"), sem("weights_ready"), sem("dve"), sem("last_block_zero")
        s_x = [sem(f"x_in{u}") for u in range(NODE_U)]
        s_st = [sem(f"h_stored{u}") for u in range(NODE_U)]
        s_tp, s_xt, s_mm, s_out, s_ev = sem("turned"), sem("turned_copied"), sem("product"), sem("product_read"), sem("h_ready")
        with nc.Block() as block:

            @block.sync
            def _(sp):
                sp.dma_start(w[:, :, 0:D], k.a["L0_gnn_W1"].rearrange("(c p) n -> p c n", p=P)).then_inc(s_w, 16)
                for m, n in enumerate(("L0_gnn_a1_src", "L0_gnn_a1_dst")):
                    sp.dma_start(av[:, m, :], k.a[n].rearrange("h c -> (h c)").partition_broadcast(P)).then_inc(s_w, 16)

                def body(i):
                    for u in range(NODE_U):
                        n = i * NODE_U + u
                        after(sp, s_tp, n - NODE_U + 1)
                        if isinstance(n, int) and n == NB - 1:
                            sp.wait_ge(s_last, 1)
                            sp.dma_start(xin[0:NLAST, u, :], k.a["x"][n * P:N, :]).then_inc(s_x[u], 16)
                        else:
                            sp.dma_start(xin[:, u, :], rows_of(k.a["x"], n)).then_inc(s_x[u], 16)
                turns(sp, NODE_TURNS, body)

            @block.vector
            def _(dve):
                link = Chain(dve, s_dve)
                dve.wait_ge(s_w, 48)
                for m in range(2):
                    link(nc.vector.tensor_tensor(wa[:, :, :], w[:, :, 0:D],
                                                 av[:, m:m + 1, :].to_broadcast([P, 2, D]), ALU.mult))
                    nc.vector.tensor_reduce(w[:, :, D + m * HEADS:D + (m + 1) * HEADS],
                                            wa[:, :, :].rearrange("p c (h e) -> p c h e", h=HEADS), AX_X,
                                            ALU.add).then_inc(s_wx, 1)
                    dve.wait_ge(s_wx, m + 1)

                def copy(o, i):
                    return nc.vector.tensor_copy(o[:, :, :], i[:, :, :])

                def body(i):
                    for u in range(NODE_U):
                        n = i * NODE_U + u
                        if isinstance(n, int) and n == NB - NODE_U:
                            dve.wait_ge(s_tp, NB - NODE_U)
                            nc.vector.memset(xin[:, NODE_U - 1, :], 0.0).then_inc(s_last, 1)
                        dve.wait_ge(s_tp, n + 1)
                        after(dve, s_mm, n - 1 if u else n)
                        copy(xt[u % 2], tps[u % 2]).then_inc(s_xt, 1)
                turns(dve, NODE_TURNS, body)

            @block.tensor
            def _(pe):
                pe.wait_ge(s_wx, 2)
                pe_project(k, pe, xin, NODE_U, lambda e, i, u: e.wait_ge(s_x[u], 16 * (i + 1)), tps, s_tp, s_xt, xt,
                           [(0, [(c, w[:, c, :]) for c in range(2)])], ops, s_mm, s_out, [(0, P), (P, P)])

            @block.scalar
            def _(act):
                def body(i):
                    for u in range(NODE_U):
                        n = i * NODE_U + u
                        act.wait_ge(s_mm, n + 1)
                        after(act, s_st[u], 16 * i)
                        nc.scalar.activation(hout[:, u, :], ops[u % 2][:, 0:D], ACT.Copy).then_inc(s_ev, 1)
                        nc.scalar.activation(k.node_s[:, :, n:n + 1] if isinstance(n, int) else k.node_s[:, :, bass.ds(n, 1)],
                                             ops[u % 2][:, D:W].rearrange("p (c o) -> p c o", o=1), ACT.Copy).then_inc(s_out, 1)
                        act.wait_ge(s_ev, n + 1)
                        act.dma_start(rows_of(k.h1_d, n), hout[:, u, :]).then_inc(s_st[u], 16)
                turns(act, NODE_TURNS, body)
                for u in range(NODE_U):
                    act.wait_ge(s_st[u], 16 * NODE_TURNS)



def split_table(k, link, node, rest, tab):
    nc = k.nc
    link(nc.vector.tensor_copy(tab[0], node))
    link(nc.vector.tensor_tensor(rest, node, tab[0], ALU.subtract))
    link(nc.vector.tensor_copy(tab[1], rest))
    link(nc.vector.tensor_tensor(rest, rest, tab[1], ALU.subtract))
    link(nc.vector.tensor_copy(tab[2], rest))


def lookup_src(k, C, node, out_row):
    k.phase()
    nc, sb, sem = k.nc, k.sb, k.sem
    NL = RW // LC // 2
    with ExitStack() as ctx:
        tab = sb(ctx, "src_table", [P, 3, C, NB], BF16)
        rest = sb(ctx, "src_rest", [P, C, NB])
        low = [sb(ctx, f"low{h}", [P, LC * ROWS], BF16) for h in range(2)]
        hot = [sb(ctx, f"hot{h}", [P, LC * ROWS], BF16) for h in range(2)]
        mask = [sb(ctx, f"mask{h}", [ROWS, LC, NB], BF16) for h in range(2)]
        prod = [sb(ctx, f"prod{h}", [ROWS, LC, C, NB]) for h in range(2)]
        stride = 256 if C > 1 else 64
        ps = [k.psum(ctx, f"cand{h}", [P, LC, stride]) for h in range(2)]
        s_low = [sem(f"low_in{h}") for h in range(2)]
        s_dve, s_tab, s_hot, s_mask, s_mm, s_prod, s_red = (sem("dve"), sem("table"), sem("hot"), sem("mask"),
                                                            sem("candidates"), sem("picked"), sem("summed"))
        with nc.Block() as block:

            @block.sync
            def _(sp):
                def body(i):
                    for h in range(2):
                        j = (2 * i + h) * LC
                        after(sp, s_hot, 2 * i + h - 1)
                        src = k.slo_d[bass.ds(j, LC), :] if not isinstance(j, int) else k.slo_d[j:j + LC, :]
                        sp.dma_start(low[h][:, :], src.rearrange("j r -> (j r)").partition_broadcast(P)).then_inc(s_low[h], 16)
                turns(sp, NL, body)

            @block.vector
            def _(dve):
                link = Chain(dve, s_dve)
                split_table(k, link, node, rest[:, :, :], [tab[:, m, :, :] for m in range(3)])
                nc.vector.memset(rest[:, 0, 0:1], 0.0).then_inc(s_tab, 1)

                def body(i):
                    for h in range(2):
                        n = 2 * i + h
                        j = n * LC
                        dve.wait_ge(s_low[h], 16 * (i + 1))
                        after(dve, s_mm, n - 1)
                        nc.vector.tensor_scalar(hot[h][:, :], low[h][:, :], k.iota_part[:, 0:1], None,
                                                ALU.is_equal).then_inc(s_hot, 1)
                        after(dve, s_prod, n - 1)
                        hi = k.src_hi[:, j:j + LC] if isinstance(j, int) else k.src_hi[:, bass.ds(j, LC)]
                        nc.vector.tensor_tensor(mask[h][:, :, :], hi.unsqueeze(2).to_broadcast([ROWS, LC, NB]),
                                                k.iota_nb[0:ROWS, :].unsqueeze(1).to_broadcast([ROWS, LC, NB]),
                                                ALU.is_equal).then_inc(s_mask, 1)
                    for h in range(2):
                        n = 2 * i + h
                        j = n * LC
                        dve.wait_ge(s_mm, n + 1)
                        dve.wait_ge(s_mask, n + 1)
                        after(dve, s_red, n - 1)
                        nc.vector.tensor_tensor(
                            prod[h][:, :, :, :], ps[h][0:ROWS, :, 0:C * NB].rearrange("r j (c b) -> r j c b", c=C),
                            mask[h][:, :, :].unsqueeze(2).to_broadcast([ROWS, LC, C, NB]), ALU.mult).then_inc(s_prod, 1)
                        dve.wait_ge(s_prod, n + 1)
                        o = out_row[:, :, j:j + LC] if isinstance(j, int) else out_row[:, :, bass.ds(j, LC)]
                        nc.vector.tensor_reduce(o.rearrange("r c j -> r j c"), prod[h][:, :, :, :], AX_X,
                                                ALU.add).then_inc(s_red, 1)
                turns(dve, NL, body)

            @block.tensor
            def _(pe):
                pe.wait_ge(s_tab, 1)

                def body(i):
                    for h in range(2):
                        n = 2 * i + h
                        pe.wait_ge(s_hot, n + 1)
                        after(pe, s_prod, n - 1)
                        for j in range(LC):
                            for m in range(3):
                                last = nc.tensor.matmul(ps[h][0:ROWS, j, 0:C * NB],
                                                        hot[h][:, j * ROWS:(j + 1) * ROWS],
                                                        tab[:, m, :, :].rearrange("p c b -> p (c b)"),
                                                        start=(m == 0), stop=(m == 2))
                        last.then_inc(s_mm, 1)
                turns(pe, NL, body)


def lookup_dst(k, C, node, out_step, rel=None):
    k.phase()
    nc, sb, sem = k.nc, k.sb, k.sem
    H = U // 2
    kinds = 1 if rel is None else 3
    with ExitStack() as ctx:
        tab = sb(ctx, "dst_table", [P, NB, 3, C], BF16)
        rest = sb(ctx, "dst_rest", [P, C, NB])
        rtab = sb(ctx, "rel_table", [P, 2, 3], BF16)
        part2 = sb(ctx, "iota_part2", [P, 1])
        low = [sb(ctx, f"dlow{h}", [P, 2, H * P], BF16) for h in range(2)]
        hot = [sb(ctx, f"dhot{h}", [P, kinds, H * P], BF16) for h in range(2)]
        ps = [k.psum(ctx, f"vals{h}", [P, H, 16]) for h in range(2)]
        s_low = [sem(f"dlow_in{h}") for h in range(2)]
        s_dve, s_tab, s_hot, s_mm, s_red = sem("dve"), sem("table"), sem("hot"), sem("values"), sem("summed")
        dmas = 1 if rel is None else 2
        with nc.Block() as block:

            @block.sync
            def _(sp):
                def body(i):
                    for h in range(2):
                        s = (2 * i + h) * H
                        after(sp, s_hot, (2 * i + h - 1) * kinds)
                        for q, d in enumerate((k.dlo_d, k.elo_d)[0:dmas]):
                            src = d[s:s + H, :] if isinstance(s, int) else d[bass.ds(s, H), :]
                            sp.dma_start(low[h][:, q, :],
                                         src.rearrange("s e -> (s e)").partition_broadcast(P)).then_inc(s_low[h], 16)
                turns(sp, TURNS, body)

            @block.vector
            def _(dve):
                link = Chain(dve, s_dve)
                split_table(k, link, node, rest[:, :, :],
                            [tab[:, :, m, :].rearrange("p b c -> p c b") for m in range(3)])
                if rel is not None:
                    link(nc.vector.tensor_scalar(part2[:, :], k.iota_part[:, :], float(P), None, ALU.add))
                    split_table(k, link, rel, rest[:, 0, 0:2], [rtab[:, :, m] for m in range(3)])
                nc.vector.memset(rest[:, 0, 0:1], 0.0).then_inc(s_tab, 1)

                def body(i):
                    for h in range(2):
                        n = 2 * i + h
                        dve.wait_ge(s_low[h], 16 * dmas * (i + 1))
                        after(dve, s_mm, n - 1)
                        for q, (x, p) in enumerate(((0, k.iota_part), (1, k.iota_part), (1, part2))[0:kinds]):
                            nc.vector.tensor_scalar(hot[h][:, q, :], low[h][:, x, :], p[:, 0:1], None,
                                                    ALU.is_equal).then_inc(s_hot, 1)
                    for h in range(2):
                        n = 2 * i + h
                        s = n * H
                        dve.wait_ge(s_mm, n + 1)
                        o = out_step[:, s:s + H, :] if isinstance(s, int) else out_step[:, bass.ds(s, H), :]
                        nc.vector.tensor_reduce(o, ps[h][:, :, 0:3 * C].rearrange("p s (m c) -> p s c m", m=3), AX_X,
                                                ALU.add).then_inc(s_red, 1)
                turns(dve, TURNS, body)

            @block.tensor
            def _(pe):
                pe.wait_ge(s_tab, 1)

                def body(i):
                    for h in range(2):
                        n = 2 * i + h
                        pe.wait_ge(s_hot, (n + 1) * kinds)
                        after(pe, s_red, n - 1)
                        for u in range(H):
                            s = n * H + u
                            b = pe.value_load(k.block_of[0:1, s:s + 1] if isinstance(s, int) else k.block_of[0:1, bass.ds(s, 1)],
                                              min_val=0, max_val=NB - 1)
                            last = nc.tensor.matmul(ps[h][:, u, 0:3 * C], hot[h][:, 0, u * P:(u + 1) * P],
                                                    tab[:, bass.ds(b, 1), :, :].rearrange("p b m c -> p (b m c)"),
                                                    start=True, stop=(rel is None))
                            for q in range(1, kinds):
                                last = nc.tensor.matmul(ps[h][:, u, 0:3], hot[h][:, q, u * P:(u + 1) * P],
                                                        rtab[:, q - 1, :], start=False, stop=(q == kinds - 1))
                        last.then_inc(s_mm, 1)
                turns(pe, TURNS, body)


def segment_max(k, C, es, most):
    k.phase()
    nc, sb, sem = k.nc, k.sb, k.sem
    with ExitStack() as ctx:
        ahead = sb(ctx, "ahead", [ROWS, C, RW])
        cut = [sb(ctx, f"cut{d}", [ROWS, RW]) for d in range(2)]
        on = sb(ctx, "handed_on", [ROWS, 2 * C])
        cutmin = sb(ctx, "cutmin", [ROWS, 1])
        on_t = sb(ctx, "handed_on_t", [C, 2, ROWS])
        run = sb(ctx, "run", [C, 2, ROWS + 1])
        carry = sb(ctx, "carry", [ROWS, 2, C])
        tps = [k.psum(ctx, f"tps{i}", [P, P]) for i in range(3)]
        s_dve, s_on, s_tp, s_run, s_cp = sem("dve"), sem("handed_on"), sem("turned"), sem("run"), sem("carry_turned")
        with nc.Block() as block:

            @block.vector
            def _(dve):
                link = Chain(dve, s_dve)
                link(nc.vector.tensor_scalar(cut[0][:, :], k.first_row[:, :], -BIG, None, ALU.mult))
                link(nc.vector.tensor_scalar(cut[1][:, :], k.last_row[:, :], -BIG, None, ALU.mult))
                link(nc.vector.memset(run[:, :, :], -BIG))
                for d in range(2):
                    way = slice(None, None, -1) if d else slice(None)
                    end = 0 if d else RW - 1
                    src, dst = (ahead, most) if d else (es, ahead)
                    for c in range(C):
                        link(nc.vector.tensor_tensor_scan(dst[:, c, way], cut[d][:, way], src[:, c, way], -BIG,
                                                          ALU.add, ALU.max))
                    link(nc.vector.tensor_reduce(cutmin[:, :], cut[d][:, :], AX_X, ALU.min))
                    link(nc.vector.tensor_copy(on[:, C:2 * C], cutmin[:, 0:1].to_broadcast([ROWS, C])))
                    nc.vector.tensor_copy(on[:, 0:C], dst[:, :, end]).then_inc(s_on, 1)
                    dve.wait_ge(s_tp, 2 * (d + 1))
                    for m in range(2):
                        link(nc.vector.tensor_copy(on_t[:, m, :], tps[m][0:C, 0:ROWS]))
                    o = run[:, d, 0:ROWS] if d else run[:, d, 1:ROWS + 1]
                    nc.vector.tensor_tensor_scan(o[:, way], on_t[:, 1, way], on_t[:, 0, way], -BIG,
                                                 ALU.add, ALU.max).then_inc(s_run, 1)
                    dve.wait_ge(s_cp, d + 1)
                    link(nc.vector.tensor_copy(carry[:, d, :], tps[2][0:ROWS, 0:C]))
                    for c in range(C):
                        link(nc.vector.tensor_tensor_scan(dst[:, c, way], cut[d][:, way], src[:, c, way],
                                                          carry[:, d, c:c + 1], ALU.add, ALU.max))

            @block.tensor
            def _(pe):
                for d in range(2):
                    pe.wait_ge(s_on, d + 1)
                    for m in range(2):
                        nc.tensor.transpose(tps[m][0:C, 0:ROWS], on[:, m * C:(m + 1) * C],
                                            k.ident[0:ROWS, 0:ROWS]).then_inc(s_tp, 1)
                    pe.wait_ge(s_run, d + 1)
                    o = run[:, d, 1:ROWS + 1] if d else run[:, d, 0:ROWS]
                    nc.tensor.transpose(tps[2][0:ROWS, 0:C], o, k.ident[0:C, 0:C]).then_inc(s_cp, 1)


def expand(k, rows_steps):
    k.phase()
    nc, sem = k.nc, k.sem
    with ExitStack() as ctx:
        ps = [k.psum(ctx, f"pair{i}", [P, 2, 512]) for i in range(2)]
        s_mm, s_ev = sem("expanded"), sem("expanded_read")
        with nc.Block() as block:

            @block.tensor
            def _(pe):
                for q, (row, _) in enumerate(rows_steps):
                    after(pe, s_ev, q - 1)
                    for g in range(TPR):
                        for h in range(2):
                            last = nc.tensor.matmul(ps[q % 2][:, h, 0:HALF], row[:, g * P:(g + 1) * P],
                                                    k.steptile[:, g, h * HALF:(h + 1) * HALF],
                                                    start=(g == 0), stop=(g == TPR - 1))
                    last.then_inc(s_mm, 1)

            @block.scalar
            def _(act):
                for q, (_, step) in enumerate(rows_steps):
                    act.wait_ge(s_mm, q + 1)
                    nc.scalar.activation(step.rearrange("p (a s) -> p a s", a=2), ps[q % 2][:, :, 0:HALF],
                                         ACT.Copy).then_inc(s_ev, 1)


def gat_layer(k, ctx, C, rows_d):
    nc, sb, sem = k.nc, k.sb, k.sem
    W = D + 2 * C
    acc = sb(ctx, "acc", [P, NB, W])
    with ExitStack() as inner:
        wx = sb(inner, "wx", [P, STEPS, 2 * C])
        with ExitStack() as c2:
            both = sb(c2, "es_and_most", [P, 2 * C, STEPS])
            with ExitStack() as c3:
                es_row = sb(c3, "es_row", [ROWS, C, RW])
                most_row = sb(c3, "most_row", [ROWS, C, RW])
                lookup_src(k, C, k.node_s[:, 0:C, :], es_row)
                segment_max(k, C, es_row, most_row)
                expand(k, [(r[:, c, :], both[:, m * C + c, :]) for m, r in enumerate((es_row, most_row)) for c in range(C)])
            ed = sb(c2, "ed_step", [P, STEPS, C])
            lookup_dst(k, C, k.node_s[:, HEADS:HEADS + C, :], ed)
            edge_weights(k, C, both, ed, wx)
        row_steps(k, C, rows_d, acc, wx)
    return acc


def edge_weights(k, C, both, ed, wx):
    k.phase()
    nc, sem = k.nc, k.sem
    with ExitStack() as ctx:
        s_dve, s_u, s_w = sem("dve"), sem("exponent"), sem("weight")
        both4 = both[:, :, :].rearrange("p (m c) s -> p m c s", m=2)
        leaky = k.sb(ctx, "leaky", [P, 2 * C, STEPS])
        with nc.Block() as block:

            @block.vector
            def _(dve):
                link = Chain(dve, s_dve)
                for c in range(2 * C):
                    link(nc.vector.tensor_tensor(both[:, c, :], both[:, c, :], ed[:, :, c % C], ALU.add))
                flat, lf = both[:, :, :].rearrange("p c s -> p (c s)"), leaky[:, :, :].rearrange("p c s -> p (c s)")
                link(nc.vector.scalar_tensor_tensor(out=lf, in0=flat, scalar=0.2, in1=flat, op0=ALU.mult, op1=ALU.max))
                nc.vector.tensor_tensor(leaky[:, 0:C, :], leaky[:, 0:C, :], leaky[:, C:2 * C, :],
                                        ALU.subtract).then_inc(s_u, 1)
                for c in range(C):
                    link(nc.vector.tensor_tensor(wx[:, :, C + c], leaky[:, C + c, :], k.first_step[:, :], ALU.mult))

            @block.scalar
            def _(act):
                act.wait_ge(s_u, 1)
                for c in range(C):
                    nc.scalar.activation(wx[:, :, c], leaky[:, c, :], ACT.Exp).then_inc(s_w, 1)


def row_steps(k, C, rows_d, acc, wx):
    k.phase()
    nc, sb, sem = k.nc, k.sb, k.sem
    W = D + 2 * C
    H = U // 2
    with ExitStack() as ctx:
        rows = sb(ctx, "rows", [P, U, D])
        weighed = sb(ctx, "weighed", [P, U, W])
        hot = sb(ctx, "hot", [P, U, P])
        idx = sb(ctx, "idx", [P, U], I32)
        ps = [k.psum(ctx, f"sum{i}", [P, 512]) for i in range(2)]
        s_idx = sem("indices")
        s_row = [sem(f"row_in{u}") for u in range(U)]
        s_hot, s_wt, s_wc, s_mm, s_acc, s_zero = (sem("hot"), sem("weighed"), sem("weights_copied"), sem("summed"),
                                                  sem("added"), sem("zeroed"))
        with nc.Block() as block:

            @block.gpsimd
            def _(pool):
                def body(i):
                    for u in range(U):
                        n = i * U + u
                        if u % H == 0:
                            pool.wait_ge(s_idx, 2 * i + u // H + 1)
                        after(pool, s_wt, n - U + 1)
                        settled(pool, k.passed)
                        pool.indirect_dma_start(
                            out=rows[:, u, :], out_offset=None, in_=rows_d,
                            in_offset=bass.IndirectOffsetOnAxis(ap=idx[:, u:u + 1], axis=0)).then_inc(s_row[u], 16)
                turns(pool, TURNS, body)

            def indices(act, i, h):
                for u in range(h * H, (h + 1) * H):
                    after(act, s_row[u], 16 * i)
                s = i * U + h * H
                settled(act, k.passed)
                nc.scalar.activation(idx[:, h * H:(h + 1) * H],
                                     k.src_step[:, s:s + H] if isinstance(s, int) else k.src_step[:, bass.ds(s, H)],
                                     ACT.Copy).then_inc(s_idx, 1)

            @block.scalar
            def _(act):
                def body(i):
                    for h in range(2):
                        indices(act, i, h)
                    for u in range(U):
                        n = i * U + u
                        after(act, s_mm, n - U + 1)
                        w = wx[:, n, :] if isinstance(n, int) else wx[:, bass.ds(n, 1), :].rearrange("p o c -> p (o c)")
                        settled(act, k.passed)
                        nc.scalar.activation(weighed[:, u, D:W], w, ACT.Copy).then_inc(s_wc, 1)
                        if C == 1:
                            act.wait_ge(s_row[u], 16 * (i + 1))
                            settled(act, k.passed)
                            nc.scalar.activation(weighed[:, u, 0:D], rows[:, u, :], ACT.Copy,
                                                 scale=w[:, 0:1]).then_inc(s_wt, 1)
                turns(act, TURNS, body)

            @block.vector
            def _(dve):
                nc.vector.memset(acc[:, :, :], 0.0).then_inc(s_zero, 1)
                dve.wait_ge(s_zero, 1)

                def body(i):
                    def prepare(u):
                        n = i * U + u
                        after(dve, s_mm, n - U + 1)
                        d = k.dst_step[:, n:n + 1] if isinstance(n, int) else k.dst_step[:, bass.ds(n, 1)]
                        nc.vector.tensor_scalar(hot[:, u, :], k.iota_row[:, 0:P], d, None, ALU.is_equal).then_inc(s_hot, 1)
                        if C > 1:
                            dve.wait_ge(s_row[u], 16 * (i + 1))
                            w = wx[:, n:n + 1, 0:C] if isinstance(n, int) else wx[:, bass.ds(n, 1), 0:C]
                            nc.vector.tensor_tensor(
                                weighed[:, u, 0:D].rearrange("p (c e) -> p c e", c=C),
                                rows[:, u, :].rearrange("p (c e) -> p c e", c=C),
                                w.rearrange("p o c -> p c o").to_broadcast([P, C, D // C]), ALU.mult).then_inc(s_wt, 1)

                    def add(u):
                        n = i * U + u
                        b = dve.value_load(k.block_of[0:1, n:n + 1] if isinstance(n, int) else k.block_of[0:1, bass.ds(n, 1)],
                                           min_val=0, max_val=NB - 1)
                        dve.wait_ge(s_mm, n + 1)
                        after(dve, s_acc, n)
                        o = acc[:, bass.ds(b, 1), :].rearrange("p o w -> p (o w)")
                        nc.vector.tensor_tensor(o, o, ps[u % 2][:, 0:W],
                                                ALU.add).then_inc(s_acc, 1)

                    for u in range(U):
                        prepare(u)
                        if u >= 2:
                            add(u - 2)
                    add(U - 2)
                    add(U - 1)
                turns(dve, TURNS, body)

            @block.tensor
            def _(pe):
                def body(i):
                    for u in range(U):
                        n = i * U + u
                        pe.wait_ge(s_hot, n + 1)
                        pe.wait_ge(s_wt, n + 1)
                        pe.wait_ge(s_wc, n + 1)
                        after(pe, s_acc, n - 1)
                        nc.tensor.matmul(ps[u % 2][:, 0:W], hot[:, u, :], weighed[:, u, :],
                                         start=True, stop=True).then_inc(s_mm, 1)
                turns(pe, TURNS, body)



def softmax_end(k, C, acc, h_d):
    k.phase()
    nc, sb, sem = k.nc, k.sb, k.sem
    with ExitStack() as ctx:
        hs = sb(ctx, "h_self", [P, SELFB, D])
        e, m, z, fe, fs = (sb(ctx, n, [P, C, SELFB]) for n in ("e_self", "e_most", "none", "f_edges", "f_self"))
        other = sb(ctx, "no_loop", [P, SELFB])
        loop = sb(ctx, "loop", [P, SELFB])
        coef = sb(ctx, "coef", [P, C, NB])
        s_dve, s_h, s_x, s_f = sem("dve"), sem("h_in"), sem("exponents"), sem("factors")
        first = slice(0, SELFB)
        with nc.Block() as block:

            @block.sync
            def _(sp):
                sp.dma_start(hs[:, :, :], h_d[0:SELFB * P, :].rearrange("(b p) d -> p b d", p=P)).then_inc(s_h, 16)

            @block.vector
            def _(dve):
                link = Chain(dve, s_dve)
                v = nc.vector
                den = acc[:, :, D:D + C].rearrange("p b c -> p c b")
                top = acc[:, first, D + C:D + 2 * C].rearrange("p b c -> p c b")
                link(v.memset(other[:, :], 0.0))
                link(v.tensor_scalar(other[:, SELFB - 1:SELFB], k.iota_part[:, :], SELF - (SELFB - 1) * P - 0.5, None, ALU.is_gt))
                link(v.tensor_scalar(loop[:, :], other[:, :], -1.0, 1.0, ALU.mult, ALU.add))
                link(v.tensor_tensor(e[:, :, :], k.node_s[:, 0:C, first], k.node_s[:, HEADS:HEADS + C, first], ALU.add))
                link(v.scalar_tensor_tensor(out=e[:, :, :], in0=e[:, :, :], scalar=0.2, in1=e[:, :, :], op0=ALU.mult, op1=ALU.max))
                for c in range(C):
                    link(v.scalar_tensor_tensor(out=e[:, c, :], in0=other[:, :], scalar=-BIG, in1=e[:, c, :],
                                                op0=ALU.mult, op1=ALU.add))
                link(v.tensor_scalar(z[:, :, :], den[:, :, first], 0.0, -BIG, ALU.is_equal, ALU.mult))
                link(v.tensor_tensor(m[:, :, :], top, z[:, :, :], ALU.add))
                link(v.tensor_tensor(z[:, :, :], m[:, :, :], e[:, :, :], ALU.max))
                link(v.tensor_tensor(m[:, :, :], m[:, :, :], z[:, :, :], ALU.subtract))
                v.tensor_tensor(e[:, :, :], e[:, :, :], z[:, :, :], ALU.subtract).then_inc(s_x, 1)
                link(v.tensor_copy(coef[:, :, :], den))
                dve.wait_ge(s_f, 2)
                for c in range(C):
                    link(v.tensor_tensor(fs[:, c, :], fs[:, c, :], loop[:, :], ALU.mult))
                link(v.tensor_tensor(coef[:, :, first], coef[:, :, first], fe[:, :, :], ALU.mult))
                link(v.tensor_tensor(coef[:, :, first], coef[:, :, first], fs[:, :, :], ALU.add))
                link(v.tensor_scalar(coef[:, :, :], coef[:, :, :], 1e-30, None, ALU.max))
                link(v.reciprocal(coef[:, :, :], coef[:, :, :]))
                link(v.tensor_tensor(fs[:, :, :], fs[:, :, :], coef[:, :, first], ALU.mult))
                link(v.tensor_tensor(coef[:, :, first], coef[:, :, first], fe[:, :, :], ALU.mult))
                dve.wait_ge(s_h, 16)
                for c in range(C):
                    o = slice(c * D // C, (c + 1) * D // C)
                    link(v.tensor_tensor(acc[:, :, o], acc[:, :, o], coef[:, c, :].unsqueeze(2).to_broadcast([P, NB, D // C]), ALU.mult))
                    link(v.tensor_tensor(hs[:, :, o], hs[:, :, o], fs[:, c, :].unsqueeze(2).to_broadcast([P, SELFB, D // C]), ALU.mult))
                link(v.tensor_tensor(acc[:, first, 0:D], acc[:, first, 0:D], hs[:, :, :], ALU.add))

            @block.scalar
            def _(act):
                act.wait_ge(s_x, 1)
                act.wait_ge(s_dve, 3 + 2 + C + 4)
                nc.scalar.activation(fe[:, :, :], m[:, :, :], ACT.Exp).then_inc(s_f, 1)
                nc.scalar.activation(fs[:, :, :], e[:, :, :], ACT.Exp).then_inc(s_f, 1)


def norm_factors(k, dve, link, x, stats, mean, rstd, s_var, s_root):
    v = k.nc.vector
    with dve.Fori(0, NB) as n:
        v.bn_stats(at(stats, n), at(x, n)).then_inc(s_var, 1)
    dve.wait_ge(s_var, NB)
    me, ve, mo, vo = (stats[:, :, q] for q in (1, 2, 4, 5))
    link(v.tensor_tensor(mean, me, mo, ALU.subtract))
    link(v.tensor_tensor(mean, mean, mean, ALU.mult))
    link(v.tensor_tensor(rstd, ve, vo, ALU.add))
    link(v.tensor_scalar(rstd, rstd, 1.0 / D, EPS, ALU.mult, ALU.add))
    link(v.scalar_tensor_tensor(out=rstd, in0=mean, scalar=0.25, in1=rstd, op0=ALU.mult, op1=ALU.add))
    link(v.tensor_tensor(mean, me, mo, ALU.add))
    v.tensor_scalar(mean, mean, 0.5, None, ALU.mult).then_inc(s_var, 1)
    dve.wait_ge(s_var, NB + 1)
    dve.wait_ge(s_root, 1)
    link(v.reciprocal(rstd, rstd))


def at(x, n):
    return x[:, n, :] if isinstance(n, int) else x[:, bass.ds(n, 1), :].rearrange("p o d -> p (o d)")


def col(x, n):
    return x[:, n:n + 1] if isinstance(n, int) else x[:, bass.ds(n, 1)]


def gat_epilogue_1(k, acc):
    nc, sb, sem = k.nc, k.sb, k.sem
    softmax_end(k, HEADS, acc, k.h1_d)
    k.phase()
    W = D + 2
    with ExitStack() as ctx:
        w = sb(ctx, "w2x", [P, 2, W])
        av = sb(ctx, "a2_rows", [P, 2, D])
        wa = sb(ctx, "w2_times_a", [P, 2, D])
        vec = sb(ctx, "affine", [P, 3, D])
        stats, mean, var, rstd = sb(ctx, "stats", [P, NB, 6]), sb(ctx, "mean", [P, NB]), sb(ctx, "var", [P, NB]), sb(ctx, "rstd", [P, NB])
        eps = sb(ctx, "zero", [P, 1])
        y = sb(ctx, "normed", [P, NODE_U, D])
        xin = sb(ctx, "xin", [P, NODE_U, D])
        hout = sb(ctx, "hout", [P, NODE_U, D])
        xt = [sb(ctx, f"xt{i}", [P, 2, P]) for i in range(2)]
        tps = [k.psum(ctx, f"tps{i}", [P, 2, P]) for i in range(2)]
        ops = [k.psum(ctx, f"ops{i}", [P, 512]) for i in range(2)]
        s_w, s_wx, s_dve, s_var, s_root = sem("weights_in"), sem("weights_ready"), sem("dve"), sem("statistics"), sem("root")
        s_y, s_x = sem("normed"), sem("relu")
        s_st = [sem(f"h_stored{u}") for u in range(NODE_U)]
        s_tp, s_xt, s_mm, s_out, s_ev = sem("turned"), sem("turned_copied"), sem("product"), sem("product_read"), sem("h_ready")
        with nc.Block() as block:

            @block.sync
            def _(sp):
                sp.dma_start(w[:, :, 0:D], k.a["L0_gnn_W2"].rearrange("(c p) n -> p c n", p=P)).then_inc(s_w, 16)
                for m, n in enumerate(("L0_gnn_a2_src", "L0_gnn_a2_dst")):
                    sp.dma_start(av[:, m, :], k.a[n].rearrange("h c -> (h c)").partition_broadcast(P)).then_inc(s_w, 16)
                for m, n in enumerate(("L0_gnn_b1", "L0_gnn_ln_g", "L0_gnn_ln_b")):
                    sp.dma_start(vec[:, m, :], k.a[n].partition_broadcast(P)).then_inc(s_w, 16)

            @block.vector
            def _(dve):
                link = Chain(dve, s_dve)
                v = nc.vector
                dve.wait_ge(s_w, 16 * 6)
                for m in range(2):
                    link(v.tensor_tensor(wa[:, :, :], w[:, :, 0:D], av[:, m:m + 1, :].to_broadcast([P, 2, D]), ALU.mult))
                    v.tensor_reduce(w[:, :, D + m:D + m + 1], wa[:, :, :].unsqueeze(2), AX_X, ALU.add).then_inc(s_wx, 1)
                    dve.wait_ge(s_wx, m + 1)
                link(v.tensor_tensor(acc[:, :, 0:D], acc[:, :, 0:D], vec[:, 0:1, :].to_broadcast([P, NB, D]), ALU.add))
                norm_factors(k, dve, link, acc[:, :, 0:D], stats, mean[:, :], rstd[:, :], s_var, s_root)

                def body(i):
                    def norm(u):
                        n = i * NODE_U + u
                        after(dve, s_x, n - NODE_U + 1)
                        v.tensor_scalar(y[:, u, :], at(acc, n)[:, 0:D], col(mean, n), col(rstd, n),
                                        ALU.subtract, ALU.mult).then_inc(s_y, 1)
                        dve.wait_ge(s_y, 3 * n + 1)
                        v.tensor_tensor(y[:, u, :], y[:, u, :], vec[:, 1, :], ALU.mult).then_inc(s_y, 1)
                        dve.wait_ge(s_y, 3 * n + 2)
                        v.tensor_tensor(y[:, u, :], y[:, u, :], vec[:, 2, :], ALU.add).then_inc(s_y, 1)

                    def copy(u):
                        n = i * NODE_U + u
                        dve.wait_ge(s_tp, n + 1)
                        after(dve, s_mm, n - 1 if u else n)
                        v.tensor_copy(xt[u % 2][:, :, :], tps[u % 2][:, :, :]).then_inc(s_xt, 1)

                    for u in range(NODE_U):
                        norm(u)
                        if u:
                            copy(u - 1)
                    copy(NODE_U - 1)
                turns(dve, NODE_TURNS, body)

            @block.tensor
            def _(pe):
                pe.wait_ge(s_wx, 2)
                pe_project(k, pe, xin, NODE_U, lambda e, i, u: e.wait_ge(s_x, i * NODE_U + u + 1), tps, s_tp, s_xt, xt,
                           [(0, [(c, w[:, c, :]) for c in range(2)])], ops, s_mm, s_out, [(0, P), (P, P)])

            @block.scalar
            def _(act):
                act.wait_ge(s_var, NB + 1)
                nc.scalar.activation(rstd[:, :], rstd[:, :], ACT.Sqrt).then_inc(s_root, 1)

                def body(i):
                    def relu(u):
                        n = i * NODE_U + u
                        act.wait_ge(s_y, 3 * n + 3)
                        after(act, s_tp, n - NODE_U + 1)
                        nc.scalar.activation(xin[:, u, :], y[:, u, :], ACT.Relu).then_inc(s_x, 1)

                    def store(u):
                        n = i * NODE_U + u
                        act.wait_ge(s_mm, n + 1)
                        after(act, s_st[u], 16 * i)
                        nc.scalar.activation(hout[:, u, :], ops[u % 2][:, 0:D], ACT.Copy).then_inc(s_ev, 1)
                        o = k.node_s[:, 0:2 * HEADS:HEADS, n:n + 1] if isinstance(n, int) else k.node_s[:, 0:2 * HEADS:HEADS, bass.ds(n, 1)]
                        nc.scalar.activation(o, ops[u % 2][:, D:W].rearrange("p (c o) -> p c o", o=1), ACT.Copy).then_inc(s_out, 1)
                        act.wait_ge(s_ev, n + 1)
                        act.dma_start(rows_of(k.h2_d, n), hout[:, u, :]).then_inc(s_st[u], 16)

                    for u in range(NODE_U):
                        relu(u)
                        if u:
                            store(u - 1)
                    store(NODE_U - 1)
                turns(act, NODE_TURNS, body)
                for u in range(NODE_U):
                    act.wait_ge(s_st[u], 16 * NODE_TURNS)


def load_nodes(k, sp, x_d, tile, s):
    sp.dma_start(tile[:, 0:NFULL, :], x_d[0:NFULL * P, :].rearrange("(b p) d -> p b d", p=P)).then_inc(s, 16)
    sp.dma_start(tile[0:NLAST, NFULL, :], x_d[NFULL * P:N, :]).then_inc(s, 16)


def gat_epilogue_2(k, acc):
    nc, sb, sem = k.nc, k.sb, k.sem
    softmax_end(k, 1, acc, k.h2_d)
    k.phase()
    with ExitStack() as ctx:
        x = sb(ctx, "x_all", [P, NB, D])
        b2 = sb(ctx, "b2_row", [P, D])
        w3 = sb(ctx, "w3", [P, 6, 3 * D])
        arow = sb(ctx, "a_row", [P, 3 * D])
        wv = sb(ctx, "w3_a", [P, 6])
        wb = sb(ctx, "w3_a_wide", [P, 2, P])
        rel = sb(ctx, "rel_rows", [P, 2, D])
        wrow = sb(ctx, "w_rel_row", [P, D])
        w = sb(ctx, "w_cols", [P, 2, 2])
        stats, mean, rstd = sb(ctx, "stats", [P, NB, 6]), sb(ctx, "mean", [P, NB]), sb(ctx, "rstd", [P, NB])
        xin = sb(ctx, "xin", [P, NODE_U, D])
        xt = [sb(ctx, f"xt{i}", [P, 2, P]) for i in range(2)]
        tps = [k.psum(ctx, f"tps{i}", [P, 2, P]) for i in range(2)]
        ops = [k.psum(ctx, f"ops{i}", [P, 512]) for i in range(2)]
        wps = k.psum(ctx, "w_row_ps", [P, 2, P])
        s_in, s_zero, s_dve, s_var, s_root = sem("in"), sem("zeroed"), sem("dve"), sem("statistics"), sem("root")
        s_wb, s_wp, s_x = sem("w_wide"), sem("w_row"), sem("normed")
        s_st = [sem(f"x1_stored{u}") for u in range(NODE_U)]
        s_tp, s_xt, s_mm, s_out = sem("turned"), sem("turned_copied"), sem("product"), sem("product_read")
        with nc.Block() as block:

            @block.gpsimd
            def _(pool):
                nc.gpsimd.memset(x[:, NFULL, :], 0.0).then_inc(s_zero, 1)
                nc.gpsimd.memset(rel[:, :, :], 0.0).then_inc(s_zero, 1)

            @block.sync
            def _(sp):
                sp.wait_ge(s_zero, 2)
                load_nodes(k, sp, k.a["x"], x, s_in)
                sp.dma_start(b2[:, :], k.a["L0_gnn_b2"].partition_broadcast(P)).then_inc(s_in, 16)
                sp.dma_start(w3[:, :, :], k.a["L1_gnn_W3"].rearrange("(q p) n -> p q n", p=P)).then_inc(s_in, 16)
                sp.dma_start(arow[:, :], k.a["L1_gnn_a"].rearrange("n o -> (n o)").partition_broadcast(P)).then_inc(s_in, 16)
                sp.dma_start(rel[:, 0, :], k.a["L1_gnn_rel_emb"][0:P, :]).then_inc(s_in, 16)
                sp.dma_start(rel[0:REL - P, 1, :], k.a["L1_gnn_rel_emb"][P:REL, :]).then_inc(s_in, 16)

            @block.vector
            def _(dve):
                link = Chain(dve, s_dve)
                v = nc.vector
                dve.wait_ge(s_in, 16 * 7)
                link(v.tensor_tensor(w3[:, :, :], w3[:, :, :], arow[:, :].unsqueeze(1).to_broadcast([P, 6, 3 * D]), ALU.mult))
                link(v.tensor_reduce(wv[:, :], w3[:, :, :], AX_X, ALU.add))
                for q in range(2):
                    v.tensor_copy(wb[:, q, :], wv[:, 4 + q:5 + q].to_broadcast([P, P])).then_inc(s_wb, 1)
                v.tensor_copy(w[:, :, :], wv[:, 0:4].rearrange("p (m c) -> p c m", m=2)).then_inc(s_wb, 1)
                dve.wait_ge(s_wp, 1)
                link(v.tensor_copy(wrow[:, :], wps[:, :, :].rearrange("p q n -> p (q n)")))
                link(v.tensor_tensor(rel[:, :, :], rel[:, :, :], wrow[:, :].unsqueeze(1).to_broadcast([P, 2, D]), ALU.mult))
                link(v.tensor_reduce(k.srel[:, :], rel[:, :, :], AX_X, ALU.add))
                link(v.tensor_tensor(x[:, :, :], x[:, :, :], acc[:, :, 0:D], ALU.add))
                link(v.tensor_tensor(x[:, :, :], x[:, :, :], b2[:, :].unsqueeze(1).to_broadcast([P, NB, D]), ALU.add))
                norm_factors(k, dve, link, x, stats, mean[:, :], rstd[:, :], s_var, s_root)

                def body(i):
                    def norm(u):
                        n = i * NODE_U + u
                        after(dve, s_tp, n - NODE_U + 1)
                        after(dve, s_st[u], 16 * i)
                        v.tensor_scalar(xin[:, u, :], at(x, n), col(mean, n), col(rstd, n),
                                        ALU.subtract, ALU.mult).then_inc(s_x, 1)

                    def copy(u):
                        n = i * NODE_U + u
                        dve.wait_ge(s_tp, n + 1)
                        after(dve, s_mm, n - 1 if u else n)
                        v.tensor_copy(xt[u % 2][:, :, :], tps[u % 2][:, :, :]).then_inc(s_xt, 1)

                    for u in range(NODE_U):
                        norm(u)
                        if u:
                            copy(u - 1)
                    copy(NODE_U - 1)
                turns(dve, NODE_TURNS, body)

            @block.tensor
            def _(pe):
                pe.wait_ge(s_wb, 3)
                for q in range(2):
                    last = nc.tensor.matmul(wps[:, q, :], wb[:, q, :], k.ident[:, :], start=True, stop=True)
                last.then_inc(s_wp, 1)
                pe_project(k, pe, xin, NODE_U, lambda e, i, u: e.wait_ge(s_x, i * NODE_U + u + 1), tps, s_tp, s_xt, xt,
                           [(0, [(c, w[:, c, :]) for c in range(2)])], ops, s_mm, s_out, [(0, P), (P, P)])

            @block.scalar
            def _(act):
                act.wait_ge(s_var, NB + 1)
                nc.scalar.activation(rstd[:, :], rstd[:, :], ACT.Sqrt).then_inc(s_root, 1)

                def body(i):
                    for u in range(NODE_U):
                        n = i * NODE_U + u
                        act.wait_ge(s_x, n + 1)
                        act.dma_start(rows_of(k.x1_d, n), xin[:, u, :]).then_inc(s_st[u], 16)
                        act.wait_ge(s_mm, n + 1)
                        settled(act, k.passed)
                        o = k.node_s[:, 0:2 * HEADS:HEADS, n:n + 1] if isinstance(n, int) else k.node_s[:, 0:2 * HEADS:HEADS, bass.ds(n, 1)]
                        nc.scalar.activation(o, ops[u % 2][:, 0:2].rearrange("p (c o) -> p c o", o=1), ACT.Copy).then_inc(s_out, 1)
                turns(act, NODE_TURNS, body)
                for u in range(NODE_U):
                    act.wait_ge(s_st[u], 16 * NODE_TURNS)


RW_COLS = D + REL + 1


def relation_layer(k, ctx):
    nc, sb, sem = k.nc, k.sb, k.sem
    acc = sb(ctx, "acc", [P, NB, RW_COLS])
    with ExitStack() as inner:
        alpha = sb(inner, "alpha", [P, STEPS])
        with ExitStack() as c2:
            es = sb(c2, "es_step", [P, 1, STEPS])
            ed = sb(c2, "ed_step", [P, STEPS, 1])
            with ExitStack() as c3:
                es_row = sb(c3, "es_row", [ROWS, 1, RW])
                lookup_src(k, 1, k.node_s[:, 0:1, :], es_row)
                expand(k, [(es_row[:, 0, :], es[:, 0, :])])
            lookup_dst(k, 1, k.node_s[:, HEADS:HEADS + 1, :], ed, rel=k.srel[:, :])
            k.phase()
            s_dve, s_u, s_w = sem("dve"), sem("score"), sem("exp")
            with nc.Block() as block:

                @block.vector
                def _(dve):
                    link = Chain(dve, s_dve)
                    e = es[:, 0, :]
                    link(nc.vector.tensor_tensor(e, e, ed[:, :, 0], ALU.add))
                    nc.vector.scalar_tensor_tensor(out=e, in0=e, scalar=0.01, in1=e, op0=ALU.mult,
                                                   op1=ALU.max).then_inc(s_u, 1)
                    dve.wait_ge(s_w, 1)
                    link(nc.vector.reciprocal(e, alpha[:, :]))
                    link(nc.vector.tensor_tensor(alpha[:, :], alpha[:, :], e, ALU.mult))

                @block.scalar
                def _(act):
                    act.wait_ge(s_u, 1)
                    nc.scalar.activation(alpha[:, :], es[:, 0, :], ACT.Exp).then_inc(s_w, 1)
        relation_steps(k, acc, alpha)
    return acc


def relation_steps(k, acc, alpha):
    k.phase()
    nc, sb, sem = k.nc, k.sb, k.sem
    W = RW_COLS
    H = U // 2
    with ExitStack() as ctx:
        rows = sb(ctx, "rows", [P, U, W])
        hot = sb(ctx, "hot", [P, U, P])
        idx = sb(ctx, "idx", [P, U], I32)
        ps = [k.psum(ctx, f"sum{i}", [P, 512]) for i in range(2)]
        s_idx = sem("indices")
        s_row = [sem(f"row_in{u}") for u in range(U)]
        s_hot, s_rel, s_mm, s_acc, s_zero = sem("hot"), sem("relation_hot"), sem("summed"), sem("added"), sem("zeroed")
        with nc.Block() as block:

            @block.gpsimd
            def _(pool):
                def body(i):
                    for u in range(U):
                        n = i * U + u
                        if u % H == 0:
                            pool.wait_ge(s_idx, 2 * i + u // H + 1)
                        after(pool, s_mm, n - U + 1)
                        settled(pool, k.passed)
                        pool.indirect_dma_start(
                            out=rows[:, u, 0:D], out_offset=None, in_=k.x1_d,
                            in_offset=bass.IndirectOffsetOnAxis(ap=idx[:, u:u + 1], axis=0)).then_inc(s_row[u], 16)
                turns(pool, TURNS, body)

            @block.scalar
            def _(act):
                def body(i):
                    for h in range(2):
                        for u in range(h * H, (h + 1) * H):
                            after(act, s_row[u], 16 * i)
                        s = i * U + h * H
                        settled(act, k.passed)
                        nc.scalar.activation(idx[:, h * H:(h + 1) * H],
                                             k.src_step[:, s:s + H] if isinstance(s, int) else k.src_step[:, bass.ds(s, H)],
                                             ACT.Copy).then_inc(s_idx, 1)
                turns(act, TURNS, body)

            @block.vector
            def _(dve):
                nc.vector.memset(acc[:, :, :], 0.0).then_inc(s_zero, 1)
                nc.vector.memset(rows[:, :, W - 1:W], 1.0).then_inc(s_zero, 1)
                dve.wait_ge(s_zero, 2)

                def body(i):
                    def prepare(u):
                        n = i * U + u
                        after(dve, s_mm, n - U + 1)
                        nc.vector.tensor_scalar(hot[:, u, :], k.iota_row[:, 0:P], col(k.dst_step, n), col(alpha, n),
                                                ALU.is_equal, ALU.mult).then_inc(s_hot, 1)
                        nc.vector.tensor_scalar(rows[:, u, D:D + REL], k.iota_row[:, 0:REL], col(k.et_step, n), None,
                                                ALU.is_equal).then_inc(s_rel, 1)

                    def add(u):
                        n = i * U + u
                        b = dve.value_load(col(k.block_of[0:1, :], n), min_val=0, max_val=NB - 1)
                        dve.wait_ge(s_mm, n + 1)
                        after(dve, s_acc, n)
                        o = at(acc, b)
                        nc.vector.tensor_tensor(o, o, ps[u % 2][:, 0:W], ALU.add).then_inc(s_acc, 1)

                    for u in range(U):
                        prepare(u)
                        if u >= 2:
                            add(u - 2)
                    add(U - 2)
                    add(U - 1)
                turns(dve, TURNS, body)

            @block.tensor
            def _(pe):
                pe.wait_ge(s_zero, 2)

                def body(i):
                    for u in range(U):
                        n = i * U + u
                        pe.wait_ge(s_row[u], 16 * (i + 1))
                        pe.wait_ge(s_hot, n + 1)
                        pe.wait_ge(s_rel, n + 1)
                        after(pe, s_acc, n - 1)
                        nc.tensor.matmul(ps[u % 2][:, 0:W], hot[:, u, :], rows[:, u, :],
                                         start=True, stop=True).then_inc(s_mm, 1)
                turns(pe, TURNS, body)


def relation_epilogue(k, acc):
    k.phase()
    nc, sb, sem = k.nc, k.sb, k.sem
    WX = D + REL + D
    chunks = [(0, P), (P, P), (2 * P, P), (3 * P, REL - P), (D + REL, P), (D + REL + P, P)]
    with ExitStack() as ctx:
        x = sb(ctx, "x1_all", [P, NB, D])
        wn = sb(ctx, "w_neighbour", [P, 2, D])
        wr = sb(ctx, "rel_times_wn", [P, 2, D])
        wl = sb(ctx, "loop_weights", [P, 2, 2 * D])
        some = sb(ctx, "has_edges", [P, NB])
        stats, mean, rstd = sb(ctx, "stats", [P, NB, 6]), sb(ctx, "mean", [P, NB]), sb(ctx, "rstd", [P, NB])
        s_in, s_dve, s_var, s_root = sem("in"), sem("dve"), sem("statistics"), sem("root")
        with ExitStack() as c2:
            rel = sb(c2, "rel_rows", [P, 2, D])
            relt = sb(c2, "rel_turned", [P, 2, 2 * P])
            rps = k.psum(c2, "rel_ps", [P, 2, 2, P])
            wps = [k.psum(c2, f"wr_ps{i}", [P, 512]) for i in range(2)]
            s_zero, s_rt, s_rc, s_wr = sem("zeroed"), sem("rel_turned"), sem("rel_copied"), sem("rel_product")
            with nc.Block() as block:

                @block.gpsimd
                def _(pool):
                    nc.gpsimd.memset(rel[:, :, :], 0.0).then_inc(s_zero, 1)

                @block.sync
                def _(sp):
                    sp.dma_start(x[:, :, :], k.x1_d.rearrange("(b p) d -> p b d", p=P)).then_inc(s_in, 16)
                    sp.dma_start(wn[:, :, :], k.a["L1_gnn_weight_neighbor"].rearrange("(c p) n -> p c n", p=P)).then_inc(s_in, 16)
                    for m, n in enumerate(("L1_gnn_loop_weight", "L1_gnn_evolve_loop_weight")):
                        sp.dma_start(wl[:, :, m * D:(m + 1) * D], k.a[n].rearrange("(c p) n -> p c n", p=P)).then_inc(s_in, 16)
                    sp.wait_ge(s_zero, 1)
                    sp.dma_start(rel[:, 0, :], k.a["L1_gnn_rel_emb"][0:P, :]).then_inc(s_in, 16)
                    sp.dma_start(rel[0:REL - P, 1, :], k.a["L1_gnn_rel_emb"][P:REL, :]).then_inc(s_in, 16)
                    sp.wait_ge(s_in, 96)

                @block.tensor
                def _(pe):
                    pe.wait_ge(s_in, 96)
                    for r in range(2):
                        for c in range(2):
                            last = nc.tensor.transpose(rps[:, c, r, :], rel[:, r, c * P:(c + 1) * P], k.ident[:, :])
                    last.then_inc(s_rt, 1)
                    pe.wait_ge(s_rc, 1)
                    for r in range(2):
                        for c in range(2):
                            last = nc.tensor.matmul(wps[r][:, 0:D], relt[:, c, r * P:(r + 1) * P], wn[:, c, :],
                                                    start=(c == 0), stop=(c == 1))
                    last.then_inc(s_wr, 1)

                @block.vector
                def _(dve):
                    link = Chain(dve, s_dve)
                    dve.wait_ge(s_rt, 1)
                    nc.vector.tensor_copy(relt[:, :, :], rps[:, :, :, :].rearrange("p c r n -> p c (r n)")).then_inc(s_rc, 1)
                    dve.wait_ge(s_wr, 1)
                    for r in range(2):
                        link(nc.vector.tensor_copy(wr[:, r, :], wps[r][:, 0:D]))
                    link(nc.vector.tensor_scalar(some[:, :], acc[:, :, RW_COLS - 1], 0.0, None, ALU.is_gt))
        with ExitStack() as c2:
            xin = sb(c2, "xin", [P, 2, WX])
            xt = [sb(c2, f"xt{i}", [P, 6, P]) for i in range(2)]
            mix = [t[:, 0:2 * D].rearrange("p (m d) -> p m d", m=2) for t in (k.dst_step, k.et_step)]
            s_x, s_tp, s_xt, s_mm, s_nb, s_lp, s_mix = (sem(n) for n in (
                "xin", "turned", "turned_copied", "product", "messages_read", "part_copied", "mixed"))
            with ExitStack() as c3:
                tps = [k.psum(c3, f"tps{i}", [P, 8, P]) for i in range(2)]
                ops = [k.psum(c3, f"ops{i}", [P, 1024]) for i in range(2)]
                with nc.Block() as block:

                    @block.tensor
                    def _(pe):
                        ws = [wn[:, 0, :], wn[:, 1, :], wr[:, 0, :], wr[0:REL - P, 1, :]]
                        pe_project(k, pe, xin, 2, lambda e, i, u: e.wait_ge(s_x, 2 * (i * NODE_U + u + 1)), tps, s_tp, s_xt, xt,
                                   [(0, [(4, wl[:, 0, :]), (5, wl[:, 1, :])]), (512, list(enumerate(ws)))],
                                   ops, s_mm, s_mix, chunks, per=4)

                    @block.scalar
                    def _(act):
                        def body(i):
                            def load(u):
                                n = i * NODE_U + u
                                after(act, s_tp, n - 1 if u else n)
                                settled(act, k.passed)
                                nc.scalar.activation(xin[:, u % 2, 0:D + REL], at(acc, n)[:, 0:D + REL], ACT.Copy).then_inc(s_x, 1)
                                nc.scalar.activation(xin[:, u % 2, D + REL:WX], at(x, n), ACT.Copy).then_inc(s_x, 1)

                            def read(u):
                                n = i * NODE_U + u
                                act.wait_ge(s_mm, n + 1)
                                after(act, s_mix, 4 * (n - 1 if u else n))
                                nc.scalar.activation(mix[u % 2][:, 0, :], ops[u % 2][:, 512:512 + D], ACT.Relu).then_inc(s_nb, 1)
                                nc.scalar.activation(mix[u % 2][:, 1, :], ops[u % 2][:, D:2 * D], ACT.Copy).then_inc(s_nb, 1)

                            for u in range(NODE_U):
                                load(u)
                                if u:
                                    read(u - 1)
                            read(NODE_U - 1)
                        turns(act, NODE_TURNS, body)

                    @block.vector
                    def _(dve):
                        v = nc.vector

                        def body(i):
                            def copy(u):
                                n = i * NODE_U + u
                                dve.wait_ge(s_tp, n + 1)
                                after(dve, s_mm, n - 1 if u else n)
                                for lo, hi, p in ((0, 3, P), (3, 4, REL - P), (4, 6, P)):
                                    last = v.tensor_copy(xt[u % 2][0:p, lo:hi, :], tps[u % 2][0:p, lo:hi, :])
                                    if lo < 4:
                                        last.then_inc(s_lp, 1)
                                last.then_inc(s_xt, 1)

                            def join(u):
                                n = i * NODE_U + u
                                dve.wait_ge(s_nb, 2 * n + 2)
                                m0, m1 = mix[u % 2][:, 0, :], mix[u % 2][:, 1, :]
                                xn = at(x, n)
                                v.tensor_tensor(xn, xn, m0, ALU.add).then_inc(s_mix, 1)
                                dve.wait_ge(s_mix, 4 * n + 1)
                                v.tensor_tensor(xn, xn, m1, ALU.add).then_inc(s_mix, 1)
                                dve.wait_ge(s_mix, 4 * n + 2)
                                v.tensor_tensor(m1, ops[u % 2][:, 0:D], m1, ALU.subtract).then_inc(s_mix, 1)
                                dve.wait_ge(s_mix, 4 * n + 3)
                                v.scalar_tensor_tensor(out=xn, in0=m1, scalar=col(some, n), in1=xn, op0=ALU.mult,
                                                       op1=ALU.add).then_inc(s_mix, 1)

                            for u in range(NODE_U):
                                copy(u)
                                if u:
                                    join(u - 1)
                            join(NODE_U - 1)
                        turns(dve, NODE_TURNS, body)
        s_done, s_st = sem("normed"), sem("stored")
        y = acc[:, :, 0:D]
        with nc.Block() as block:

            @block.vector
            def _(dve):
                link = Chain(dve, s_dve, 3)
                norm_factors(k, dve, link, x, stats, mean[:, :], rstd[:, :], s_var, s_root)
                with dve.Fori(0, NB) as n:
                    nc.vector.tensor_scalar(at(y, n), at(x, n), col(mean, n), col(rstd, n),
                                            ALU.subtract, ALU.mult).then_inc(s_done, 1)

            @block.scalar
            def _(act):
                act.wait_ge(s_var, NB + 1)
                nc.scalar.activation(rstd[:, :], rstd[:, :], ACT.Sqrt).then_inc(s_root, 1)

            @block.sync
            def _(sp):
                for q in range(4):
                    lo, hi = q * 12, (q + 1) * 12
                    sp.wait_ge(s_done, hi)
                    sp.dma_start(k.out[lo * P:hi * P, :].rearrange("(b p) d -> p b d", p=P), y[:, lo:hi, :]).then_inc(s_st, 16)
                sp.wait_ge(s_done, NB)
                sp.dma_start(k.out[NFULL * P:N, :], y[0:NLAST, NFULL, :]).then_inc(s_st, 16)
                sp.wait_ge(s_st, 16 * 5)


_INS = ["x", "src", "dst", "edge_type_200", "L0_gnn_W1", "L0_gnn_a1_src", "L0_gnn_a1_dst", "L0_gnn_b1", "L0_gnn_ln_g",
        "L0_gnn_ln_b", "L0_gnn_W2", "L0_gnn_a2_src", "L0_gnn_a2_dst", "L0_gnn_b2", "L1_gnn_rel_emb",
        "L1_gnn_weight_neighbor", "L1_gnn_a", "L1_gnn_W3", "L1_gnn_loop_weight", "L1_gnn_evolve_loop_weight"]


def kernel(**inputs):
    import numpy as _np
    import concourse.bacc as _bacc
    from concourse import mybir as _mybir
    from concourse.bass_utils import run_bass_kernel_spmd as _run

    nc = _bacc.Bacc("TRN2", target_bir_lowering=False, num_devices=1)
    arrays, args = {}, {}
    for name in _INS:
        a = _np.ascontiguousarray(inputs[name])
        arrays[f"in_{name}_dram"] = a
        args[name] = nc.dram_tensor(f"in_{name}_dram", a.shape, _mybir.dt.from_np(a.dtype), kind="ExternalInput").ap()
    out = nc.dram_tensor("out_0_dram", (N, D), _mybir.dt.float32, kind="ExternalOutput").ap()
    program(nc, args, out)
    r = _run(nc, [arrays], core_ids=[0])
    return r.results[0]["out_0_dram"]
```

```python
from contextlib import ExitStack

import concourse.bass as bass
from concourse import mybir

F32 = mybir.dt.float32
BF16 = mybir.dt.bfloat16
I32 = mybir.dt.int32
ALU = mybir.AluOpType
ACT = mybir.ActivationFunctionType
AX_X = mybir.AxisListType.X

P = 128
N, D, E = 6250, 256, 100000
NB = -(-N // P)
NFULL, NLAST = N // P, N % P
TILES = -(-E // P)
TPR = 7
RW = TPR * P
ROWS = -(-TILES // TPR)
EFULL, ELAST = E // RW, E % RW
U = 16
H = U // 2
TURNS = -(-(TILES + NB - 1) // U)
STEPS = TURNS * U
HALF = STEPS // 2
NCH = -(-STEPS // P)
SELF = 1250
SELFB = -(-SELF // P)
HEADS, HID = 4, 64
REL = 200
LC = 8
BIG = 1e30
PAD_DST = 8191
NODE_U = 7
NODE_TURNS = NB // NODE_U
EPS = 1e-5
assert HALF * 2 == STEPS and HALF <= 512
assert NODE_TURNS * NODE_U == NB and EFULL == ROWS - 1 and ROWS * TPR >= TILES
assert RW % (4 * LC) == 0 and STEPS % (4 * U) == 0


class Chain:

    def __init__(self, eng, sem, base=0):
        self.eng, self.sem, self.base, self.n = eng, sem, base, 0

    def __call__(self, ins):
        ins.then_inc(self.sem, 1)
        self.n += 1
        self.eng.wait_ge(self.sem, self.base + self.n)


def after(eng, sem, value):
    if not (isinstance(value, int) and value <= 0):
        eng.wait_ge(sem, value)


def settled(eng, passed):
    eng.sem_inc(passed, 1)


def blocks_of(k, engine, i):
    steps = k.block_of[0:1, i * U:(i + 1) * U] if isinstance(i, int) else k.block_of[0:1, bass.ds(i * U, U)]
    return k.nc.values_load_multi_w_load_instructions(
        steps, engines=[engine], min_val=0, max_val=NB - 1,
        skip_runtime_bounds_check_because="step s = tile + block, with 0 <= tile < TILES counted up to s")[1]


def turns(eng, n, body):
    body(0)
    with eng.Fori(1, n - 1) as i:
        body(i)
    body(n - 1)


def program(nc, a, out):
    with ExitStack() as top:
        k = Kernel(nc, a, out, top)
        edge_structure(k)
        first_projection(k)
        with ExitStack() as ctx:
            acc = gat_layer(k, ctx, HEADS, k.h1_d)
            gat_epilogue_1(k, acc)
        with ExitStack() as ctx:
            acc = gat_layer(k, ctx, 1, k.h2_d)
            gat_epilogue_2(k, acc)
        with ExitStack() as ctx:
            acc = relation_layer(k, ctx)
            relation_epilogue(k, acc)


class Kernel:

    def __init__(self, nc, a, out, ctx):
        self.nc, self.a, self.out, self.ctx = nc, a, out, ctx
        self.names = 0
        self.sems = []
        self.passed = ctx.enter_context(nc.semaphore("waits_passed"))
        sb = self.sb
        self.h1_d = nc.dram_tensor("h1_rows", (NB * P, D), F32, kind="Internal").ap()
        self.h2_d = nc.dram_tensor("h2_rows", (NB * P, D), F32, kind="Internal").ap()
        self.x1_d = nc.dram_tensor("x1_rows", (NB * P, D + 1), F32, kind="Internal").ap()
        self.dlo_d = nc.dram_tensor("dst_local_by_step", (NCH * P, P), BF16, kind="Internal").ap()
        self.elo_d = nc.dram_tensor("relation_by_step", (NCH * P, P), BF16, kind="Internal").ap()
        self.slo_d = nc.dram_tensor("src_low_by_column", (RW, ROWS), BF16, kind="Internal").ap()
        self.iota_row = sb(ctx, "iota_row", [P, RW])
        self.iota_part = sb(ctx, "iota_part", [P, 1])
        self.tile_no = sb(ctx, "tile_no", [P, TPR])
        self.iota_nb = sb(ctx, "iota_nb", [P, NB], BF16)
        self.ident = sb(ctx, "ident", [P, P])
        self.steptile = sb(ctx, "steptile", [ROWS, TPR, STEPS])
        self.src_step = sb(ctx, "src_step", [P, STEPS], I32)
        self.dst_step = sb(ctx, "dst_step", [P, STEPS])
        self.et_step = sb(ctx, "et_step", [P, STEPS])
        self.first_step = sb(ctx, "first_step", [P, STEPS])
        self.block_of = sb(ctx, "block_of", [1, STEPS], I32)
        self.src_hi = sb(ctx, "src_hi", [ROWS, RW], BF16)
        self.first_row = sb(ctx, "first_row", [ROWS, RW], BF16)
        self.last_row = sb(ctx, "last_row", [ROWS, RW], BF16)
        self.srel = sb(ctx, "srel", [P, 2])
        self.node_s = sb(ctx, "node_s", [P, 2 * HEADS, NB])

    def sb(self, ctx, name, shape, dt=F32):
        return ctx.enter_context(self.nc.sbuf_tensor(self.fresh(name), shape, dt))

    def psum(self, ctx, name, shape, dt=F32):
        return ctx.enter_context(self.nc.psum_tensor(self.fresh(name), shape, dt))

    def sem(self, name):
        self.sems.append(self.nc.alloc_semaphore(name=self.fresh(name)))
        return self.sems[-1]

    def phase(self):
        if self.sems:
            self.nc.clear_and_free_semaphores(self.sems)
            self.nc.all_engine_barrier()
        self.sems = []

    def fresh(self, name):
        self.names += 1
        return f"{name}_{self.names}"


def edge_structure(k):
    k.phase()
    nc, sb, sem = k.nc, k.sb, k.sem
    with ExitStack() as ctx:
        ints = {n: sb(ctx, f"{n}_int", [ROWS, RW], I32) for n in ("src", "dst", "et")}
        flt = {n: sb(ctx, f"{n}_flt", [ROWS, RW]) for n in ("src", "dst", "et")}
        low_i = sb(ctx, "low_i", [ROWS, RW], I32)
        low_f = sb(ctx, "low_f", [ROWS, RW])
        first_f = sb(ctx, "first_f", [ROWS, RW])
        prev_i = sb(ctx, "prev_i", [ROWS, 1], I32)
        next_i = sb(ctx, "next_i", [ROWS, 1], I32)
        prev_f = sb(ctx, "prev_f", [ROWS, 1])
        next_f = sb(ctx, "next_f", [ROWS, 1])
        hi_i = sb(ctx, "hi_i", [ROWS, TPR], I32)
        first_of_tile = sb(ctx, "first_of_tile", [ROWS, TPR])
        begun = sb(ctx, "begun", [ROWS, TPR, STEPS], BF16)
        ones = sb(ctx, "ones_bf", [ROWS, P], BF16)
        tile_of = sb(ctx, "tile_of", [P, STEPS])
        block_f = sb(ctx, "block_f", [P, STEPS])
        low_t = sb(ctx, "low_t", [P, TPR, ROWS], BF16)
        dst_t = sb(ctx, "dst_t", [P, NCH, P], BF16)
        et_t = sb(ctx, "et_t", [P, NCH, P], BF16)
        pair = [k.psum(ctx, f"pair{i}", [P, 2, 512]) for i in range(3)]
        tps = [k.psum(ctx, f"tps{i}", [P, P]) for i in range(2)]
        s_fill, s_in, s_iota = sem("filled"), sem("edges_in"), sem("iotas")
        s_dve, s_ge, s_one = sem("dve"), sem("begun"), sem("ones")
        s_cnt, s_sel, s_exp, s_evac = sem("counted"), sem("steptile"), sem("expanded"), sem("evacuated")
        s_dst = sem("dst_local")
        s_dstf, s_low, s_tp, s_tc, s_lowd = sem("dst_step"), sem("low"), sem("turned"), sem("turned_out"), sem("low_out")
        names = ("src", "dst", "et")
        with nc.Block() as block:

            @block.gpsimd
            def _(pool):
                nc.gpsimd.memset(ints["src"][:, :], 0).then_inc(s_fill, 1)
                nc.gpsimd.memset(ints["et"][:, :], 0).then_inc(s_fill, 1)
                nc.gpsimd.memset(ints["dst"][:, :], PAD_DST).then_inc(s_fill, 1)
                nc.gpsimd.memset(prev_i[:, :], -1).then_inc(s_fill, 1)
                nc.gpsimd.memset(next_i[:, :], PAD_DST + 1).then_inc(s_fill, 1)
                nc.gpsimd.memset(dst_t[:, :, :], 0.0).then_inc(s_fill, 1)
                nc.gpsimd.memset(et_t[:, :, :], 0.0).then_inc(s_fill, 1)
                io = dict(allow_small_or_imprecise_dtypes=True)
                nc.gpsimd.iota(k.iota_row[:, :], pattern=[[1, RW]], base=0, channel_multiplier=0, **io).then_inc(s_iota, 1)
                nc.gpsimd.iota(k.iota_part[:, :], pattern=[[0, 1]], base=0, channel_multiplier=1, **io).then_inc(s_iota, 1)
                nc.gpsimd.iota(k.tile_no[:, :], pattern=[[1, TPR]], base=0, channel_multiplier=TPR, **io).then_inc(s_iota, 1)
                nc.gpsimd.iota(k.iota_nb[:, :], pattern=[[1, NB]], base=0, channel_multiplier=0, **io).then_inc(s_iota, 1)

            @block.sync
            def _(sp):
                sp.wait_ge(s_fill, 5)
                for n, src in (("dst", k.a["dst"]), ("src", k.a["src"]), ("et", k.a["edge_type_200"])):
                    sp.dma_start(ints[n][0:EFULL, :], src[0:EFULL * RW].rearrange("(p j) -> p j", j=RW)).then_inc(s_in, 16)
                    sp.dma_start(ints[n][EFULL:ROWS, 0:ELAST],
                                 src[EFULL * RW:E].rearrange("(p j) -> p j", p=1)).then_inc(s_in, 16)
                dst_rows = k.a["dst"][0:EFULL * RW].rearrange("(p j) -> p j", j=RW)
                with nc.allow_non_contiguous_dma(reason="one element of each partition"):
                    sp.dma_start(prev_i[1:ROWS, :], dst_rows[:, RW - 1:RW]).then_inc(s_in, 16)
                    sp.dma_start(next_i[0:EFULL - 1, :], dst_rows[1:EFULL, 0:1]).then_inc(s_in, 16)
                    sp.dma_start(next_i[EFULL - 1:EFULL, :],
                                 k.a["dst"][EFULL * RW:EFULL * RW + 1].rearrange("(p j) -> p j", p=1)).then_inc(s_in, 16)
                sp.wait_ge(s_tc, TPR)
                sp.dma_start(k.slo_d.rearrange("(g p) r -> p g r", p=P), low_t[:, :, :]).then_inc(s_lowd, 16)
                sp.wait_ge(s_tc, TPR + NCH)
                sp.dma_start(k.dlo_d.rearrange("(c p) e -> p c e", p=P), dst_t[:, :, :]).then_inc(s_lowd, 16)
                sp.wait_ge(s_tc, TPR + 2 * NCH)
                sp.dma_start(k.elo_d.rearrange("(c p) e -> p c e", p=P), et_t[:, :, :]).then_inc(s_lowd, 16)
                sp.wait_ge(s_lowd, 48)

            @block.vector
            def _(dve):
                link = Chain(dve, s_dve)
                dve.wait_ge(s_iota, 4)
                nc.vector.memset(ones[:, :], 1.0).then_inc(s_one, 1)
                nc.vector.tensor_scalar(k.ident[:, :], k.iota_row[:, 0:P], k.iota_part[:, 0:1], None,
                                        ALU.is_equal).then_inc(s_one, 1)
                dve.wait_ge(s_in, 16 * 9)
                link(nc.vector.tensor_scalar(hi_i[:, :], ints["dst"][:, 0:RW:P], 7, None, ALU.logical_shift_right))
                link(nc.vector.tensor_tensor(first_of_tile[:, :], hi_i[:, :], k.tile_no[0:ROWS, :], ALU.add))
                for g in range(TPR):
                    nc.vector.tensor_scalar(begun[:, g, :], k.iota_row[0:ROWS, 0:STEPS], first_of_tile[:, g:g + 1],
                                            None, ALU.is_ge).then_inc(s_ge, 1)
                link(nc.vector.tensor_scalar(low_i[:, :], ints["src"][:, :], P - 1, None, ALU.bitwise_and))
                nc.vector.tensor_copy(low_f[:, :], low_i[:, :]).then_inc(s_low, 1)
                dve.wait_ge(s_low, 1)
                link(nc.vector.tensor_scalar(low_i[:, :], ints["src"][:, :], 7, None, ALU.logical_shift_right))
                link(nc.vector.tensor_copy(k.src_hi[:, :], low_i[:, :]))
                for n in names:
                    nc.vector.tensor_copy(flt[n][:, :], ints[n][:, :]).then_inc(s_dstf, 1)
                link(nc.vector.tensor_copy(prev_f[:, :], prev_i[:, :]))
                link(nc.vector.tensor_copy(next_f[:, :], next_i[:, :]))
                dve.wait_ge(s_dstf, 3)
                df = flt["dst"]
                link(nc.vector.tensor_tensor(first_f[:, 1:RW], df[:, 1:RW], df[:, 0:RW - 1], ALU.not_equal))
                nc.vector.tensor_tensor(first_f[:, 0:1], df[:, 0:1], prev_f[:, :], ALU.not_equal).then_inc(s_dstf, 1)
                dve.wait_ge(s_dstf, 4)
                link(nc.vector.tensor_copy(k.first_row[:, :], first_f[:, :]))
                link(nc.vector.tensor_copy(k.last_row[:, 0:RW - 1], first_f[:, 1:RW]))
                link(nc.vector.tensor_tensor(k.last_row[:, RW - 1:RW], df[:, RW - 1:RW], next_f[:, :], ALU.not_equal))
                dve.wait_ge(s_cnt, 1)
                link(nc.vector.tensor_scalar(tile_of[:, :].rearrange("p (a s) -> p a s", a=2), pair[0][:, :, 0:HALF],
                                             -1.0, 0.0, ALU.add, ALU.max))
                link(nc.vector.tensor_tensor(block_f[:, :], k.iota_row[:, 0:STEPS], tile_of[:, :], ALU.subtract))
                link(nc.vector.tensor_scalar(k.block_of[:, :], block_f[0:1, :], NB - 1.0, None, ALU.min))
                for g in range(TPR):
                    nc.vector.tensor_scalar(k.steptile[:, g, :], tile_of[0:ROWS, :], k.tile_no[0:ROWS, g:g + 1], None,
                                            ALU.is_equal).then_inc(s_sel, 1)
                dve.wait_ge(s_exp, 1)
                nc.vector.scalar_tensor_tensor(
                    out=k.dst_step[:, :].rearrange("p (a s) -> p a s", a=2),
                    in0=block_f[:, :].rearrange("p (a s) -> p a s", a=2), scalar=-float(P),
                    in1=pair[1][:, :, 0:HALF], op0=ALU.mult, op1=ALU.add).then_inc(s_dst, 1)

            @block.tensor
            def _(pe):
                pe.wait_ge(s_one, 2)
                for g in range(TPR):
                    pe.wait_ge(s_ge, g + 1)
                    for h in range(2):
                        last = nc.tensor.matmul(pair[0][:, h, 0:HALF], ones[:, :],
                                                begun[:, g, h * HALF:(h + 1) * HALF],
                                                start=(g == 0), stop=(g == TPR - 1))
                last.then_inc(s_cnt, 1)
                pe.wait_ge(s_low, 1)
                for g in range(TPR):
                    if g >= 2:
                        pe.wait_ge(s_tc, g - 1)
                    nc.tensor.transpose(tps[g % 2][:, 0:ROWS], low_f[:, g * P:(g + 1) * P],
                                        k.ident[0:ROWS, 0:ROWS]).then_inc(s_tp, 1)
                pe.wait_ge(s_dstf, 4)
                pe.wait_ge(s_sel, TPR)
                for q, x in enumerate((flt["dst"], flt["src"], flt["et"], first_f)):
                    if q == 3:
                        pe.wait_ge(s_dst, 1)
                    for g in range(TPR):
                        for h in range(2):
                            last = nc.tensor.matmul(pair[(q + 1) % 3][:, h, 0:HALF], x[:, g * P:(g + 1) * P],
                                                    k.steptile[:, g, h * HALF:(h + 1) * HALF],
                                                    start=(g == 0), stop=(g == TPR - 1))
                    last.then_inc(s_exp, 1)
                pe.wait_ge(s_evac, 2)
                for m, x in enumerate((k.dst_step, k.et_step)):
                    for c in range(NCH):
                        n, at = min(P, STEPS - c * P), TPR + m * NCH + c
                        pe.wait_ge(s_tc, at - 1)
                        nc.tensor.transpose(tps[at % 2][0:n, :], x[:, c * P:c * P + n],
                                            k.ident[:, :]).then_inc(s_tp, 1)

            @block.scalar
            def _(act):
                for g in range(TPR):
                    act.wait_ge(s_tp, g + 1)
                    nc.scalar.activation(low_t[:, g, :], tps[g % 2][:, 0:ROWS], ACT.Copy).then_inc(s_tc, 1)
                for q, y in enumerate((None, k.src_step, k.et_step, k.first_step)):
                    if y is None:
                        continue
                    act.wait_ge(s_exp, q + 1)
                    nc.scalar.activation(y[:, :].rearrange("p (a s) -> p a s", a=2),
                                         pair[(q + 1) % 3][:, :, 0:HALF], ACT.Copy).then_inc(s_evac, 1)
                act.wait_ge(s_fill, 7)
                for m, y in enumerate((dst_t, et_t)):
                    for c in range(NCH):
                        n, at = min(P, STEPS - c * P), TPR + m * NCH + c
                        act.wait_ge(s_tp, at + 1)
                        nc.scalar.activation(y[0:n, c, :], tps[at % 2][0:n, :], ACT.Copy).then_inc(s_tc, 1)



def pe_project(k, pe, xin, slots, s_x, tps, s_tp, s_xt, xt, w, ops, s_mm, s_out, chunks, per=1):
    nc = k.nc

    def body(i):
        def turn_block(u):
            n = i * NODE_U + u
            s_x(pe, i, u)
            after(pe, s_xt, n - 1 if u else n)
            for c, (lo, wd) in enumerate(chunks):
                last = nc.tensor.transpose(tps[u % 2][0:wd, c, :], xin[:, u % slots, lo:lo + wd], k.ident[:, :])
            last.then_inc(s_tp, 1)

        def multiply(u):
            n = i * NODE_U + u
            pe.wait_ge(s_xt, n + 1)
            after(pe, s_out, per * (n - 1 if u else n))
            for group in w:
                o, cs = group
                for m, (c, wt) in enumerate(cs):
                    wd = chunks[c][1]
                    last = nc.tensor.matmul(ops[u % 2][:, o:o + wt.shape[-1]], xt[u % 2][0:wd, c, :], wt,
                                            start=(m == 0), stop=(m == len(cs) - 1))
            last.then_inc(s_mm, 1)

        for u in range(NODE_U):
            turn_block(u)
            if u:
                multiply(u - 1)
        multiply(NODE_U - 1)

    turns(pe, NODE_TURNS, body)


def rows_of(dram, n):
    return dram[bass.ds(n * P, P), :] if not isinstance(n, int) else dram[n * P:(n + 1) * P, :]


def first_projection(k):
    k.phase()
    nc, sb, sem = k.nc, k.sb, k.sem
    W = D + 2 * HEADS
    with ExitStack() as ctx:
        w = sb(ctx, "w1x", [P, 2, W])
        av = sb(ctx, "a_rows", [P, 2, D])
        wa = sb(ctx, "w1_times_a", [P, 2, D])
        xin = sb(ctx, "xin", [P, NODE_U, D])
        hout = sb(ctx, "hout", [P, NODE_U, D])
        xt = [sb(ctx, f"xt{i}", [P, 2, P]) for i in range(2)]
        tps = [k.psum(ctx, f"tps{i}", [P, 2, P]) for i in range(2)]
        ops = [k.psum(ctx, f"ops{i}", [P, 512]) for i in range(2)]
        s_w, s_wx, s_dve, s_last = sem("weights_in"), sem("weights_ready"), sem("dve"), sem("last_block_zero")
        s_x = [sem(f"x_in{u}") for u in range(NODE_U)]
        s_st = [sem(f"h_stored{u}") for u in range(NODE_U)]
        s_tp, s_xt, s_mm, s_out, s_ev = sem("turned"), sem("turned_copied"), sem("product"), sem("product_read"), sem("h_ready")
        with nc.Block() as block:

            @block.sync
            def _(sp):
                sp.dma_start(w[:, :, 0:D], k.a["L0_gnn_W1"].rearrange("(c p) n -> p c n", p=P)).then_inc(s_w, 16)
                for m, n in enumerate(("L0_gnn_a1_src", "L0_gnn_a1_dst")):
                    sp.dma_start(av[:, m, :], k.a[n].rearrange("h c -> (h c)").partition_broadcast(P)).then_inc(s_w, 16)

                def body(i):
                    for u in range(NODE_U):
                        n = i * NODE_U + u
                        after(sp, s_tp, n - NODE_U + 1)
                        if isinstance(n, int) and n == NB - 1:
                            sp.wait_ge(s_last, 1)
                            sp.dma_start(xin[0:NLAST, u, :], k.a["x"][n * P:N, :]).then_inc(s_x[u], 16)
                        else:
                            sp.dma_start(xin[:, u, :], rows_of(k.a["x"], n)).then_inc(s_x[u], 16)
                turns(sp, NODE_TURNS, body)

            @block.vector
            def _(dve):
                link = Chain(dve, s_dve)
                dve.wait_ge(s_w, 48)
                for m in range(2):
                    link(nc.vector.tensor_tensor(wa[:, :, :], w[:, :, 0:D],
                                                 av[:, m:m + 1, :].to_broadcast([P, 2, D]), ALU.mult))
                    nc.vector.tensor_reduce(w[:, :, D + m * HEADS:D + (m + 1) * HEADS],
                                            wa[:, :, :].rearrange("p c (h e) -> p c h e", h=HEADS), AX_X,
                                            ALU.add).then_inc(s_wx, 1)
                    dve.wait_ge(s_wx, m + 1)

                def copy(o, i):
                    return nc.vector.tensor_copy(o[:, :, :], i[:, :, :])

                def body(i):
                    for u in range(NODE_U):
                        n = i * NODE_U + u
                        if isinstance(n, int) and n == NB - NODE_U:
                            dve.wait_ge(s_tp, NB - NODE_U)
                            nc.vector.memset(xin[:, NODE_U - 1, :], 0.0).then_inc(s_last, 1)
                        dve.wait_ge(s_tp, n + 1)
                        after(dve, s_mm, n - 1 if u else n)
                        copy(xt[u % 2], tps[u % 2]).then_inc(s_xt, 1)
                turns(dve, NODE_TURNS, body)

            @block.tensor
            def _(pe):
                pe.wait_ge(s_wx, 2)
                pe_project(k, pe, xin, NODE_U, lambda e, i, u: e.wait_ge(s_x[u], 16 * (i + 1)), tps, s_tp, s_xt, xt,
                           [(0, [(c, w[:, c, :]) for c in range(2)])], ops, s_mm, s_out, [(0, P), (P, P)])

            @block.scalar
            def _(act):
                def body(i):
                    for u in range(NODE_U):
                        n = i * NODE_U + u
                        act.wait_ge(s_mm, n + 1)
                        after(act, s_st[u], 16 * i)
                        nc.scalar.activation(hout[:, u, :], ops[u % 2][:, 0:D], ACT.Copy).then_inc(s_ev, 1)
                        nc.scalar.activation(k.node_s[:, :, n:n + 1] if isinstance(n, int) else k.node_s[:, :, bass.ds(n, 1)],
                                             ops[u % 2][:, D:W].rearrange("p (c o) -> p c o", o=1), ACT.Copy).then_inc(s_out, 1)
                        act.wait_ge(s_ev, n + 1)
                        act.dma_start(rows_of(k.h1_d, n), hout[:, u, :]).then_inc(s_st[u], 16)
                turns(act, NODE_TURNS, body)
                for u in range(NODE_U):
                    act.wait_ge(s_st[u], 16 * NODE_TURNS)



def split_table(k, link, node, rest, tab):
    nc = k.nc
    link(nc.vector.tensor_copy(tab[0], node))
    link(nc.vector.tensor_tensor(rest, node, tab[0], ALU.subtract))
    link(nc.vector.tensor_copy(tab[1], rest))
    link(nc.vector.tensor_tensor(rest, rest, tab[1], ALU.subtract))
    link(nc.vector.tensor_copy(tab[2], rest))


def lookup_src(k, C, node, out_row):
    k.phase()
    nc, sb, sem = k.nc, k.sb, k.sem
    NQ = 4
    NL = RW // LC // NQ
    with ExitStack() as ctx:
        tab = sb(ctx, "src_table", [P, 3, C, NB], BF16)
        rest = sb(ctx, "src_rest", [P, C, NB])
        low = [sb(ctx, f"low{q}", [P, LC * ROWS], BF16) for q in range(NQ)]
        hot = [sb(ctx, f"hot{q}", [P, LC * ROWS], BF16) for q in range(NQ)]
        mask = [sb(ctx, f"mask{h}", [ROWS, LC, NB], BF16) for h in range(2)]
        prod = [sb(ctx, f"prod{h}", [ROWS, LC, C, NB]) for h in range(2)]
        ps = [k.psum(ctx, f"cand{h}", [P, LC, 256 if C > 1 else 64]) for h in range(2)]
        s_low = [sem(f"low_in{q}") for q in range(NQ)]
        s_dve, s_tab, s_hot, s_mask, s_mm, s_prod, s_red = (sem("dve"), sem("table"), sem("hot"), sem("mask"),
                                                            sem("candidates"), sem("picked"), sem("summed"))
        with nc.Block() as block:

            @block.sync
            def _(sp):
                def body(i):
                    for q in range(NQ):
                        n = NQ * i + q
                        after(sp, s_hot, n - NQ + 1)
                        src = k.slo_d[bass.ds(n * LC, LC), :] if not isinstance(n, int) else k.slo_d[n * LC:(n + 1) * LC, :]
                        sp.dma_start(low[q][:, :], src.rearrange("j r -> (j r)").partition_broadcast(P)).then_inc(s_low[q], 16)
                turns(sp, NL, body)

            @block.vector
            def _(dve):
                link = Chain(dve, s_dve)
                split_table(k, link, node, rest[:, :, :], [tab[:, m, :, :] for m in range(3)])
                nc.vector.memset(rest[:, 0, 0:1], 0.0).then_inc(s_tab, 1)

                def one_hot(i, q):
                    n = NQ * i + q
                    dve.wait_ge(s_low[q], 16 * (i + 1))
                    after(dve, s_mm, n - NQ + 1)
                    nc.vector.tensor_scalar(hot[q][:, :], low[q][:, :], k.iota_part[:, 0:1], None,
                                            ALU.is_equal).then_inc(s_hot, 1)
                    after(dve, s_prod, n - 1)
                    hi = k.src_hi[:, n * LC:(n + 1) * LC] if isinstance(n, int) else k.src_hi[:, bass.ds(n * LC, LC)]
                    nc.vector.tensor_tensor(mask[q % 2][:, :, :], hi.unsqueeze(2).to_broadcast([ROWS, LC, NB]),
                                            k.iota_nb[0:ROWS, :].unsqueeze(1).to_broadcast([ROWS, LC, NB]),
                                            ALU.is_equal).then_inc(s_mask, 1)

                def pick(n, h):
                    j = n * LC
                    dve.wait_ge(s_mm, n + 1)
                    dve.wait_ge(s_mask, n + 1)
                    after(dve, s_red, n - 1)
                    nc.vector.tensor_tensor(
                        prod[h][:, :, :, :], ps[h][0:ROWS, :, 0:C * NB].rearrange("r j (c b) -> r j c b", c=C),
                        mask[h][:, :, :].unsqueeze(2).to_broadcast([ROWS, LC, C, NB]), ALU.mult).then_inc(s_prod, 1)
                    dve.wait_ge(s_prod, n + 1)
                    o = out_row[:, :, j:j + LC] if isinstance(j, int) else out_row[:, :, bass.ds(j, LC)]
                    nc.vector.tensor_reduce(o.rearrange("r c j -> r j c"), prod[h][:, :, :, :], AX_X,
                                            ALU.add).then_inc(s_red, 1)

                def body(i):
                    for q in range(NQ):
                        one_hot(i, q)
                        if not (isinstance(i, int) and i == 0 and q == 0):
                            pick(NQ * i + q - 1, (q - 1) % 2)
                turns(dve, NL, body)
                pick(NQ * NL - 1, 1)

            @block.tensor
            def _(pe):
                pe.wait_ge(s_tab, 1)

                def body(i):
                    for q in range(NQ):
                        n = NQ * i + q
                        pe.wait_ge(s_hot, n + 1)
                        after(pe, s_prod, n - 1)
                        for j in range(LC):
                            for m in range(3):
                                last = nc.tensor.matmul(ps[q % 2][0:ROWS, j, 0:C * NB],
                                                        hot[q][:, j * ROWS:(j + 1) * ROWS],
                                                        tab[:, m, :, :].rearrange("p c b -> p (c b)"),
                                                        start=(m == 0), stop=(m == 2))
                        last.then_inc(s_mm, 1)
                turns(pe, NL, body)


def lookup_dst(k, C, node, out_step, rel=None):
    k.phase()
    nc, sb, sem = k.nc, k.sb, k.sem
    NQ = 4
    NL = STEPS // U // NQ
    kinds = 1 if rel is None else 3
    with ExitStack() as ctx:
        tab = sb(ctx, "dst_table", [P, NB, 3, C], BF16)
        rest = sb(ctx, "dst_rest", [P, C, NB])
        rtab = sb(ctx, "rel_table", [P, 2, 3], BF16)
        part2 = sb(ctx, "iota_part2", [P, 1])
        dmas = 1 if rel is None else 2
        low = [sb(ctx, f"dlow{q}", [P, dmas, U * P], BF16) for q in range(NQ)]
        hot = [sb(ctx, f"dhot{h}", [P, kinds, U * P], BF16) for h in range(2)]
        ps = [k.psum(ctx, f"vals{h}", [P, U, 16]) for h in range(2)]
        s_low = [sem(f"dlow_in{q}") for q in range(NQ)]
        s_dve, s_tab, s_hot, s_mm, s_red = sem("dve"), sem("table"), sem("hot"), sem("values"), sem("summed")
        with nc.Block() as block:

            @block.sync
            def _(sp):
                def body(i):
                    for q in range(NQ):
                        n = NQ * i + q
                        after(sp, s_hot, (n - NQ + 1) * kinds)
                        for m, d in enumerate((k.dlo_d, k.elo_d)[0:dmas]):
                            src = d[n * U:(n + 1) * U, :] if isinstance(n, int) else d[bass.ds(n * U, U), :]
                            sp.dma_start(low[q][:, m, :],
                                         src.rearrange("s e -> (s e)").partition_broadcast(P)).then_inc(s_low[q], 16)
                turns(sp, NL, body)

            @block.vector
            def _(dve):
                link = Chain(dve, s_dve)
                split_table(k, link, node, rest[:, :, :],
                            [tab[:, :, m, :].rearrange("p b c -> p c b") for m in range(3)])
                if rel is not None:
                    link(nc.vector.tensor_scalar(part2[:, :], k.iota_part[:, :], float(P), None, ALU.add))
                    split_table(k, link, rel, rest[:, 0, 0:2], [rtab[:, :, m] for m in range(3)])
                nc.vector.memset(rest[:, 0, 0:1], 0.0).then_inc(s_tab, 1)

                def one_hot(i, q):
                    n = NQ * i + q
                    dve.wait_ge(s_low[q], 16 * dmas * (i + 1))
                    after(dve, s_mm, n - 1)
                    for m, (x, p) in enumerate(((0, k.iota_part), (1, k.iota_part), (1, part2))[0:kinds]):
                        nc.vector.tensor_scalar(hot[q % 2][:, m, :], low[q][:, x, :], p[:, 0:1], None,
                                                ALU.is_equal).then_inc(s_hot, 1)

                def total(n, h):
                    dve.wait_ge(s_mm, n + 1)
                    o = out_step[:, n * U:(n + 1) * U, :] if isinstance(n, int) else out_step[:, bass.ds(n * U, U), :]
                    nc.vector.tensor_reduce(o, ps[h][:, :, 0:3 * C].rearrange("p s (m c) -> p s c m", m=3), AX_X,
                                            ALU.add).then_inc(s_red, 1)

                def body(i):
                    for q in range(NQ):
                        one_hot(i, q)
                        if not (isinstance(i, int) and i == 0 and q == 0):
                            total(NQ * i + q - 1, (q - 1) % 2)
                turns(dve, NL, body)
                total(NQ * NL - 1, 1)

            @block.tensor
            def _(pe):
                pe.wait_ge(s_tab, 1)

                def body(i):
                    for q in range(NQ):
                        n = NQ * i + q
                        blocks = blocks_of(k, mybir.EngineType.PE, n)
                        pe.wait_ge(s_hot, (n + 1) * kinds)
                        after(pe, s_red, n - 1)
                        for u in range(U):
                            o = ps[q % 2][:, u, 0:3 * C]
                            hots = hot[q % 2][:, :, u * P:(u + 1) * P]
                            last = nc.tensor.matmul(o, hots[:, 0, :],
                                                    tab[:, bass.ds(blocks[u], 1), :, :].rearrange("p b m c -> p (b m c)"),
                                                    start=True, stop=(rel is None))
                            for m in range(1, kinds):
                                last = nc.tensor.matmul(o, hots[:, m, :], rtab[:, m - 1, :], start=False,
                                                        stop=(m == kinds - 1))
                        last.then_inc(s_mm, 1)
                turns(pe, NL, body)


def segment_max(k, C, es, most):
    k.phase()
    nc, sb, sem = k.nc, k.sb, k.sem
    with ExitStack() as ctx:
        ahead = sb(ctx, "ahead", [ROWS, C, RW])
        cut = [sb(ctx, f"cut{d}", [ROWS, RW]) for d in range(2)]
        on = sb(ctx, "handed_on", [ROWS, 2 * C])
        cutmin = sb(ctx, "cutmin", [ROWS, 1])
        on_t = sb(ctx, "handed_on_t", [C, 2, ROWS])
        run = sb(ctx, "run", [C, 2, ROWS + 1])
        carry = sb(ctx, "carry", [ROWS, 2, C])
        tps = [k.psum(ctx, f"tps{i}", [P, P]) for i in range(3)]
        s_dve, s_on, s_tp, s_run, s_cp = sem("dve"), sem("handed_on"), sem("turned"), sem("run"), sem("carry_turned")
        with nc.Block() as block:

            @block.vector
            def _(dve):
                link = Chain(dve, s_dve)
                link(nc.vector.tensor_scalar(cut[0][:, :], k.first_row[:, :], -BIG, None, ALU.mult))
                link(nc.vector.tensor_scalar(cut[1][:, :], k.last_row[:, :], -BIG, None, ALU.mult))
                link(nc.vector.memset(run[:, :, :], -BIG))
                for d in range(2):
                    way = slice(None, None, -1) if d else slice(None)
                    end = 0 if d else RW - 1
                    src, dst = (ahead, most) if d else (es, ahead)
                    for c in range(C):
                        link(nc.vector.tensor_tensor_scan(dst[:, c, way], cut[d][:, way], src[:, c, way], -BIG,
                                                          ALU.add, ALU.max))
                    link(nc.vector.tensor_reduce(cutmin[:, :], cut[d][:, :], AX_X, ALU.min))
                    link(nc.vector.tensor_copy(on[:, C:2 * C], cutmin[:, 0:1].to_broadcast([ROWS, C])))
                    nc.vector.tensor_copy(on[:, 0:C], dst[:, :, end]).then_inc(s_on, 1)
                    dve.wait_ge(s_tp, 2 * (d + 1))
                    for m in range(2):
                        link(nc.vector.tensor_copy(on_t[:, m, :], tps[m][0:C, 0:ROWS]))
                    o = run[:, d, 0:ROWS] if d else run[:, d, 1:ROWS + 1]
                    nc.vector.tensor_tensor_scan(o[:, way], on_t[:, 1, way], on_t[:, 0, way], -BIG,
                                                 ALU.add, ALU.max).then_inc(s_run, 1)
                    dve.wait_ge(s_cp, d + 1)
                    link(nc.vector.tensor_copy(carry[:, d, :], tps[2][0:ROWS, 0:C]))
                    for c in range(C):
                        link(nc.vector.tensor_tensor_scan(dst[:, c, way], cut[d][:, way], src[:, c, way],
                                                          carry[:, d, c:c + 1], ALU.add, ALU.max))

            @block.tensor
            def _(pe):
                for d in range(2):
                    pe.wait_ge(s_on, d + 1)
                    for m in range(2):
                        nc.tensor.transpose(tps[m][0:C, 0:ROWS], on[:, m * C:(m + 1) * C],
                                            k.ident[0:ROWS, 0:ROWS]).then_inc(s_tp, 1)
                    pe.wait_ge(s_run, d + 1)
                    o = run[:, d, 1:ROWS + 1] if d else run[:, d, 0:ROWS]
                    nc.tensor.transpose(tps[2][0:ROWS, 0:C], o, k.ident[0:C, 0:C]).then_inc(s_cp, 1)


def expand(k, rows_steps):
    k.phase()
    nc, sem = k.nc, k.sem
    with ExitStack() as ctx:
        ps = [k.psum(ctx, f"pair{i}", [P, 2, 512]) for i in range(2)]
        s_mm, s_ev = sem("expanded"), sem("expanded_read")
        with nc.Block() as block:

            @block.tensor
            def _(pe):
                for q, (row, _) in enumerate(rows_steps):
                    after(pe, s_ev, q - 1)
                    for g in range(TPR):
                        for h in range(2):
                            last = nc.tensor.matmul(ps[q % 2][:, h, 0:HALF], row[:, g * P:(g + 1) * P],
                                                    k.steptile[:, g, h * HALF:(h + 1) * HALF],
                                                    start=(g == 0), stop=(g == TPR - 1))
                    last.then_inc(s_mm, 1)

            @block.scalar
            def _(act):
                for q, (_, step) in enumerate(rows_steps):
                    act.wait_ge(s_mm, q + 1)
                    nc.scalar.activation(step.rearrange("p (a s) -> p a s", a=2), ps[q % 2][:, :, 0:HALF],
                                         ACT.Copy).then_inc(s_ev, 1)


def gat_layer(k, ctx, C, rows_d):
    W = D + 2 * C
    acc = k.sb(ctx, "acc", [P, NB, W])
    flat = acc[:, :, :].rearrange("p b w -> p (b w)")
    both = flat[:, 0:2 * C * STEPS].rearrange("p (c s) -> p c s", c=2 * C)
    ed = flat[:, 2 * C * STEPS:3 * C * STEPS].rearrange("p (s c) -> p s c", c=C)
    assert 3 * C * STEPS <= NB * W
    with ExitStack() as inner:
        wx = k.sb(inner, "wx", [P, STEPS, 2 * C])
        with ExitStack() as c2:
            es_row = k.sb(c2, "es_row", [ROWS, C, RW])
            most_row = k.sb(c2, "most_row", [ROWS, C, RW])
            lookup_src(k, C, k.node_s[:, 0:C, :], es_row)
            segment_max(k, C, es_row, most_row)
            expand(k, [(r[:, c, :], both[:, m * C + c, :]) for m, r in enumerate((es_row, most_row)) for c in range(C)])
        lookup_dst(k, C, k.node_s[:, HEADS:HEADS + C, :], ed)
        edge_weights(k, C, both, ed, wx)
        row_steps(k, C, rows_d, acc, wx)
    return acc


def edge_weights(k, C, both, ed, wx):
    k.phase()
    nc, sem = k.nc, k.sem
    with ExitStack() as ctx:
        s_dve, s_u, s_w = sem("dve"), sem("exponent"), sem("weight")
        both4 = both[:, :, :].rearrange("p (m c) s -> p m c s", m=2)
        leaky = k.sb(ctx, "leaky", [P, 2 * C, STEPS])
        with nc.Block() as block:

            @block.vector
            def _(dve):
                link = Chain(dve, s_dve)
                for c in range(2 * C):
                    link(nc.vector.tensor_tensor(both[:, c, :], both[:, c, :], ed[:, :, c % C], ALU.add))
                flat, lf = both[:, :, :].rearrange("p c s -> p (c s)"), leaky[:, :, :].rearrange("p c s -> p (c s)")
                link(nc.vector.scalar_tensor_tensor(out=lf, in0=flat, scalar=0.2, in1=flat, op0=ALU.mult, op1=ALU.max))
                nc.vector.tensor_tensor(leaky[:, 0:C, :], leaky[:, 0:C, :], leaky[:, C:2 * C, :],
                                        ALU.subtract).then_inc(s_u, 1)
                for c in range(C):
                    link(nc.vector.tensor_tensor(wx[:, :, C + c], leaky[:, C + c, :], k.first_step[:, :], ALU.mult))

            @block.scalar
            def _(act):
                act.wait_ge(s_u, 1)
                for c in range(C):
                    nc.scalar.activation(wx[:, :, c], leaky[:, c, :], ACT.Exp).then_inc(s_w, 1)


def indices(k, act, idx, s_idx, s_row, i, h):
    for u in range(h * H, (h + 1) * H):
        after(act, s_row[u], 16 * i)
    s = i * U + h * H
    settled(act, k.passed)
    k.nc.scalar.activation(idx[:, h * H:(h + 1) * H],
                           k.src_step[:, s:s + H] if isinstance(s, int) else k.src_step[:, bass.ds(s, H)],
                           ACT.Copy).then_inc(s_idx, 1)


def hand_indices(k, act, idx, s_idx, s_row, i, u):
    if u == 0:
        indices(k, act, idx, s_idx, s_row, i, 1)
    if u == H and not (isinstance(i, int) and i == TURNS - 1):
        indices(k, act, idx, s_idx, s_row, i + 1, 0)


def row_steps(k, C, rows_d, acc, wx):
    k.phase()
    nc, sb, sem = k.nc, k.sb, k.sem
    W = D + 2 * C
    with ExitStack() as ctx:
        rows = sb(ctx, "rows", [P, U, D])
        weighed = sb(ctx, "weighed", [P, U, W])
        hot = sb(ctx, "hot", [P, U, P])
        idx = sb(ctx, "idx", [P, U], I32)
        ps = [k.psum(ctx, f"sum{i}", [P, 512]) for i in range(2)]
        s_idx = sem("indices")
        s_row = [sem(f"row_in{u}") for u in range(U)]
        s_hot, s_wt, s_wc, s_mm, s_acc, s_zero = (sem("hot"), sem("weighed"), sem("weights_copied"), sem("summed"),
                                                  sem("added"), sem("zeroed"))
        with nc.Block() as block:

            @block.gpsimd
            def _(pool):
                def body(i):
                    for u in range(U):
                        n = i * U + u
                        if u % H == 0:
                            pool.wait_ge(s_idx, 2 * i + u // H + 1)
                        after(pool, s_wt, n - U + 1)
                        settled(pool, k.passed)
                        pool.indirect_dma_start(
                            out=rows[:, u, :], out_offset=None, in_=rows_d,
                            in_offset=bass.IndirectOffsetOnAxis(ap=idx[:, u:u + 1], axis=0)).then_inc(s_row[u], 16)
                turns(pool, TURNS, body)

            @block.scalar
            def _(act):
                indices(k, act, idx, s_idx, s_row, 0, 0)

                def body(i):
                    for u in range(U):
                        n = i * U + u
                        hand_indices(k, act, idx, s_idx, s_row, i, u)
                        after(act, s_mm, n - U + 1)
                        w = wx[:, n, :] if isinstance(n, int) else wx[:, bass.ds(n, 1), :].rearrange("p o c -> p (o c)")
                        settled(act, k.passed)
                        nc.scalar.activation(weighed[:, u, D:W], w, ACT.Copy).then_inc(s_wc, 1)
                        if C == 1:
                            act.wait_ge(s_row[u], 16 * (i + 1))
                            settled(act, k.passed)
                            nc.scalar.activation(weighed[:, u, 0:D], rows[:, u, :], ACT.Copy,
                                                 scale=w[:, 0:1]).then_inc(s_wt, 1)
                turns(act, TURNS, body)

            @block.vector
            def _(dve):
                nc.vector.memset(acc[:, :, :], 0.0).then_inc(s_zero, 1)
                dve.wait_ge(s_zero, 1)

                def body(i):
                    blocks = blocks_of(k, mybir.EngineType.DVE, i)

                    def prepare(u):
                        n = i * U + u
                        after(dve, s_mm, n - U + 1)
                        d = k.dst_step[:, n:n + 1] if isinstance(n, int) else k.dst_step[:, bass.ds(n, 1)]
                        nc.vector.tensor_scalar(hot[:, u, :], k.iota_row[:, 0:P], d, None, ALU.is_equal).then_inc(s_hot, 1)
                        if C > 1:
                            dve.wait_ge(s_row[u], 16 * (i + 1))
                            w = wx[:, n:n + 1, 0:C] if isinstance(n, int) else wx[:, bass.ds(n, 1), 0:C]
                            nc.vector.tensor_tensor(
                                weighed[:, u, 0:D].rearrange("p (c e) -> p c e", c=C),
                                rows[:, u, :].rearrange("p (c e) -> p c e", c=C),
                                w.rearrange("p o c -> p c o").to_broadcast([P, C, D // C]), ALU.mult).then_inc(s_wt, 1)

                    def add(u):
                        n = i * U + u
                        b = blocks[u]
                        dve.wait_ge(s_mm, n + 1)
                        after(dve, s_acc, n)
                        o = acc[:, bass.ds(b, 1), :].rearrange("p o w -> p (o w)")
                        nc.vector.tensor_tensor(o, o, ps[u % 2][:, 0:W],
                                                ALU.add).then_inc(s_acc, 1)

                    for u in range(U):
                        prepare(u)
                        if u >= 2:
                            add(u - 2)
                    add(U - 2)
                    add(U - 1)
                turns(dve, TURNS, body)

            @block.tensor
            def _(pe):
                def body(i):
                    for u in range(U):
                        n = i * U + u
                        pe.wait_ge(s_hot, n + 1)
                        pe.wait_ge(s_wt, n + 1)
                        pe.wait_ge(s_wc, n + 1)
                        after(pe, s_acc, n - 1)
                        nc.tensor.matmul(ps[u % 2][:, 0:W], hot[:, u, :], weighed[:, u, :],
                                         start=True, stop=True).then_inc(s_mm, 1)
                turns(pe, TURNS, body)



def softmax_end(k, C, acc, h_d):
    k.phase()
    nc, sb, sem = k.nc, k.sb, k.sem
    with ExitStack() as ctx:
        hs = sb(ctx, "h_self", [P, SELFB, D])
        e, m, z, fe, fs = (sb(ctx, n, [P, C, SELFB]) for n in ("e_self", "e_most", "none", "f_edges", "f_self"))
        other = sb(ctx, "no_loop", [P, SELFB])
        loop = sb(ctx, "loop", [P, SELFB])
        coef = sb(ctx, "coef", [P, C, NB])
        s_dve, s_h, s_x, s_f = sem("dve"), sem("h_in"), sem("exponents"), sem("factors")
        first = slice(0, SELFB)
        with nc.Block() as block:

            @block.sync
            def _(sp):
                sp.dma_start(hs[:, :, :], h_d[0:SELFB * P, :].rearrange("(b p) d -> p b d", p=P)).then_inc(s_h, 16)

            @block.vector
            def _(dve):
                link = Chain(dve, s_dve)
                v = nc.vector
                den = acc[:, :, D:D + C].rearrange("p b c -> p c b")
                top = acc[:, first, D + C:D + 2 * C].rearrange("p b c -> p c b")
                link(v.memset(other[:, :], 0.0))
                link(v.tensor_scalar(other[:, SELFB - 1:SELFB], k.iota_part[:, :], SELF - (SELFB - 1) * P - 0.5, None, ALU.is_gt))
                link(v.tensor_scalar(loop[:, :], other[:, :], -1.0, 1.0, ALU.mult, ALU.add))
                link(v.tensor_tensor(e[:, :, :], k.node_s[:, 0:C, first], k.node_s[:, HEADS:HEADS + C, first], ALU.add))
                link(v.scalar_tensor_tensor(out=e[:, :, :], in0=e[:, :, :], scalar=0.2, in1=e[:, :, :], op0=ALU.mult, op1=ALU.max))
                for c in range(C):
                    link(v.scalar_tensor_tensor(out=e[:, c, :], in0=other[:, :], scalar=-BIG, in1=e[:, c, :],
                                                op0=ALU.mult, op1=ALU.add))
                link(v.tensor_scalar(z[:, :, :], den[:, :, first], 0.0, -BIG, ALU.is_equal, ALU.mult))
                link(v.tensor_tensor(m[:, :, :], top, z[:, :, :], ALU.add))
                link(v.tensor_tensor(z[:, :, :], m[:, :, :], e[:, :, :], ALU.max))
                link(v.tensor_tensor(m[:, :, :], m[:, :, :], z[:, :, :], ALU.subtract))
                v.tensor_tensor(e[:, :, :], e[:, :, :], z[:, :, :], ALU.subtract).then_inc(s_x, 1)
                link(v.tensor_copy(coef[:, :, :], den))
                dve.wait_ge(s_f, 2)
                for c in range(C):
                    link(v.tensor_tensor(fs[:, c, :], fs[:, c, :], loop[:, :], ALU.mult))
                link(v.tensor_tensor(coef[:, :, first], coef[:, :, first], fe[:, :, :], ALU.mult))
                link(v.tensor_tensor(coef[:, :, first], coef[:, :, first], fs[:, :, :], ALU.add))
                link(v.tensor_scalar(coef[:, :, :], coef[:, :, :], 1e-30, None, ALU.max))
                link(v.reciprocal(coef[:, :, :], coef[:, :, :]))
                link(v.tensor_tensor(fs[:, :, :], fs[:, :, :], coef[:, :, first], ALU.mult))
                link(v.tensor_tensor(coef[:, :, first], coef[:, :, first], fe[:, :, :], ALU.mult))
                dve.wait_ge(s_h, 16)
                for c in range(C):
                    o = slice(c * D // C, (c + 1) * D // C)
                    link(v.tensor_tensor(acc[:, :, o], acc[:, :, o], coef[:, c, :].unsqueeze(2).to_broadcast([P, NB, D // C]), ALU.mult))
                    link(v.tensor_tensor(hs[:, :, o], hs[:, :, o], fs[:, c, :].unsqueeze(2).to_broadcast([P, SELFB, D // C]), ALU.mult))
                link(v.tensor_tensor(acc[:, first, 0:D], acc[:, first, 0:D], hs[:, :, :], ALU.add))

            @block.scalar
            def _(act):
                act.wait_ge(s_x, 1)
                act.wait_ge(s_dve, 3 + 2 + C + 4)
                nc.scalar.activation(fe[:, :, :], m[:, :, :], ACT.Exp).then_inc(s_f, 1)
                nc.scalar.activation(fs[:, :, :], e[:, :, :], ACT.Exp).then_inc(s_f, 1)


def norm_factors(k, dve, link, x, stats, mean, rstd, s_var, s_root):
    v = k.nc.vector
    with dve.Fori(0, NB) as n:
        v.bn_stats(at(stats, n), at(x, n)).then_inc(s_var, 1)
    dve.wait_ge(s_var, NB)
    me, ve, mo, vo = (stats[:, :, q] for q in (1, 2, 4, 5))
    link(v.tensor_tensor(mean, me, mo, ALU.subtract))
    link(v.tensor_tensor(mean, mean, mean, ALU.mult))
    link(v.tensor_tensor(rstd, ve, vo, ALU.add))
    link(v.tensor_scalar(rstd, rstd, 1.0 / D, EPS, ALU.mult, ALU.add))
    link(v.scalar_tensor_tensor(out=rstd, in0=mean, scalar=0.25, in1=rstd, op0=ALU.mult, op1=ALU.add))
    link(v.tensor_tensor(mean, me, mo, ALU.add))
    v.tensor_scalar(mean, mean, 0.5, None, ALU.mult).then_inc(s_var, 1)
    dve.wait_ge(s_var, NB + 1)
    dve.wait_ge(s_root, 1)
    link(v.reciprocal(rstd, rstd))


def at(x, n):
    return x[:, n, :] if isinstance(n, int) else x[:, bass.ds(n, 1), :].rearrange("p o d -> p (o d)")


def col(x, n):
    return x[:, n:n + 1] if isinstance(n, int) else x[:, bass.ds(n, 1)]


def gat_epilogue_1(k, acc):
    nc, sb, sem = k.nc, k.sb, k.sem
    softmax_end(k, HEADS, acc, k.h1_d)
    k.phase()
    W = D + 2
    with ExitStack() as ctx:
        w = sb(ctx, "w2x", [P, 2, W])
        av = sb(ctx, "a2_rows", [P, 2, D])
        wa = sb(ctx, "w2_times_a", [P, 2, D])
        vec = sb(ctx, "affine", [P, 3, D])
        stats, mean, var, rstd = sb(ctx, "stats", [P, NB, 6]), sb(ctx, "mean", [P, NB]), sb(ctx, "var", [P, NB]), sb(ctx, "rstd", [P, NB])
        eps = sb(ctx, "zero", [P, 1])
        y = sb(ctx, "normed", [P, NODE_U, D])
        xin = sb(ctx, "xin", [P, NODE_U, D])
        hout = sb(ctx, "hout", [P, NODE_U, D])
        xt = [sb(ctx, f"xt{i}", [P, 2, P]) for i in range(2)]
        tps = [k.psum(ctx, f"tps{i}", [P, 2, P]) for i in range(2)]
        ops = [k.psum(ctx, f"ops{i}", [P, 512]) for i in range(2)]
        s_w, s_wx, s_dve, s_var, s_root = sem("weights_in"), sem("weights_ready"), sem("dve"), sem("statistics"), sem("root")
        s_y, s_x = sem("normed"), sem("relu")
        s_st = [sem(f"h_stored{u}") for u in range(NODE_U)]
        s_tp, s_xt, s_mm, s_out, s_ev = sem("turned"), sem("turned_copied"), sem("product"), sem("product_read"), sem("h_ready")
        with nc.Block() as block:

            @block.sync
            def _(sp):
                sp.dma_start(w[:, :, 0:D], k.a["L0_gnn_W2"].rearrange("(c p) n -> p c n", p=P)).then_inc(s_w, 16)
                for m, n in enumerate(("L0_gnn_a2_src", "L0_gnn_a2_dst")):
                    sp.dma_start(av[:, m, :], k.a[n].rearrange("h c -> (h c)").partition_broadcast(P)).then_inc(s_w, 16)
                for m, n in enumerate(("L0_gnn_b1", "L0_gnn_ln_g", "L0_gnn_ln_b")):
                    sp.dma_start(vec[:, m, :], k.a[n].partition_broadcast(P)).then_inc(s_w, 16)

            @block.vector
            def _(dve):
                link = Chain(dve, s_dve)
                v = nc.vector
                dve.wait_ge(s_w, 16 * 6)
                for m in range(2):
                    link(v.tensor_tensor(wa[:, :, :], w[:, :, 0:D], av[:, m:m + 1, :].to_broadcast([P, 2, D]), ALU.mult))
                    v.tensor_reduce(w[:, :, D + m:D + m + 1], wa[:, :, :].unsqueeze(2), AX_X, ALU.add).then_inc(s_wx, 1)
                    dve.wait_ge(s_wx, m + 1)
                link(v.tensor_tensor(acc[:, :, 0:D], acc[:, :, 0:D], vec[:, 0:1, :].to_broadcast([P, NB, D]), ALU.add))
                norm_factors(k, dve, link, acc[:, :, 0:D], stats, mean[:, :], rstd[:, :], s_var, s_root)

                def body(i):
                    def norm(u):
                        n = i * NODE_U + u
                        after(dve, s_x, n - NODE_U + 1)
                        v.tensor_scalar(y[:, u, :], at(acc, n)[:, 0:D], col(mean, n), col(rstd, n),
                                        ALU.subtract, ALU.mult).then_inc(s_y, 1)
                        dve.wait_ge(s_y, 3 * n + 1)
                        v.tensor_tensor(y[:, u, :], y[:, u, :], vec[:, 1, :], ALU.mult).then_inc(s_y, 1)
                        dve.wait_ge(s_y, 3 * n + 2)
                        v.tensor_tensor(y[:, u, :], y[:, u, :], vec[:, 2, :], ALU.add).then_inc(s_y, 1)

                    def copy(u):
                        n = i * NODE_U + u
                        dve.wait_ge(s_tp, n + 1)
                        after(dve, s_mm, n - 1 if u else n)
                        v.tensor_copy(xt[u % 2][:, :, :], tps[u % 2][:, :, :]).then_inc(s_xt, 1)

                    for u in range(NODE_U):
                        norm(u)
                        if u:
                            copy(u - 1)
                    copy(NODE_U - 1)
                turns(dve, NODE_TURNS, body)

            @block.tensor
            def _(pe):
                pe.wait_ge(s_wx, 2)
                pe_project(k, pe, xin, NODE_U, lambda e, i, u: e.wait_ge(s_x, i * NODE_U + u + 1), tps, s_tp, s_xt, xt,
                           [(0, [(c, w[:, c, :]) for c in range(2)])], ops, s_mm, s_out, [(0, P), (P, P)])

            @block.scalar
            def _(act):
                act.wait_ge(s_var, NB + 1)
                nc.scalar.activation(rstd[:, :], rstd[:, :], ACT.Sqrt).then_inc(s_root, 1)

                def body(i):
                    def relu(u):
                        n = i * NODE_U + u
                        act.wait_ge(s_y, 3 * n + 3)
                        after(act, s_tp, n - NODE_U + 1)
                        nc.scalar.activation(xin[:, u, :], y[:, u, :], ACT.Relu).then_inc(s_x, 1)

                    def store(u):
                        n = i * NODE_U + u
                        act.wait_ge(s_mm, n + 1)
                        after(act, s_st[u], 16 * i)
                        nc.scalar.activation(hout[:, u, :], ops[u % 2][:, 0:D], ACT.Copy).then_inc(s_ev, 1)
                        o = k.node_s[:, 0:2 * HEADS:HEADS, n:n + 1] if isinstance(n, int) else k.node_s[:, 0:2 * HEADS:HEADS, bass.ds(n, 1)]
                        nc.scalar.activation(o, ops[u % 2][:, D:W].rearrange("p (c o) -> p c o", o=1), ACT.Copy).then_inc(s_out, 1)
                        act.wait_ge(s_ev, n + 1)
                        act.dma_start(rows_of(k.h2_d, n), hout[:, u, :]).then_inc(s_st[u], 16)

                    for u in range(NODE_U):
                        relu(u)
                        if u:
                            store(u - 1)
                    store(NODE_U - 1)
                turns(act, NODE_TURNS, body)
                for u in range(NODE_U):
                    act.wait_ge(s_st[u], 16 * NODE_TURNS)


def load_nodes(k, sp, x_d, tile, s):
    sp.dma_start(tile[:, 0:NFULL, :], x_d[0:NFULL * P, :].rearrange("(b p) d -> p b d", p=P)).then_inc(s, 16)
    sp.dma_start(tile[0:NLAST, NFULL, :], x_d[NFULL * P:N, :]).then_inc(s, 16)


def gat_epilogue_2(k, acc):
    nc, sb, sem = k.nc, k.sb, k.sem
    softmax_end(k, 1, acc, k.h2_d)
    k.phase()
    with ExitStack() as ctx:
        x = sb(ctx, "x_all", [P, NB, D])
        b2 = sb(ctx, "b2_row", [P, D])
        w3 = sb(ctx, "w3", [P, 6, 3 * D])
        arow = sb(ctx, "a_row", [P, 3 * D])
        wv = sb(ctx, "w3_a", [P, 6])
        wb = sb(ctx, "w3_a_wide", [P, 2, P])
        rel = sb(ctx, "rel_rows", [P, 2, D])
        wrow = sb(ctx, "w_rel_row", [P, D])
        w = sb(ctx, "w_cols", [P, 2, 2])
        stats, mean, rstd = sb(ctx, "stats", [P, NB, 6]), sb(ctx, "mean", [P, NB]), sb(ctx, "rstd", [P, NB])
        xin = sb(ctx, "xin", [P, NODE_U, D + 1])
        xt = [sb(ctx, f"xt{i}", [P, 2, P]) for i in range(2)]
        tps = [k.psum(ctx, f"tps{i}", [P, 2, P]) for i in range(2)]
        ops = [k.psum(ctx, f"ops{i}", [P, 512]) for i in range(2)]
        wps = k.psum(ctx, "w_row_ps", [P, 2, P])
        s_in, s_zero, s_dve, s_var, s_root = sem("in"), sem("zeroed"), sem("dve"), sem("statistics"), sem("root")
        s_wb, s_wp, s_x = sem("w_wide"), sem("w_row"), sem("normed")
        s_st = [sem(f"x1_stored{u}") for u in range(NODE_U)]
        s_tp, s_xt, s_mm, s_out, s_sc = (sem("turned"), sem("turned_copied"), sem("product"), sem("product_read"),
                                         sem("score_beside"))
        with nc.Block() as block:

            @block.gpsimd
            def _(pool):
                nc.gpsimd.memset(x[:, NFULL, :], 0.0).then_inc(s_zero, 1)
                nc.gpsimd.memset(rel[:, :, :], 0.0).then_inc(s_zero, 1)

            @block.sync
            def _(sp):
                sp.wait_ge(s_zero, 2)
                load_nodes(k, sp, k.a["x"], x, s_in)
                sp.dma_start(b2[:, :], k.a["L0_gnn_b2"].partition_broadcast(P)).then_inc(s_in, 16)
                sp.dma_start(w3[:, :, :], k.a["L1_gnn_W3"].rearrange("(q p) n -> p q n", p=P)).then_inc(s_in, 16)
                sp.dma_start(arow[:, :], k.a["L1_gnn_a"].rearrange("n o -> (n o)").partition_broadcast(P)).then_inc(s_in, 16)
                sp.dma_start(rel[:, 0, :], k.a["L1_gnn_rel_emb"][0:P, :]).then_inc(s_in, 16)
                sp.dma_start(rel[0:REL - P, 1, :], k.a["L1_gnn_rel_emb"][P:REL, :]).then_inc(s_in, 16)

            @block.vector
            def _(dve):
                link = Chain(dve, s_dve)
                v = nc.vector
                dve.wait_ge(s_in, 16 * 7)
                link(v.tensor_tensor(w3[:, :, :], w3[:, :, :], arow[:, :].unsqueeze(1).to_broadcast([P, 6, 3 * D]), ALU.mult))
                link(v.tensor_reduce(wv[:, :], w3[:, :, :], AX_X, ALU.add))
                for q in range(2):
                    v.tensor_copy(wb[:, q, :], wv[:, 4 + q:5 + q].to_broadcast([P, P])).then_inc(s_wb, 1)
                v.tensor_copy(w[:, :, :], wv[:, 0:4].rearrange("p (m c) -> p c m", m=2)).then_inc(s_wb, 1)
                dve.wait_ge(s_wp, 1)
                link(v.tensor_copy(wrow[:, :], wps[:, :, :].rearrange("p q n -> p (q n)")))
                link(v.tensor_tensor(rel[:, :, :], rel[:, :, :], wrow[:, :].unsqueeze(1).to_broadcast([P, 2, D]), ALU.mult))
                link(v.tensor_reduce(k.srel[:, :], rel[:, :, :], AX_X, ALU.add))
                link(v.tensor_tensor(x[:, :, :], x[:, :, :], acc[:, :, 0:D], ALU.add))
                link(v.tensor_tensor(x[:, :, :], x[:, :, :], b2[:, :].unsqueeze(1).to_broadcast([P, NB, D]), ALU.add))
                norm_factors(k, dve, link, x, stats, mean[:, :], rstd[:, :], s_var, s_root)

                def body(i):
                    def norm(u):
                        n = i * NODE_U + u
                        after(dve, s_tp, n - NODE_U + 1)
                        after(dve, s_st[u], 16 * i)
                        v.tensor_scalar(xin[:, u, 0:D], at(x, n), col(mean, n), col(rstd, n),
                                        ALU.subtract, ALU.mult).then_inc(s_x, 1)

                    def copy(u):
                        n = i * NODE_U + u
                        dve.wait_ge(s_tp, n + 1)
                        after(dve, s_mm, n - 1 if u else n)
                        v.tensor_copy(xt[u % 2][:, :, :], tps[u % 2][:, :, :]).then_inc(s_xt, 1)

                    for u in range(NODE_U):
                        norm(u)
                        if u:
                            copy(u - 1)
                    copy(NODE_U - 1)
                turns(dve, NODE_TURNS, body)

            @block.tensor
            def _(pe):
                pe.wait_ge(s_wb, 3)
                for q in range(2):
                    last = nc.tensor.matmul(wps[:, q, :], wb[:, q, :], k.ident[:, :], start=True, stop=True)
                last.then_inc(s_wp, 1)
                pe_project(k, pe, xin, NODE_U, lambda e, i, u: e.wait_ge(s_x, i * NODE_U + u + 1), tps, s_tp, s_xt, xt,
                           [(0, [(c, w[:, c, :]) for c in range(2)])], ops, s_mm, s_out, [(0, P), (P, P)])

            @block.scalar
            def _(act):
                act.wait_ge(s_var, NB + 1)
                nc.scalar.activation(rstd[:, :], rstd[:, :], ACT.Sqrt).then_inc(s_root, 1)

                def body(i):
                    for u in range(NODE_U):
                        n = i * NODE_U + u
                        act.wait_ge(s_mm, n + 1)
                        after(act, s_st[u], 16 * i)
                        settled(act, k.passed)
                        nc.scalar.activation(xin[:, u, D:D + 1], ops[u % 2][:, 0:1], ACT.Copy).then_inc(s_sc, 1)
                        nc.scalar.activation(col(k.node_s[:, HEADS, :], n), ops[u % 2][:, 1:2], ACT.Copy).then_inc(s_out, 1)
                        act.wait_ge(s_sc, n + 1)
                        act.wait_ge(s_x, n + 1)
                        act.dma_start(rows_of(k.x1_d, n), xin[:, u, :]).then_inc(s_st[u], 16)
                turns(act, NODE_TURNS, body)
                for u in range(NODE_U):
                    act.wait_ge(s_st[u], 16 * NODE_TURNS)


ONE_HOT = D + 1
ONES = ONE_HOT + REL
RW_COLS = ONES + 1


def relation_layer(k, ctx):
    acc = k.sb(ctx, "acc", [P, NB, RW_COLS])
    with ExitStack() as inner:
        ed = k.sb(inner, "ed_step", [P, STEPS, 1])
        lookup_dst(k, 1, k.node_s[:, HEADS:HEADS + 1, :], ed, rel=k.srel[:, :])
        relation_steps(k, acc, ed[:, :, 0])
    return acc


def relation_steps(k, acc, rest_of_score):
    k.phase()
    nc, sb, sem = k.nc, k.sb, k.sem
    W = RW_COLS
    with ExitStack() as ctx:
        rows = sb(ctx, "rows", [P, U, W])
        hot = sb(ctx, "hot", [P, U, P])
        idx = sb(ctx, "idx", [P, U], I32)
        part = sb(ctx, "score", [P, 2, H])
        inv = sb(ctx, "inverse", [P, 2, H])
        alpha = sb(ctx, "alpha", [P, 2, H])
        away = sb(ctx, "distance", [P, 2, REL])
        ps = [k.psum(ctx, f"sum{i}", [P, 512]) for i in range(2)]
        s_idx = sem("indices")
        s_row = [sem(f"row_in{u}") for u in range(U)]
        s_hot, s_rel, s_mm, s_acc, s_zero = sem("hot"), sem("relation_hot"), sem("summed"), sem("added"), sem("zeroed")
        s_sum, s_score, s_exp, s_inv, s_alpha, s_away = (sem("score_sum"), sem("score"), sem("exp"), sem("inverse"),
                                                         sem("alpha"), sem("distance"))
        with nc.Block() as block:

            @block.gpsimd
            def _(pool):
                def body(i):
                    for u in range(U):
                        n = i * U + u
                        if u % H == 0:
                            pool.wait_ge(s_idx, 2 * i + u // H + 1)
                        after(pool, s_mm, n - U + 1)
                        settled(pool, k.passed)
                        pool.indirect_dma_start(
                            out=rows[:, u, 0:D + 1], out_offset=None, in_=k.x1_d,
                            in_offset=bass.IndirectOffsetOnAxis(ap=idx[:, u:u + 1], axis=0)).then_inc(s_row[u], 16)
                turns(pool, TURNS, body)

            @block.scalar
            def _(act):
                indices(k, act, idx, s_idx, s_row, 0, 0)

                def body(i):
                    for u in range(U):
                        n = i * U + u
                        hand_indices(k, act, idx, s_idx, s_row, i, u)
                        if u % H == 0:
                            act.wait_ge(s_score, 2 * i + u // H + 1)
                            nc.scalar.activation(part[:, u // H, 0:H], part[:, u // H, 0:H], ACT.Exp).then_inc(s_exp, 1)
                        after(act, s_mm, n - U + 1)
                        settled(act, k.passed)
                        nc.scalar.activation(away[:, u % 2, :], k.iota_row[:, 0:REL], ACT.Abs, scale=-1.0,
                                             bias=col(k.et_step, n)).then_inc(s_away, 1)
                        act.wait_ge(s_away, n + 1)
                        nc.scalar.activation(rows[:, u, ONE_HOT:ONES], away[:, u % 2, :], ACT.Relu, scale=-1.0,
                                             bias=1.0).then_inc(s_rel, 1)
                turns(act, TURNS, body)

            @block.vector
            def _(dve):
                nc.vector.memset(acc[:, :, :], 0.0).then_inc(s_zero, 1)
                nc.vector.memset(rows[:, :, ONES:W], 1.0).then_inc(s_zero, 1)
                dve.wait_ge(s_zero, 2)

                def body(i):
                    blocks = blocks_of(k, mybir.EngineType.DVE, i)

                    def score(h):
                        t, s, us = 2 * i + h, i * U + h * H, slice(h * H, (h + 1) * H)
                        for u in range(h * H, (h + 1) * H):
                            dve.wait_ge(s_row[u], 16 * (i + 1))
                        r = rest_of_score[:, s:s + H] if isinstance(s, int) else rest_of_score[:, bass.ds(s, H)]
                        nc.vector.tensor_tensor(part[:, h, :], rows[:, us, D], r, ALU.add).then_inc(s_sum, 1)
                        dve.wait_ge(s_sum, t + 1)
                        nc.vector.scalar_tensor_tensor(out=part[:, h, :], in0=part[:, h, :], scalar=0.01,
                                                       in1=part[:, h, :], op0=ALU.mult, op1=ALU.max).then_inc(s_score, 1)

                    def weights(h):
                        t = 2 * i + h
                        dve.wait_ge(s_exp, t + 1)
                        nc.vector.reciprocal(inv[:, h, :], part[:, h, :]).then_inc(s_inv, 1)
                        dve.wait_ge(s_inv, t + 1)
                        after(dve, s_mm, t * H)
                        nc.vector.tensor_tensor(alpha[:, h, :], part[:, h, :], inv[:, h, :], ALU.mult).then_inc(s_alpha, 1)
                        dve.wait_ge(s_alpha, t + 1)

                    def prepare(u):
                        n = i * U + u
                        if u % H == 0:
                            weights(u // H)
                        after(dve, s_mm, n - U + 1)
                        nc.vector.tensor_scalar(hot[:, u, :], k.iota_row[:, 0:P], col(k.dst_step, n),
                                                alpha[:, u // H, u % H:u % H + 1],
                                                ALU.is_equal, ALU.mult).then_inc(s_hot, 1)

                    def add(u):
                        n = i * U + u
                        b = blocks[u]
                        dve.wait_ge(s_mm, n + 1)
                        after(dve, s_acc, n)
                        o = at(acc, b)
                        nc.vector.tensor_tensor(o, o, ps[u % 2][:, 0:W], ALU.add).then_inc(s_acc, 1)

                    for u in range(U):
                        if u % H == 0:
                            score(u // H)
                        prepare(u)
                        if u >= 2:
                            add(u - 2)
                    add(U - 2)
                    add(U - 1)
                turns(dve, TURNS, body)

            @block.tensor
            def _(pe):
                pe.wait_ge(s_zero, 2)

                def body(i):
                    for u in range(U):
                        n = i * U + u
                        pe.wait_ge(s_row[u], 16 * (i + 1))
                        pe.wait_ge(s_hot, n + 1)
                        pe.wait_ge(s_rel, n + 1)
                        after(pe, s_acc, n - 1)
                        nc.tensor.matmul(ps[u % 2][:, 0:W], hot[:, u, :], rows[:, u, :],
                                         start=True, stop=True).then_inc(s_mm, 1)
                turns(pe, TURNS, body)


def relation_epilogue(k, acc):
    k.phase()
    nc, sb, sem = k.nc, k.sb, k.sem
    X1 = ONES
    WX = X1 + D
    chunks = [(0, P), (P, P), (ONE_HOT, P), (ONE_HOT + P, REL - P), (X1, P), (X1 + P, P)]
    with ExitStack() as ctx:
        x = sb(ctx, "x1_all", [P, NB, D])
        wn = sb(ctx, "w_neighbour", [P, 2, D])
        wr = sb(ctx, "rel_times_wn", [P, 2, D])
        wl = sb(ctx, "loop_weights", [P, 2, 2 * D])
        some = sb(ctx, "has_edges", [P, NB])
        stats, mean, rstd = sb(ctx, "stats", [P, NB, 6]), sb(ctx, "mean", [P, NB]), sb(ctx, "rstd", [P, NB])
        s_in, s_dve, s_var, s_root = sem("in"), sem("dve"), sem("statistics"), sem("root")
        with ExitStack() as c2:
            rel = sb(c2, "rel_rows", [P, 2, D])
            relt = sb(c2, "rel_turned", [P, 2, 2 * P])
            rps = k.psum(c2, "rel_ps", [P, 2, 2, P])
            wps = [k.psum(c2, f"wr_ps{i}", [P, 512]) for i in range(2)]
            s_zero, s_rt, s_rc, s_wr = sem("zeroed"), sem("rel_turned"), sem("rel_copied"), sem("rel_product")
            with nc.Block() as block:

                @block.gpsimd
                def _(pool):
                    nc.gpsimd.memset(rel[:, :, :], 0.0).then_inc(s_zero, 1)

                @block.sync
                def _(sp):
                    sp.dma_start(x[:, :, :], k.x1_d[:, 0:D].rearrange("(b p) d -> p b d", p=P)).then_inc(s_in, 16)
                    sp.dma_start(wn[:, :, :], k.a["L1_gnn_weight_neighbor"].rearrange("(c p) n -> p c n", p=P)).then_inc(s_in, 16)
                    for m, n in enumerate(("L1_gnn_loop_weight", "L1_gnn_evolve_loop_weight")):
                        sp.dma_start(wl[:, :, m * D:(m + 1) * D], k.a[n].rearrange("(c p) n -> p c n", p=P)).then_inc(s_in, 16)
                    sp.wait_ge(s_zero, 1)
                    sp.dma_start(rel[:, 0, :], k.a["L1_gnn_rel_emb"][0:P, :]).then_inc(s_in, 16)
                    sp.dma_start(rel[0:REL - P, 1, :], k.a["L1_gnn_rel_emb"][P:REL, :]).then_inc(s_in, 16)
                    sp.wait_ge(s_in, 96)

                @block.tensor
                def _(pe):
                    pe.wait_ge(s_in, 96)
                    for r in range(2):
                        for c in range(2):
                            last = nc.tensor.transpose(rps[:, c, r, :], rel[:, r, c * P:(c + 1) * P], k.ident[:, :])
                    last.then_inc(s_rt, 1)
                    pe.wait_ge(s_rc, 1)
                    for r in range(2):
                        for c in range(2):
                            last = nc.tensor.matmul(wps[r][:, 0:D], relt[:, c, r * P:(r + 1) * P], wn[:, c, :],
                                                    start=(c == 0), stop=(c == 1))
                    last.then_inc(s_wr, 1)

                @block.vector
                def _(dve):
                    link = Chain(dve, s_dve)
                    dve.wait_ge(s_rt, 1)
                    nc.vector.tensor_copy(relt[:, :, :], rps[:, :, :, :].rearrange("p c r n -> p c (r n)")).then_inc(s_rc, 1)
                    dve.wait_ge(s_wr, 1)
                    for r in range(2):
                        link(nc.vector.tensor_copy(wr[:, r, :], wps[r][:, 0:D]))
                    link(nc.vector.tensor_scalar(some[:, :], acc[:, :, ONES], 0.0, None, ALU.is_gt))
        with ExitStack() as c2:
            xin = sb(c2, "xin", [P, 2, WX])
            xt = [t[:, 0:6 * P].rearrange("p (c n) -> p c n", c=6) for t in (k.first_step, k.iota_row)]
            mix = [t[:, 0:2 * D].rearrange("p (m d) -> p m d", m=2) for t in (k.dst_step, k.et_step)]
            s_x, s_tp, s_xt, s_mm, s_nb, s_lp, s_mix = (sem(n) for n in (
                "xin", "turned", "turned_copied", "product", "messages_read", "part_copied", "mixed"))
            with ExitStack() as c3:
                tps = [k.psum(c3, f"tps{i}", [P, 8, P]) for i in range(2)]
                ops = [k.psum(c3, f"ops{i}", [P, 1024]) for i in range(2)]
                with nc.Block() as block:

                    @block.tensor
                    def _(pe):
                        ws = [wn[:, 0, :], wn[:, 1, :], wr[:, 0, :], wr[0:REL - P, 1, :]]
                        pe_project(k, pe, xin, 2, lambda e, i, u: e.wait_ge(s_x, 2 * (i * NODE_U + u + 1)), tps, s_tp, s_xt, xt,
                                   [(0, [(4, wl[:, 0, :]), (5, wl[:, 1, :])]), (512, list(enumerate(ws)))],
                                   ops, s_mm, s_mix, chunks, per=4)

                    @block.scalar
                    def _(act):
                        def body(i):
                            def load(u):
                                n = i * NODE_U + u
                                after(act, s_tp, n - 1 if u else n)
                                settled(act, k.passed)
                                nc.scalar.activation(xin[:, u % 2, 0:X1], at(acc, n)[:, 0:X1], ACT.Copy).then_inc(s_x, 1)
                                nc.scalar.activation(xin[:, u % 2, X1:WX], at(x, n), ACT.Copy).then_inc(s_x, 1)

                            def read(u):
                                n = i * NODE_U + u
                                act.wait_ge(s_mm, n + 1)
                                after(act, s_mix, 4 * (n - 1 if u else n))
                                nc.scalar.activation(mix[u % 2][:, 0, :], ops[u % 2][:, 512:512 + D], ACT.Relu).then_inc(s_nb, 1)
                                nc.scalar.activation(mix[u % 2][:, 1, :], ops[u % 2][:, D:2 * D], ACT.Copy).then_inc(s_nb, 1)

                            for u in range(NODE_U):
                                load(u)
                                if u:
                                    read(u - 1)
                            read(NODE_U - 1)
                        turns(act, NODE_TURNS, body)

                    @block.vector
                    def _(dve):
                        v = nc.vector

                        def body(i):
                            def copy(u):
                                n = i * NODE_U + u
                                dve.wait_ge(s_tp, n + 1)
                                after(dve, s_mm, n - 1 if u else n)
                                for lo, hi, p in ((0, 3, P), (3, 4, REL - P), (4, 6, P)):
                                    last = v.tensor_copy(xt[u % 2][0:p, lo:hi, :], tps[u % 2][0:p, lo:hi, :])
                                    if lo < 4:
                                        last.then_inc(s_lp, 1)
                                last.then_inc(s_xt, 1)

                            def join(u):
                                n = i * NODE_U + u
                                dve.wait_ge(s_nb, 2 * n + 2)
                                m0, m1 = mix[u % 2][:, 0, :], mix[u % 2][:, 1, :]
                                xn = at(x, n)
                                v.tensor_tensor(xn, xn, m0, ALU.add).then_inc(s_mix, 1)
                                dve.wait_ge(s_mix, 4 * n + 1)
                                v.tensor_tensor(xn, xn, m1, ALU.add).then_inc(s_mix, 1)
                                dve.wait_ge(s_mix, 4 * n + 2)
                                v.tensor_tensor(m1, ops[u % 2][:, 0:D], m1, ALU.subtract).then_inc(s_mix, 1)
                                dve.wait_ge(s_mix, 4 * n + 3)
                                v.scalar_tensor_tensor(out=xn, in0=m1, scalar=col(some, n), in1=xn, op0=ALU.mult,
                                                       op1=ALU.add).then_inc(s_mix, 1)

                            for u in range(NODE_U):
                                copy(u)
                                if u:
                                    join(u - 1)
                            join(NODE_U - 1)
                        turns(dve, NODE_TURNS, body)
        s_done, s_st = sem("normed"), sem("stored")
        y = acc[:, :, 0:D]
        with nc.Block() as block:

            @block.vector
            def _(dve):
                link = Chain(dve, s_dve, 3)
                norm_factors(k, dve, link, x, stats, mean[:, :], rstd[:, :], s_var, s_root)
                with dve.Fori(0, NB) as n:
                    nc.vector.tensor_scalar(at(y, n), at(x, n), col(mean, n), col(rstd, n),
                                            ALU.subtract, ALU.mult).then_inc(s_done, 1)

            @block.scalar
            def _(act):
                act.wait_ge(s_var, NB + 1)
                nc.scalar.activation(rstd[:, :], rstd[:, :], ACT.Sqrt).then_inc(s_root, 1)

            @block.sync
            def _(sp):
                for q in range(4):
                    lo, hi = q * 12, (q + 1) * 12
                    sp.wait_ge(s_done, hi)
                    sp.dma_start(k.out[lo * P:hi * P, :].rearrange("(b p) d -> p b d", p=P), y[:, lo:hi, :]).then_inc(s_st, 16)
                sp.wait_ge(s_done, NB)
                sp.dma_start(k.out[NFULL * P:N, :], y[0:NLAST, NFULL, :]).then_inc(s_st, 16)
                sp.wait_ge(s_st, 16 * 5)


_INS = ["x", "src", "dst", "edge_type_200", "L0_gnn_W1", "L0_gnn_a1_src", "L0_gnn_a1_dst", "L0_gnn_b1", "L0_gnn_ln_g",
        "L0_gnn_ln_b", "L0_gnn_W2", "L0_gnn_a2_src", "L0_gnn_a2_dst", "L0_gnn_b2", "L1_gnn_rel_emb",
        "L1_gnn_weight_neighbor", "L1_gnn_a", "L1_gnn_W3", "L1_gnn_loop_weight", "L1_gnn_evolve_loop_weight"]


def kernel(**inputs):
    import numpy as _np
    import concourse.bacc as _bacc
    from concourse import mybir as _mybir
    from concourse.bass_utils import run_bass_kernel_spmd as _run

    nc = _bacc.Bacc("TRN2", target_bir_lowering=False, num_devices=1)
    arrays, args = {}, {}
    for name in _INS:
        a = _np.ascontiguousarray(inputs[name])
        arrays[f"in_{name}_dram"] = a
        args[name] = nc.dram_tensor(f"in_{name}_dram", a.shape, _mybir.dt.from_np(a.dtype), kind="ExternalInput").ap()
    out = nc.dram_tensor("out_0_dram", (N, D), _mybir.dt.float32, kind="ExternalOutput").ap()
    program(nc, args, out)
    r = _run(nc, [arrays], core_ids=[0])
    return r.results[0]["out_0_dram"]
```

```python
from contextlib import ExitStack

import concourse.bass as bass
from concourse import mybir

F32 = mybir.dt.float32
BF16 = mybir.dt.bfloat16
I32 = mybir.dt.int32
ALU = mybir.AluOpType
ACT = mybir.ActivationFunctionType
AX_X = mybir.AxisListType.X

P = 128
N, D, E = 6250, 256, 100000
NB = -(-N // P)
NFULL, NLAST = N // P, N % P
TILES = -(-E // P)
TPR = 7
RW = TPR * P
ROWS = -(-TILES // TPR)
EFULL, ELAST = E // RW, E % RW
U = 16
H = U // 2
QS = U // 4
LAG = 2
TURNS = -(-(TILES + NB - 1) // U)
STEPS = TURNS * U
HALF = STEPS // 2
NCH = -(-STEPS // P)
SELF = 1250
SELFB = -(-SELF // P)
HEADS, HID = 4, 64
REL = 200
BIG = 1e30
SRC_END, ET_END = 1 << 13, 1 << 8
PAD_DST = 8191
NODE_U = 7
NODE_TURNS = NB // NODE_U
EPS = 1e-5
assert HALF * 2 == STEPS and HALF <= 512
assert NODE_TURNS * NODE_U == NB and EFULL == ROWS - 1 and ROWS * TPR >= TILES
assert STEPS % (4 * U) == 0


class Chain:

    def __init__(self, eng, sem, base=0):
        self.eng, self.sem, self.base, self.n = eng, sem, base, 0

    def __call__(self, ins):
        ins.then_inc(self.sem, 1)
        self.n += 1
        self.eng.wait_ge(self.sem, self.base + self.n)


def after(eng, sem, value):
    if not (isinstance(value, int) and value <= 0):
        eng.wait_ge(sem, value)


def settled(eng, passed):
    eng.sem_inc(passed, 1)


def blocks_of(k, engine, i, n=U):
    steps = k.block_of[0:1, i * n:(i + 1) * n] if isinstance(i, int) else k.block_of[0:1, bass.ds(i * n, n)]
    return k.nc.values_load_multi_w_load_instructions(
        steps, engines=[engine], min_val=0, max_val=NB - 1,
        skip_runtime_bounds_check_because="step s = tile + block, with 0 <= tile < TILES counted up to s")[1]


def turns(eng, n, body):
    body(0)
    with eng.Fori(1, n - 1) as i:
        body(i)
    body(n - 1)


def program(nc, a, out):
    with ExitStack() as top:
        k = Kernel(nc, a, out, top)
        edge_structure(k)
        first_projection(k)
        with ExitStack() as ctx:
            acc, _ = gat_layer(k, ctx, HEADS, k.h1_d, k.es1_d)
            gat_epilogue_1(k, acc)
        with ExitStack() as ctx:
            acc, residual = gat_layer(k, ctx, 1, k.h2_d, k.es2_d, True)
            gat_epilogue_2(k, acc, residual)
        with ExitStack() as ctx:
            acc = relation_layer(k, ctx)
            relation_epilogue(k, acc)


class Kernel:

    def __init__(self, nc, a, out, ctx):
        self.nc, self.a, self.out, self.ctx = nc, a, out, ctx
        self.names = 0
        self.sems = []
        self.passed = ctx.enter_context(nc.semaphore("waits_passed"))
        sb = self.sb
        self.h1_d = nc.dram_tensor("h1_rows", (NB * P, D), F32, kind="Internal").ap()
        self.h2_d = nc.dram_tensor("h2_rows", (NB * P, D), F32, kind="Internal").ap()
        self.es1_d = nc.dram_tensor("h1_es", (NB * P, HEADS), F32, kind="Internal").ap()
        self.es2_d = nc.dram_tensor("h2_es", (NB * P, 1), F32, kind="Internal").ap()
        self.x1_d = nc.dram_tensor("x1_rows", (NB * P, D + 1), F32, kind="Internal").ap()
        self.xl_d = nc.dram_tensor("x1_and_loop_rows", (NB * P, D), F32, kind="Internal").ap()
        self.dlo_d = nc.dram_tensor("dst_local_by_step", (NCH * P, P), BF16, kind="Internal").ap()
        self.elo_d = nc.dram_tensor("relation_by_step", (NCH * P, P), BF16, kind="Internal").ap()
        self.slo_d = nc.dram_tensor("src_low_by_column", (RW, ROWS), BF16, kind="Internal").ap()
        self.iota_row = sb(ctx, "iota_row", [P, RW])
        self.iota_part = sb(ctx, "iota_part", [P, 1])
        self.tile_no = sb(ctx, "tile_no", [P, TPR])
        self.iota_nb = sb(ctx, "iota_nb", [P, NB], BF16)
        self.ident = sb(ctx, "ident", [P, P])
        self.steptile = sb(ctx, "steptile", [ROWS, TPR, STEPS])
        self.src_step = sb(ctx, "src_step", [P, STEPS], I32)
        self.dst_step = sb(ctx, "dst_step", [P, STEPS])
        self.et_step = sb(ctx, "et_step", [P, STEPS])
        self.first_step = sb(ctx, "first_step", [P, STEPS])
        self.block_of = sb(ctx, "block_of", [1, STEPS], I32)
        self.src_row = sb(ctx, "src_row", [ROWS, RW], I32)
        self.src_hi = sb(ctx, "src_hi", [ROWS, RW], BF16)
        self.first_row = sb(ctx, "first_row", [ROWS, RW], BF16)
        self.last_row = sb(ctx, "last_row", [ROWS, RW], BF16)
        self.srel = sb(ctx, "srel", [P, 2])
        self.node_s = sb(ctx, "node_s", [P, 2 * HEADS, NB])

    def sb(self, ctx, name, shape, dt=F32):
        return ctx.enter_context(self.nc.sbuf_tensor(self.fresh(name), shape, dt))

    def psum(self, ctx, name, shape, dt=F32):
        return ctx.enter_context(self.nc.psum_tensor(self.fresh(name), shape, dt))

    def sem(self, name):
        self.sems.append(self.nc.alloc_semaphore(name=self.fresh(name)))
        return self.sems[-1]

    def phase(self):
        if self.sems:
            self.nc.clear_and_free_semaphores(self.sems)
            self.nc.all_engine_barrier()
        self.sems = []

    def fresh(self, name):
        self.names += 1
        return f"{name}_{self.names}"


def edge_structure(k):
    with ExitStack() as ctx:
        edges = k.sb(ctx, "edges_int", [ROWS, 3, RW], I32)
        prev_i = k.sb(ctx, "prev_i", [ROWS, 1], I32)
        next_i = k.sb(ctx, "next_i", [ROWS, 1], I32)
        unsorted = k.sb(ctx, "unsorted", [1, 1], I32)
        load_edges(k, edges, prev_i, next_i, unsorted)
        order_edges(k, edges, prev_i, next_i, unsorted)
        lay_out_steps(k, edges, prev_i, next_i)


def load_edges(k, edges, prev_i, next_i, unsorted):
    k.phase()
    nc, sb, sem = k.nc, k.sb, k.sem
    with ExitStack() as ctx:
        ones = sb(ctx, "ones_col", [ROWS, 1])
        down = sb(ctx, "down", [ROWS, RW])
        bad = sb(ctx, "rows_bad", [ROWS, 1])
        total = k.psum(ctx, "bad_total", [P, 512])
        s_fill, s_in, s_iota, s_dve, s_bad, s_tot = (sem("filled"), sem("edges_in"), sem("iotas"), sem("dve"),
                                                     sem("rows_bad"), sem("total"))
        with nc.Block() as block:

            @block.gpsimd
            def _(pool):
                nc.gpsimd.memset(edges[:, 0, :], 0).then_inc(s_fill, 1)
                nc.gpsimd.memset(edges[:, 1, :], PAD_DST).then_inc(s_fill, 1)
                nc.gpsimd.memset(edges[:, 2, :], 0).then_inc(s_fill, 1)
                nc.gpsimd.memset(prev_i[:, :], -1).then_inc(s_fill, 1)
                nc.gpsimd.memset(next_i[:, :], PAD_DST + 1).then_inc(s_fill, 1)
                io = dict(allow_small_or_imprecise_dtypes=True)
                nc.gpsimd.iota(k.iota_row[:, :], pattern=[[1, RW]], base=0, channel_multiplier=0, **io).then_inc(s_iota, 1)
                nc.gpsimd.iota(k.iota_part[:, :], pattern=[[0, 1]], base=0, channel_multiplier=1, **io).then_inc(s_iota, 1)
                nc.gpsimd.iota(k.tile_no[:, :], pattern=[[1, TPR]], base=0, channel_multiplier=TPR, **io).then_inc(s_iota, 1)
                nc.gpsimd.iota(k.iota_nb[:, :], pattern=[[1, NB]], base=0, channel_multiplier=0, **io).then_inc(s_iota, 1)

            @block.sync
            def _(sp):
                sp.wait_ge(s_fill, 5)
                for q, src in ((1, k.a["dst"]), (0, k.a["src"]), (2, k.a["edge_type_200"])):
                    sp.dma_start(edges[0:EFULL, q, :], src[0:EFULL * RW].rearrange("(p j) -> p j", j=RW)).then_inc(s_in, 16)
                    sp.dma_start(edges[EFULL:ROWS, q, 0:ELAST],
                                 src[EFULL * RW:E].rearrange("(p j) -> p j", p=1)).then_inc(s_in, 16)
                dst_rows = k.a["dst"][0:EFULL * RW].rearrange("(p j) -> p j", j=RW)
                with nc.allow_non_contiguous_dma(reason="one element of each partition"):
                    sp.dma_start(prev_i[1:ROWS, :], dst_rows[:, RW - 1:RW]).then_inc(s_in, 16)
                    sp.dma_start(next_i[0:EFULL - 1, :], dst_rows[1:EFULL, 0:1]).then_inc(s_in, 16)
                    sp.dma_start(next_i[EFULL - 1:EFULL, :],
                                 k.a["dst"][EFULL * RW:EFULL * RW + 1].rearrange("(p j) -> p j", p=1)).then_inc(s_in, 16)

            @block.vector
            def _(dve):
                link = Chain(dve, s_dve)
                v = nc.vector
                link(v.memset(ones[:, :], 1.0))
                dve.wait_ge(s_iota, 4)
                dve.wait_ge(s_in, 16 * 9)
                link(v.tensor_scalar(k.ident[:, :], k.iota_row[:, 0:P], k.iota_part[:, 0:1], None, ALU.is_equal))
                link(v.tensor_tensor(down[:, 1:RW], edges[:, 1, 0:RW - 1], edges[:, 1, 1:RW], ALU.is_gt))
                link(v.tensor_tensor(down[:, 0:1], prev_i[:, :], edges[:, 1, 0:1], ALU.is_gt))
                v.tensor_reduce(bad[:, :], down[:, :], AX_X, ALU.max).then_inc(s_bad, 1)
                dve.wait_ge(s_tot, 1)
                link(v.tensor_scalar(unsorted[:, :], total[0:1, 0:1], 1.0, None, ALU.min))

            @block.tensor
            def _(pe):
                pe.wait_ge(s_dve, 4)
                pe.wait_ge(s_bad, 1)
                nc.tensor.matmul(total[0:1, 0:1], bad[:, :], ones[:, :], start=True, stop=True).then_inc(s_tot, 1)


def order_edges(k, edges, prev_i, next_i, unsorted):
    k.phase()
    nc, sb, sem = k.nc, k.sb, k.sem
    HI = (PAD_DST + 1) // P
    with ExitStack() as ctx:
        dst_f, part_i, part_f = sb(ctx, "dst_f", [ROWS, RW]), sb(ctx, "dst_part_i", [ROWS, RW], I32), sb(ctx, "dst_part_f", [ROWS, 2, RW])
        ones = sb(ctx, "ones", [P, P])
        below = sb(ctx, "below", [P, P])
        above = sb(ctx, "above", [P, P])
        hot_lo, hot_hi = sb(ctx, "hot_low", [ROWS, P]), sb(ctx, "hot_high", [ROWS, HI])
        hist = sb(ctx, "histogram", [P, HI])
        upto, place = sb(ctx, "upto", [P, HI]), sb(ctx, "first_place", [P, HI])
        idx, put, at_i = (sb(ctx, n, [ROWS, 1], I32) for n in ("table_index", "table_put", "place_index"))
        rec = sb(ctx, "record", [ROWS, 3], I32)
        diag, same, part = (sb(ctx, n, [ROWS, ROWS]) for n in ("diagonal", "same_dst", "same_part"))
        rank, more, free, free2 = (sb(ctx, n, [ROWS, 1]) for n in ("rank", "more", "next_free", "next_free_new"))
        dump = sb(ctx, "dump", [ROWS, 1])
        back = sb(ctx, "sorted_back", [ROWS, RW, 3], I32)
        ps, tps, bps, rps = (k.psum(ctx, n, [P, 512]) for n in ("hist_ps", "total_ps", "below_ps", "row_ps"))
        free_d = nc.dram_tensor("next_free_place", (2 * (PAD_DST + 1), 1), F32, kind="Internal").ap()
        rec_d = nc.dram_tensor("sorted_records", (ROWS * RW, 3), I32, kind="Internal").ap()
        s_dve, s_one, s_hist, s_sum, s_place, s_tab = (sem("dve"), sem("one_hots"), sem("histogram"), sem("histogram_added"),
                                                       sem("places"), sem("table_out"))
        s_tot, s_diag, s_row, s_idx, s_got, s_new, s_put, s_back, s_begin = (
            sem("totals"), sem("diagonal"), sem("row"), sem("index"), sem("table_read"), sem("places_new"),
            sem("scattered"), sem("sorted_in"), sem("begun"))

        def out_of_order(engine):
            return nc.values_load_multi_w_load_instructions(
                unsorted[0:1, 0:1], engines=[engine], min_val=0, max_val=1,
                skip_runtime_bounds_check_because="the lesser of a count and 1")[1][0]

        with nc.Block() as block:

            @block.vector
            def _(dve):
                v = nc.vector
                with dve.If(out_of_order(mybir.EngineType.DVE) > 0):
                    link = Chain(dve, s_begin)
                    link(v.tensor_copy(dst_f[:, :], edges[:, 1, :]))
                    for m, (n, op) in enumerate(((P - 1, ALU.bitwise_and), (7, ALU.logical_shift_right))):
                        link(v.tensor_scalar(part_i[:, :], edges[:, 1, :], n, None, op))
                        link(v.tensor_copy(part_f[:, m, :], part_i[:, :]))
                    link(v.memset(ones[:, :], 1.0))
                    link(v.memset(hist[:, :], 0.0))
                    link(v.tensor_scalar(below[:, :], k.iota_row[:, 0:P], k.iota_part[:, 0:1], None, ALU.is_gt))
                    link(v.tensor_scalar(above[:, :], k.iota_row[:, 0:P], k.iota_part[:, 0:1], None, ALU.is_lt))

                    def count(j):
                        after(dve, s_hist, j)
                        v.tensor_scalar(hot_lo[:, :], k.iota_row[0:ROWS, 0:P], col(part_f[:, 0, :], j), None,
                                        ALU.is_equal).then_inc(s_one, 1)
                        v.tensor_scalar(hot_hi[:, :], k.iota_row[0:ROWS, 0:HI], col(part_f[:, 1, :], j), None,
                                        ALU.is_equal).then_inc(s_one, 1)
                        dve.wait_ge(s_hist, j + 1)
                        v.tensor_tensor(hist[:, :], hist[:, :], ps[:, 0:HI], ALU.add).then_inc(s_sum, 1)
                        dve.wait_ge(s_sum, j + 1)
                    turns(dve, RW, count)
                    dve.wait_ge(s_tot, 1)
                    link(v.tensor_tensor_scan(upto[:, :], ones[:, 0:HI], tps[:, 0:HI], 0.0, ALU.mult, ALU.add))
                    link(v.tensor_tensor(place[:, :], upto[:, :], tps[:, 0:HI], ALU.subtract))
                    v.tensor_tensor(place[:, :], place[:, :], bps[:, 0:HI], ALU.add).then_inc(s_place, 1)

                    def place_batch(j):
                        c = col(dst_f, j)
                        after(dve, s_put, 32 * j)
                        link2 = Chain(dve, s_dve, 11 * j)
                        link2(v.tensor_copy(rec[:, :], col3(edges, j)))
                        v.tensor_copy(idx[:, :], rec[:, 1:2]).then_inc(s_idx, 1)
                        v.tensor_scalar(diag[:, :], k.ident[0:ROWS, 0:ROWS], c, None, ALU.mult).then_inc(s_diag, 1)
                        dve.wait_ge(s_row, j + 1)
                        link2(v.tensor_scalar(same[:, :], rps[0:ROWS, 0:ROWS], c, None, ALU.is_equal))
                        link2(v.tensor_tensor(part[:, :], same[:, :], above[0:ROWS, 0:ROWS], ALU.mult))
                        link2(v.tensor_reduce(rank[:, :], part[:, :], AX_X, ALU.add))
                        link2(v.tensor_tensor(part[:, :], same[:, :], below[0:ROWS, 0:ROWS], ALU.mult))
                        link2(v.tensor_reduce(more[:, :], part[:, :], AX_X, ALU.max))
                        link2(v.tensor_scalar(dump[:, :], k.iota_part[0:ROWS, :], PAD_DST + 1.0, c, ALU.add, ALU.subtract))
                        link2(v.tensor_tensor(dump[:, :], dump[:, :], more[:, :], ALU.mult))
                        link2(v.tensor_tensor(put[:, :], dump[:, :], c, ALU.add))
                        dve.wait_ge(s_got, 16 * (j + 1))
                        link2(v.tensor_tensor(free2[:, :], free[:, :], rank[:, :], ALU.add))
                        link2(v.tensor_copy(at_i[:, :], free2[:, :]))
                        v.tensor_scalar(free2[:, :], free2[:, :], 1.0, None, ALU.add).then_inc(s_new, 1)
                    turns(dve, RW, place_batch)
                    dve.wait_ge(s_back, 48)
                    link(v.tensor_copy(edges[:, :, :], back[:, :, :].rearrange("p j q -> p q j")))

            @block.tensor
            def _(pe):
                with pe.If(out_of_order(mybir.EngineType.PE) > 0):
                    pe.wait_ge(s_begin, 9)

                    def count(j):
                        pe.wait_ge(s_one, 2 * j + 2)
                        after(pe, s_sum, j)
                        nc.tensor.matmul(ps[:, 0:HI], hot_lo[:, :], hot_hi[:, :], start=True, stop=True).then_inc(s_hist, 1)
                    turns(pe, RW, count)
                    pe.wait_ge(s_sum, RW)
                    nc.tensor.matmul(tps[:, 0:HI], ones[:, :], hist[:, :], start=True, stop=True)
                    nc.tensor.matmul(bps[:, 0:HI], below[:, :], hist[:, :], start=True, stop=True).then_inc(s_tot, 1)

                    def row(j):
                        pe.wait_ge(s_diag, j + 1)
                        nc.tensor.matmul(rps[0:ROWS, 0:ROWS], ones[0:ROWS, 0:ROWS], diag[:, :], start=True,
                                         stop=True).then_inc(s_row, 1)
                    turns(pe, RW, row)

            @block.gpsimd
            def _(pool):
                with pool.If(out_of_order(mybir.EngineType.Pool) > 0):
                    pool.wait_ge(s_place, 1)
                    with nc.allow_non_contiguous_dma(reason="a table in another order"):
                        for half in range(2):
                            rows = free_d[half * (PAD_DST + 1):(half + 1) * (PAD_DST + 1), :]
                            pool.dma_start(rows.rearrange("(h p) o -> p (h o)", p=P), place[:, :]).then_inc(s_tab, 16)
                    pool.wait_ge(s_tab, 32)

                    def scatter(j):
                        pool.wait_ge(s_idx, j + 1)
                        after(pool, s_put, 32 * j)
                        settled(pool, k.passed)
                        pool.indirect_dma_start(out=free[:, :], out_offset=None, in_=free_d,
                                                in_offset=bass.IndirectOffsetOnAxis(ap=idx[:, 0:1], axis=0)).then_inc(s_got, 16)
                        pool.wait_ge(s_new, j + 1)
                        settled(pool, k.passed)
                        pool.indirect_dma_start(out=free_d, out_offset=bass.IndirectOffsetOnAxis(ap=put[:, 0:1], axis=0),
                                                in_=free2[:, :], in_offset=None).then_inc(s_put, 16)
                        pool.indirect_dma_start(out=rec_d, out_offset=bass.IndirectOffsetOnAxis(ap=at_i[:, 0:1], axis=0),
                                                in_=rec[:, :], in_offset=None).then_inc(s_put, 16)
                    turns(pool, RW, scatter)
                    pool.wait_ge(s_put, 32 * RW)
                    rows = rec_d.rearrange("(p j) q -> p j q", p=ROWS)
                    pool.dma_start(back[:, :, :], rows).then_inc(s_back, 16)
                    with nc.allow_non_contiguous_dma(reason="one element of each partition"):
                        pool.dma_start(prev_i[1:ROWS, :], rows[0:ROWS - 1, RW - 1, 1:2]).then_inc(s_back, 16)
                        pool.dma_start(next_i[0:ROWS - 1, :], rows[1:ROWS, 0, 1:2]).then_inc(s_back, 16)
                    pool.wait_ge(s_back, 48)


def lay_out_steps(k, edges, prev_i, next_i):
    k.phase()
    nc, sb, sem = k.nc, k.sb, k.sem
    with ExitStack() as ctx:
        ints = {n: edges[:, q, :] for q, n in enumerate(("src", "dst", "et"))}
        flt = {n: sb(ctx, f"{n}_flt", [ROWS, RW]) for n in ("src", "dst", "et")}
        low_i = sb(ctx, "low_i", [ROWS, RW], I32)
        low_f = sb(ctx, "low_f", [ROWS, RW])
        first_f = sb(ctx, "first_f", [ROWS, RW])
        prev_f = sb(ctx, "prev_f", [ROWS, 1])
        next_f = sb(ctx, "next_f", [ROWS, 1])
        hi_i = sb(ctx, "hi_i", [ROWS, TPR], I32)
        first_of_tile = sb(ctx, "first_of_tile", [ROWS, TPR])
        begun = sb(ctx, "begun", [ROWS, TPR, STEPS], BF16)
        ones = sb(ctx, "ones_bf", [ROWS, P], BF16)
        tile_of = sb(ctx, "tile_of", [P, STEPS])
        block_f = sb(ctx, "block_f", [P, STEPS])
        packed = sb(ctx, "packed", [ROWS, RW])
        packed_i, part_i = sb(ctx, "packed_step", [P, STEPS], I32), sb(ctx, "packed_part", [P, STEPS], I32)
        low_t = sb(ctx, "low_t", [P, TPR, ROWS], BF16)
        dst_t = sb(ctx, "dst_t", [P, NCH, P], BF16)
        et_t = sb(ctx, "et_t", [P, NCH, P], BF16)
        pair = [k.psum(ctx, f"pair{i}", [P, 2, 512]) for i in range(3)]
        tps = [k.psum(ctx, f"tps{i}", [P, P]) for i in range(2)]
        s_fill = sem("filled")
        s_dve, s_ge, s_one = sem("dve"), sem("begun"), sem("ones")
        s_cnt, s_sel, s_exp, s_evac = sem("counted"), sem("steptile"), sem("expanded"), sem("evacuated")
        s_dst = sem("dst_local")
        s_dstf, s_low, s_tp, s_tc, s_lowd = sem("dst_step"), sem("low"), sem("turned"), sem("turned_out"), sem("low_out")
        names = ("src", "dst", "et")
        with nc.Block() as block:

            @block.gpsimd
            def _(pool):
                nc.gpsimd.memset(dst_t[:, :, :], 0.0).then_inc(s_fill, 1)
                nc.gpsimd.memset(et_t[:, :, :], 0.0).then_inc(s_fill, 1)

            @block.sync
            def _(sp):
                sp.wait_ge(s_tc, TPR)
                sp.dma_start(k.slo_d.rearrange("(g p) r -> p g r", p=P), low_t[:, :, :]).then_inc(s_lowd, 16)
                sp.wait_ge(s_tc, TPR + NCH)
                sp.dma_start(k.dlo_d.rearrange("(c p) e -> p c e", p=P), dst_t[:, :, :]).then_inc(s_lowd, 16)
                sp.wait_ge(s_tc, TPR + 2 * NCH)
                sp.dma_start(k.elo_d.rearrange("(c p) e -> p c e", p=P), et_t[:, :, :]).then_inc(s_lowd, 16)
                sp.wait_ge(s_lowd, 48)

            @block.vector
            def _(dve):
                link = Chain(dve, s_dve)
                nc.vector.memset(ones[:, :], 1.0).then_inc(s_one, 1)
                link(nc.vector.tensor_scalar(hi_i[:, :], edges[:, 1, 0:RW:P], 7, None, ALU.logical_shift_right))
                link(nc.vector.tensor_tensor(first_of_tile[:, :], hi_i[:, :], k.tile_no[0:ROWS, :], ALU.add))
                for g in range(TPR):
                    nc.vector.tensor_scalar(begun[:, g, :], k.iota_row[0:ROWS, 0:STEPS], first_of_tile[:, g:g + 1],
                                            None, ALU.is_ge).then_inc(s_ge, 1)
                link(nc.vector.tensor_scalar(low_i[:, :], ints["src"], P - 1, None, ALU.bitwise_and))
                nc.vector.tensor_copy(low_f[:, :], low_i[:, :]).then_inc(s_low, 1)
                dve.wait_ge(s_low, 1)
                link(nc.vector.tensor_scalar(low_i[:, :], ints["src"], 7, None, ALU.logical_shift_right))
                link(nc.vector.tensor_copy(k.src_hi[:, :], low_i[:, :]))
                link(nc.vector.tensor_copy(k.src_row[:, :], ints["src"]))
                for n in names:
                    nc.vector.tensor_copy(flt[n][:, :], ints[n]).then_inc(s_dstf, 1)
                link(nc.vector.tensor_copy(prev_f[:, :], prev_i[:, :]))
                link(nc.vector.tensor_copy(next_f[:, :], next_i[:, :]))
                dve.wait_ge(s_dstf, 3)
                df = flt["dst"]
                link(nc.vector.tensor_tensor(first_f[:, 1:RW], df[:, 1:RW], df[:, 0:RW - 1], ALU.not_equal))
                nc.vector.tensor_tensor(first_f[:, 0:1], df[:, 0:1], prev_f[:, :], ALU.not_equal).then_inc(s_dstf, 1)
                dve.wait_ge(s_dstf, 4)
                link(nc.vector.scalar_tensor_tensor(out=packed[:, :], in0=flt["et"][:, :], scalar=float(SRC_END),
                                                    in1=flt["src"][:, :], op0=ALU.mult, op1=ALU.add))
                nc.vector.scalar_tensor_tensor(out=packed[:, :], in0=first_f[:, :], scalar=float(SRC_END * ET_END),
                                               in1=packed[:, :], op0=ALU.mult, op1=ALU.add).then_inc(s_dstf, 1)
                link(nc.vector.tensor_copy(k.first_row[:, :], first_f[:, :]))
                link(nc.vector.tensor_copy(k.last_row[:, 0:RW - 1], first_f[:, 1:RW]))
                link(nc.vector.tensor_tensor(k.last_row[:, RW - 1:RW], df[:, RW - 1:RW], next_f[:, :], ALU.not_equal))
                dve.wait_ge(s_cnt, 1)
                link(nc.vector.tensor_scalar(tile_of[:, :].rearrange("p (a s) -> p a s", a=2), pair[0][:, :, 0:HALF],
                                             -1.0, 0.0, ALU.add, ALU.max))
                link(nc.vector.tensor_tensor(block_f[:, :], k.iota_row[:, 0:STEPS], tile_of[:, :], ALU.subtract))
                link(nc.vector.tensor_scalar(k.block_of[:, :], block_f[0:1, :], NB - 1.0, None, ALU.min))
                for g in range(TPR):
                    nc.vector.tensor_scalar(k.steptile[:, g, :], tile_of[0:ROWS, :], k.tile_no[0:ROWS, g:g + 1], None,
                                            ALU.is_equal).then_inc(s_sel, 1)
                dve.wait_ge(s_exp, 1)
                nc.vector.scalar_tensor_tensor(
                    out=k.dst_step[:, :].rearrange("p (a s) -> p a s", a=2),
                    in0=block_f[:, :].rearrange("p (a s) -> p a s", a=2), scalar=-float(P),
                    in1=pair[1][:, :, 0:HALF], op0=ALU.mult, op1=ALU.add).then_inc(s_dst, 1)
                v = nc.vector
                dve.wait_ge(s_exp, 2)
                link(v.tensor_copy(packed_i[:, :].rearrange("p (a s) -> p a s", a=2), pair[2][:, :, 0:HALF]))
                link(v.tensor_scalar(part_i[:, :], packed_i[:, :], 13, ET_END - 1, ALU.logical_shift_right, ALU.bitwise_and))
                v.tensor_copy(k.et_step[:, :], part_i[:, :]).then_inc(s_evac, 1)
                dve.wait_ge(s_evac, 1)
                link(v.tensor_scalar(k.src_step[:, :], packed_i[:, :], SRC_END - 1, None, ALU.bitwise_and))
                link(v.tensor_scalar(part_i[:, :], packed_i[:, :], 21, None, ALU.logical_shift_right))
                link(v.tensor_copy(k.first_step[:, :], part_i[:, :]))

            @block.tensor
            def _(pe):
                pe.wait_ge(s_one, 1)
                for g in range(TPR):
                    pe.wait_ge(s_ge, g + 1)
                    for h in range(2):
                        last = nc.tensor.matmul(pair[0][:, h, 0:HALF], ones[:, :],
                                                begun[:, g, h * HALF:(h + 1) * HALF],
                                                start=(g == 0), stop=(g == TPR - 1))
                last.then_inc(s_cnt, 1)
                pe.wait_ge(s_low, 1)
                for g in range(TPR):
                    if g >= 2:
                        pe.wait_ge(s_tc, g - 1)
                    nc.tensor.transpose(tps[g % 2][:, 0:ROWS], low_f[:, g * P:(g + 1) * P],
                                        k.ident[0:ROWS, 0:ROWS]).then_inc(s_tp, 1)
                pe.wait_ge(s_dstf, 5)
                pe.wait_ge(s_sel, TPR)
                for q, x in enumerate((flt["dst"], packed)):
                    for g in range(TPR):
                        for h in range(2):
                            last = nc.tensor.matmul(pair[q + 1][:, h, 0:HALF], x[:, g * P:(g + 1) * P],
                                                    k.steptile[:, g, h * HALF:(h + 1) * HALF],
                                                    start=(g == 0), stop=(g == TPR - 1))
                    last.then_inc(s_exp, 1)
                pe.wait_ge(s_dst, 1)
                pe.wait_ge(s_evac, 1)
                for m, x in enumerate((k.dst_step, k.et_step)):
                    for c in range(NCH):
                        n, at = min(P, STEPS - c * P), TPR + m * NCH + c
                        pe.wait_ge(s_tc, at - 1)
                        nc.tensor.transpose(tps[at % 2][0:n, :], x[:, c * P:c * P + n],
                                            k.ident[:, :]).then_inc(s_tp, 1)

            @block.scalar
            def _(act):
                for g in range(TPR):
                    act.wait_ge(s_tp, g + 1)
                    nc.scalar.activation(low_t[:, g, :], tps[g % 2][:, 0:ROWS], ACT.Copy).then_inc(s_tc, 1)
                act.wait_ge(s_fill, 2)
                for m, y in enumerate((dst_t, et_t)):
                    for c in range(NCH):
                        n, at = min(P, STEPS - c * P), TPR + m * NCH + c
                        act.wait_ge(s_tp, at + 1)
                        nc.scalar.activation(y[0:n, c, :], tps[at % 2][0:n, :], ACT.Copy).then_inc(s_tc, 1)



def ahead(i, u, lead):
    if u + lead < NODE_U:
        return i, u + lead
    return None if isinstance(i, int) and i == NODE_TURNS - 1 else (i + 1, u + lead - NODE_U)


def node_turns(eng, leads, work):
    for lead, stage in leads:
        for u in range(lead):
            stage(0, u)

    def body(i):
        for u in range(NODE_U):
            for lead, stage in leads:
                place = ahead(i, u, lead)
                if place is not None:
                    stage(*place)
            work(i, u)
    turns(eng, NODE_TURNS, body)


def pe_project(k, pe, xin, slots, s_x, tps, s_tp, s_xt, xt, w, ops, s_mm, s_out, chunks):
    nc = k.nc

    def turn_block(i, u):
        n = i * NODE_U + u
        s_x(pe, i, u)
        after(pe, s_xt, n - 1 if u else n)
        for c, (lo, wd) in enumerate(chunks):
            last = nc.tensor.transpose(tps[u % 2][0:wd, c, :], xin[:, u % slots, lo:lo + wd], k.ident[:, :])
        last.then_inc(s_tp, 1)

    def multiply(i, u):
        n = i * NODE_U + u
        pe.wait_ge(s_xt, n + 1)
        after(pe, s_out, n - 1 if u else n)
        for group in w:
            o, cs = group
            for m, (c, wt) in enumerate(cs):
                wd = chunks[c][1]
                last = nc.tensor.matmul(ops[u % 2][:, o:o + wt.shape[-1]], xt[u % 2][0:wd, c, :], wt,
                                        start=(m == 0), stop=(m == len(cs) - 1))
        last.then_inc(s_mm, 1)

    node_turns(pe, [(1, turn_block)], multiply)


def rows_of(dram, n):
    return dram[bass.ds(n * P, P), :] if not isinstance(n, int) else dram[n * P:(n + 1) * P, :]


def store_turn(k, eng, dram, tile, i, s):
    n = i * NODE_U
    src = tile[:, n:n + NODE_U, :] if isinstance(n, int) else tile[:, bass.ds(n, NODE_U), :]
    dst = dram[n * P:(n + NODE_U) * P, :] if isinstance(n, int) else dram[bass.ds(n * P, NODE_U * P), :]
    with k.nc.allow_non_contiguous_dma(reason="a few numbers of each node"):
        eng.dma_start(dst.rearrange("(b p) d -> p b d", p=P), src).then_inc(s, 16)


def first_projection(k):
    k.phase()
    nc, sb, sem = k.nc, k.sb, k.sem
    W = D + 2 * HEADS
    with ExitStack() as ctx:
        w = sb(ctx, "w1x", [P, 2, W])
        av = sb(ctx, "a_rows", [P, 2, D])
        wa = sb(ctx, "w1_times_a", [P, 2, D])
        xin = sb(ctx, "xin", [P, NODE_U, D])
        hout = sb(ctx, "hout", [P, NODE_U, D])
        eout = sb(ctx, "eout", [P, NB, HEADS])
        xt = [sb(ctx, f"xt{i}", [P, 2, P]) for i in range(2)]
        tps = [k.psum(ctx, f"tps{i}", [P, 2, P]) for i in range(2)]
        ops = [k.psum(ctx, f"ops{i}", [P, 512]) for i in range(2)]
        s_w, s_wx, s_dve, s_last = sem("weights_in"), sem("weights_ready"), sem("dve"), sem("last_block_zero")
        s_es = sem("es_stored")
        s_x = [sem(f"x_in{u}") for u in range(NODE_U)]
        s_st = [sem(f"h_stored{u}") for u in range(NODE_U)]
        s_tp, s_xt, s_mm, s_out, s_ev = sem("turned"), sem("turned_copied"), sem("product"), sem("product_read"), sem("h_ready")
        with nc.Block() as block:

            @block.sync
            def _(sp):
                sp.dma_start(w[:, :, 0:D], k.a["L0_gnn_W1"].rearrange("(c p) n -> p c n", p=P)).then_inc(s_w, 16)
                for m, n in enumerate(("L0_gnn_a1_src", "L0_gnn_a1_dst")):
                    sp.dma_start(av[:, m, :], k.a[n].rearrange("h c -> (h c)").partition_broadcast(P)).then_inc(s_w, 16)

                def body(i):
                    for u in range(NODE_U):
                        n = i * NODE_U + u
                        after(sp, s_tp, n - NODE_U + 1)
                        if isinstance(n, int) and n == NB - 1:
                            sp.wait_ge(s_last, 1)
                            sp.dma_start(xin[0:NLAST, u, :], k.a["x"][n * P:N, :]).then_inc(s_x[u], 16)
                        else:
                            sp.dma_start(xin[:, u, :], rows_of(k.a["x"], n)).then_inc(s_x[u], 16)
                turns(sp, NODE_TURNS, body)

            @block.vector
            def _(dve):
                link = Chain(dve, s_dve)
                dve.wait_ge(s_w, 48)
                for m in range(2):
                    link(nc.vector.tensor_tensor(wa[:, :, :], w[:, :, 0:D],
                                                 av[:, m:m + 1, :].to_broadcast([P, 2, D]), ALU.mult))
                    nc.vector.tensor_reduce(w[:, :, D + m * HEADS:D + (m + 1) * HEADS],
                                            wa[:, :, :].rearrange("p c (h e) -> p c h e", h=HEADS), AX_X,
                                            ALU.add).then_inc(s_wx, 1)
                    dve.wait_ge(s_wx, m + 1)

                def copy(o, i):
                    return nc.vector.tensor_copy(o[:, :, :], i[:, :, :])

                def body(i):
                    for u in range(NODE_U):
                        n = i * NODE_U + u
                        if isinstance(n, int) and n == NB - NODE_U:
                            dve.wait_ge(s_tp, NB - NODE_U)
                            nc.vector.memset(xin[:, NODE_U - 1, :], 0.0).then_inc(s_last, 1)
                        dve.wait_ge(s_tp, n + 1)
                        after(dve, s_mm, n - 1 if u else n)
                        copy(xt[u % 2], tps[u % 2]).then_inc(s_xt, 1)
                turns(dve, NODE_TURNS, body)

            @block.tensor
            def _(pe):
                pe.wait_ge(s_wx, 2)
                pe_project(k, pe, xin, NODE_U, lambda e, i, u: e.wait_ge(s_x[u], 16 * (i + 1)), tps, s_tp, s_xt, xt,
                           [(0, [(c, w[:, c, :]) for c in range(2)])], ops, s_mm, s_out, [(0, P), (P, P)])

            @block.scalar
            def _(act):
                def body(i):
                    for u in range(NODE_U):
                        n = i * NODE_U + u
                        act.wait_ge(s_mm, n + 1)
                        after(act, s_st[u], 16 * i)
                        nc.scalar.activation(hout[:, u, :], ops[u % 2][:, 0:D], ACT.Copy).then_inc(s_ev, 1)
                        nc.scalar.activation(at(eout, n), ops[u % 2][:, D:D + HEADS], ACT.Copy).then_inc(s_ev, 1)
                        nc.scalar.activation(k.node_s[:, :, n:n + 1] if isinstance(n, int) else k.node_s[:, :, bass.ds(n, 1)],
                                             ops[u % 2][:, D:W].rearrange("p (c o) -> p c o", o=1), ACT.Copy).then_inc(s_out, 1)
                        act.wait_ge(s_ev, 2 * n + 2)
                        act.dma_start(rows_of(k.h1_d, n), hout[:, u, :]).then_inc(s_st[u], 16)
                    store_turn(k, act, k.es1_d, eout, i, s_es)
                turns(act, NODE_TURNS, body)
                act.wait_ge(s_es, 16 * NODE_TURNS)
                for u in range(NODE_U):
                    act.wait_ge(s_st[u], 16 * NODE_TURNS)



def split_table(k, link, node, rest, tab):
    nc = k.nc
    link(nc.vector.tensor_copy(tab[0], node))
    link(nc.vector.tensor_tensor(rest, node, tab[0], ALU.subtract))
    link(nc.vector.tensor_copy(tab[1], rest))
    link(nc.vector.tensor_tensor(rest, rest, tab[1], ALU.subtract))
    link(nc.vector.tensor_copy(tab[2], rest))


def lookups(k, C, es, es_d, out_row, ed, out_step):
    k.phase()
    nc, sb, sem = k.nc, k.sb, k.sem
    DQ = 2
    NT = STEPS // U // DQ
    SQ, LC = (4, 5) if C > 1 else (4, 7)
    JP = NT * SQ * LC
    GU = 8
    GH, GT = GU // 2, (RW - JP) // GU
    assert GT * GU == RW - JP
    with ExitStack() as ctx:
        tab = sb(ctx, "src_table", [P, 3, C, NB], BF16)
        dtab = sb(ctx, "dst_table", [P, NB, 3, C], BF16)
        rest = sb(ctx, "table_rest", [P, C, NB])
        low = [sb(ctx, f"low{q}", [P, LC * ROWS], BF16) for q in range(SQ)]
        hot = [sb(ctx, f"hot{q}", [P, LC * ROWS], BF16) for q in range(SQ)]
        mask = [sb(ctx, f"mask{h}", [ROWS, LC, NB], BF16) for h in range(2)]
        prod = [sb(ctx, f"prod{h}", [ROWS, LC, C, NB]) for h in range(2)]
        dlow = [sb(ctx, f"dlow{q}", [P, U * P], BF16) for q in range(DQ)]
        dhot = [sb(ctx, f"dhot{q}", [P, U * P], BF16) for q in range(DQ)]
        idx = sb(ctx, "idx", [ROWS, GU], I32)
        got = sb(ctx, "gathered", [ROWS, GU, C])
        ps = [k.psum(ctx, f"cand{h}", [P, LC, 256 if C > 1 else 64]) for h in range(2)]
        dps = [k.psum(ctx, f"vals{q}", [P, 512]) for q in range(DQ)]
        s_low = [sem(f"low_in{q}") for q in range(SQ)]
        s_dlow = [sem(f"dst_low_in{q}") for q in range(DQ)]
        s_row = [sem(f"gathered{u}") for u in range(GU)]
        s_dve, s_tab, s_hot, s_mask, s_mm, s_prod, s_red = (sem("dve"), sem("table"), sem("hot"), sem("mask"),
                                                            sem("candidates"), sem("picked"), sem("summed"))
        s_dhot, s_dmm, s_dred, s_idx, s_take = (sem("dst_hot"), sem("dst_values"), sem("dst_summed"), sem("indices"),
                                                sem("gathered_taken"))
        with nc.Block() as block:

            @block.gpsimd
            def _(pool):
                def body(i):
                    for u in range(GU):
                        if u % GH == 0:
                            pool.wait_ge(s_idx, 2 * i + u // GH + 1)
                            after(pool, s_take, 2 * i + u // GH - 1)
                            settled(pool, k.passed)
                        pool.indirect_dma_start(
                            out=got[:, u, :], out_offset=None, in_=es_d,
                            in_offset=bass.IndirectOffsetOnAxis(ap=idx[:, u:u + 1], axis=0)).then_inc(s_row[u], 16)
                turns(pool, GT, body)

            @block.scalar
            def _(act):
                def hand(i, h):
                    j = JP + i * GU + h * GH
                    src = k.src_row[:, j:j + GH] if isinstance(j, int) else k.src_row[:, bass.ds(j, GH)]
                    settled(act, k.passed)
                    nc.scalar.activation(idx[:, h * GH:(h + 1) * GH], src, ACT.Copy).then_inc(s_idx, 1)
                hand(0, 0)
                hand(0, 1)

                def body(i):
                    for h in range(2):
                        for u in range(h * GH, (h + 1) * GH):
                            act.wait_ge(s_row[u], 16 * (i + 1))
                        j = JP + i * GU + h * GH
                        o = out_row[:, :, j:j + GH] if isinstance(j, int) else out_row[:, :, bass.ds(j, GH)]
                        settled(act, k.passed)
                        nc.scalar.activation(o.rearrange("r c j -> r j c"), got[:, h * GH:(h + 1) * GH, :],
                                             ACT.Copy).then_inc(s_take, 1)
                        if not (isinstance(i, int) and i == GT - 1):
                            hand(i + 1, h)
                turns(act, GT, body)

            @block.sync
            def _(sp):
                def body(i):
                    for q in range(SQ):
                        n = SQ * i + q
                        after(sp, s_hot, n - SQ + 1)
                        src = k.slo_d[bass.ds(n * LC, LC), :] if not isinstance(n, int) else k.slo_d[n * LC:(n + 1) * LC, :]
                        sp.dma_start(low[q][:, :], src.rearrange("j r -> (j r)").partition_broadcast(P)).then_inc(s_low[q], 16)
                    for q in range(DQ):
                        n = DQ * i + q
                        after(sp, s_dhot, n - DQ + 1)
                        src = k.dlo_d[bass.ds(n * U, U), :] if not isinstance(n, int) else k.dlo_d[n * U:(n + 1) * U, :]
                        sp.dma_start(dlow[q][:, :], src.rearrange("s e -> (s e)").partition_broadcast(P)).then_inc(s_dlow[q], 16)
                turns(sp, NT, body)

            @block.vector
            def _(dve):
                v = nc.vector
                link = Chain(dve, s_dve)
                split_table(k, link, es, rest[:, :, :], [tab[:, m, :, :] for m in range(3)])
                split_table(k, link, ed, rest[:, :, :], [dtab[:, :, m, :].rearrange("p b c -> p c b") for m in range(3)])
                v.memset(rest[:, 0, 0:1], 0.0).then_inc(s_tab, 1)

                def one_hot(i, q):
                    n = SQ * i + q
                    dve.wait_ge(s_low[q], 16 * (i + 1))
                    after(dve, s_mm, n - SQ + 1)
                    v.tensor_scalar(hot[q][:, :], low[q][:, :], k.iota_part[:, 0:1], None, ALU.is_equal).then_inc(s_hot, 1)
                    after(dve, s_prod, n - 1)
                    hi = k.src_hi[:, n * LC:(n + 1) * LC] if isinstance(n, int) else k.src_hi[:, bass.ds(n * LC, LC)]
                    v.tensor_tensor(mask[q % 2][:, :, :], hi.unsqueeze(2).to_broadcast([ROWS, LC, NB]),
                                    k.iota_nb[0:ROWS, :].unsqueeze(1).to_broadcast([ROWS, LC, NB]),
                                    ALU.is_equal).then_inc(s_mask, 1)

                def pick(n, h):
                    j = n * LC
                    dve.wait_ge(s_mm, n + 1)
                    dve.wait_ge(s_mask, n + 1)
                    after(dve, s_red, n - 1)
                    v.tensor_tensor(
                        prod[h][:, :, :, :], ps[h][0:ROWS, :, 0:C * NB].rearrange("r j (c b) -> r j c b", c=C),
                        mask[h][:, :, :].unsqueeze(2).to_broadcast([ROWS, LC, C, NB]), ALU.mult).then_inc(s_prod, 1)
                    dve.wait_ge(s_prod, n + 1)
                    o = out_row[:, :, j:j + LC] if isinstance(j, int) else out_row[:, :, bass.ds(j, LC)]
                    v.tensor_reduce(o.rearrange("r c j -> r j c"), prod[h][:, :, :, :], AX_X, ALU.add).then_inc(s_red, 1)

                def dst_hot(i, q):
                    n = DQ * i + q
                    dve.wait_ge(s_dlow[q], 16 * (i + 1))
                    after(dve, s_dmm, n - DQ + 1)
                    v.tensor_scalar(dhot[q][:, :], dlow[q][:, :], k.iota_part[:, 0:1], None, ALU.is_equal).then_inc(s_dhot, 1)

                def total(n, q):
                    dve.wait_ge(s_dmm, n + 1)
                    o = out_step[:, n * U:(n + 1) * U, :] if isinstance(n, int) else out_step[:, bass.ds(n * U, U), :]
                    vals = dps[q][:, 0:U * 3 * C].rearrange("p (s m c) -> p s c m", m=3, c=C)
                    v.tensor_reduce(o, vals, AX_X, ALU.add).then_inc(s_dred, 1)

                def body(i):
                    first = isinstance(i, int) and i == 0
                    for q in range(SQ):
                        one_hot(i, q)
                        if q % 2 == 0:
                            dst_hot(i, q // 2)
                        if not (first and q == 0):
                            pick(SQ * i + q - 1, (q - 1) % 2)
                        if q % 2 == 0 and not (first and q == 0):
                            total(DQ * i + q // 2 - 1, (q // 2 - 1) % DQ)
                turns(dve, NT, body)
                pick(SQ * NT - 1, 1)
                total(DQ * NT - 1, DQ - 1)

            @block.tensor
            def _(pe):
                pe.wait_ge(s_tab, 1)

                def source(n, q):
                    pe.wait_ge(s_hot, n + 1)
                    after(pe, s_prod, n - 1)
                    for j in range(LC):
                        for m in range(3):
                            last = nc.tensor.matmul(ps[q % 2][0:ROWS, j, 0:C * NB], hot[q][:, j * ROWS:(j + 1) * ROWS],
                                                    tab[:, m, :, :].rearrange("p c b -> p (c b)"),
                                                    start=(m == 0), stop=(m == 2))
                    last.then_inc(s_mm, 1)

                def destination(n, q, blocks):
                    pe.wait_ge(s_dhot, n + 1)
                    after(pe, s_dred, n - DQ + 1)
                    for u in range(U):
                        last = nc.tensor.matmul(dps[q][:, u * 3 * C:(u + 1) * 3 * C], dhot[q][:, u * P:(u + 1) * P],
                                                dtab[:, bass.ds(blocks[u], 1), :, :].rearrange("p b m c -> p (b m c)"),
                                                start=True, stop=True)
                    last.then_inc(s_dmm, 1)

                def body(i):
                    blocks = blocks_of(k, mybir.EngineType.PE, i, DQ * U)
                    for q in range(DQ):
                        source(SQ * i + 2 * q, 2 * q)
                        destination(DQ * i + q, q, blocks[q * U:(q + 1) * U])
                        source(SQ * i + 2 * q + 1, 2 * q + 1)
                turns(pe, NT, body)


def lookup_dst(k, node, out_step, rel):
    k.phase()
    nc, sb, sem = k.nc, k.sb, k.sem
    NQ = 4
    NL = STEPS // U // NQ
    KINDS, LOWS = 3, 2
    with ExitStack() as ctx:
        tab = sb(ctx, "dst_table", [P, NB, 3], BF16)
        rest = sb(ctx, "dst_rest", [P, NB])
        rtab = sb(ctx, "rel_table", [P, 2, 3], BF16)
        part2 = sb(ctx, "iota_part2", [P, 1])
        low = [sb(ctx, f"dlow{q}", [P, LOWS, U * P], BF16) for q in range(NQ)]
        hot = [sb(ctx, f"dhot{h}", [P, KINDS, U * P], BF16) for h in range(2)]
        ps = [k.psum(ctx, f"vals{h}", [P, U, 16]) for h in range(2)]
        s_low = [sem(f"dlow_in{q}") for q in range(NQ)]
        s_dve, s_tab, s_hot, s_mm, s_red = sem("dve"), sem("table"), sem("hot"), sem("values"), sem("summed")
        with nc.Block() as block:

            @block.sync
            def _(sp):
                def body(i):
                    for q in range(NQ):
                        n = NQ * i + q
                        after(sp, s_hot, (n - NQ + 1) * KINDS)
                        for m, d in enumerate((k.dlo_d, k.elo_d)):
                            src = d[n * U:(n + 1) * U, :] if isinstance(n, int) else d[bass.ds(n * U, U), :]
                            sp.dma_start(low[q][:, m, :],
                                         src.rearrange("s e -> (s e)").partition_broadcast(P)).then_inc(s_low[q], 16)
                turns(sp, NL, body)

            @block.vector
            def _(dve):
                link = Chain(dve, s_dve)
                split_table(k, link, node, rest[:, :], [tab[:, :, m] for m in range(3)])
                link(nc.vector.tensor_scalar(part2[:, :], k.iota_part[:, :], float(P), None, ALU.add))
                split_table(k, link, rel, rest[:, 0:2], [rtab[:, :, m] for m in range(3)])
                nc.vector.memset(rest[:, 0:1], 0.0).then_inc(s_tab, 1)

                def one_hot(i, q):
                    n = NQ * i + q
                    dve.wait_ge(s_low[q], 16 * LOWS * (i + 1))
                    after(dve, s_mm, n - 1)
                    for m, (x, p) in enumerate(((0, k.iota_part), (1, k.iota_part), (1, part2))):
                        nc.vector.tensor_scalar(hot[q % 2][:, m, :], low[q][:, x, :], p[:, 0:1], None,
                                                ALU.is_equal).then_inc(s_hot, 1)

                def total(n, h):
                    dve.wait_ge(s_mm, n + 1)
                    o = out_step[:, n * U:(n + 1) * U] if isinstance(n, int) else out_step[:, bass.ds(n * U, U)]
                    nc.vector.tensor_reduce(o, ps[h][:, :, 0:3], AX_X, ALU.add).then_inc(s_red, 1)

                def body(i):
                    for q in range(NQ):
                        one_hot(i, q)
                        if not (isinstance(i, int) and i == 0 and q == 0):
                            total(NQ * i + q - 1, (q - 1) % 2)
                turns(dve, NL, body)
                total(NQ * NL - 1, 1)

            @block.tensor
            def _(pe):
                pe.wait_ge(s_tab, 1)

                def body(i):
                    for q in range(NQ):
                        n = NQ * i + q
                        if q % 2 == 0:
                            two = blocks_of(k, mybir.EngineType.PE, 2 * i + q // 2, 2 * U)
                        blocks = two[(q % 2) * U:(q % 2 + 1) * U]
                        pe.wait_ge(s_hot, (n + 1) * KINDS)
                        after(pe, s_red, n - 1)
                        for u in range(U):
                            o = ps[q % 2][:, u, 0:3]
                            hots = hot[q % 2][:, :, u * P:(u + 1) * P]
                            last = nc.tensor.matmul(o, hots[:, 0, :],
                                                    tab[:, bass.ds(blocks[u], 1), :].rearrange("p b m -> p (b m)"),
                                                    start=True, stop=False)
                            for m in range(1, KINDS):
                                last = nc.tensor.matmul(o, hots[:, m, :], rtab[:, m - 1, :], start=False,
                                                        stop=(m == KINDS - 1))
                        last.then_inc(s_mm, 1)
                turns(pe, NL, body)


def softmax_weights(k, C, es, most, both, ed, wx):
    k.phase()
    nc, sb, sem = k.nc, k.sb, k.sem
    with ExitStack() as ctx:
        ahead = sb(ctx, "ahead", [ROWS, C, RW])
        cut = [sb(ctx, f"cut{d}", [ROWS, RW]) for d in range(2)]
        on = sb(ctx, "handed_on", [ROWS, 2 * C])
        cutmin = sb(ctx, "cutmin", [ROWS, 1])
        on_t = sb(ctx, "handed_on_t", [C, 2, ROWS])
        run = sb(ctx, "run", [C, 2, ROWS + 1])
        carry = sb(ctx, "carry", [ROWS, 2, C])
        tps = [k.psum(ctx, f"tps{i}", [P, P]) for i in range(3)]
        pair = [k.psum(ctx, f"pair{i}", [P, 2, 512]) for i in range(2)]
        s_exp, s_ev, s_u, s_w = sem("expanded"), sem("expanded_read"), sem("exponent"), sem("weight")
        s_most = sem("most_ready")
        s_dve, s_on, s_tp, s_run, s_cp = sem("dve"), sem("handed_on"), sem("turned"), sem("run"), sem("carry_turned")
        with nc.Block() as block:

            @block.vector
            def _(dve):
                link = Chain(dve, s_dve)
                link(nc.vector.tensor_scalar(cut[0][:, :], k.first_row[:, :], -BIG, None, ALU.mult))
                link(nc.vector.tensor_scalar(cut[1][:, :], k.last_row[:, :], -BIG, None, ALU.mult))
                link(nc.vector.memset(run[:, :, :], -BIG))
                for d in range(2):
                    way = slice(None, None, -1) if d else slice(None)
                    end = 0 if d else RW - 1
                    src, dst = (ahead, most) if d else (es, ahead)
                    for c in range(C):
                        link(nc.vector.tensor_tensor_scan(dst[:, c, way], cut[d][:, way], src[:, c, way], -BIG,
                                                          ALU.add, ALU.max))
                    link(nc.vector.tensor_reduce(cutmin[:, :], cut[d][:, :], AX_X, ALU.min))
                    link(nc.vector.tensor_copy(on[:, C:2 * C], cutmin[:, 0:1].to_broadcast([ROWS, C])))
                    nc.vector.tensor_copy(on[:, 0:C], dst[:, :, end]).then_inc(s_on, 1)
                    dve.wait_ge(s_tp, 2 * (d + 1))
                    for m in range(2):
                        link(nc.vector.tensor_copy(on_t[:, m, :], tps[m][0:C, 0:ROWS]))
                    o = run[:, d, 0:ROWS] if d else run[:, d, 1:ROWS + 1]
                    nc.vector.tensor_tensor_scan(o[:, way], on_t[:, 1, way], on_t[:, 0, way], -BIG,
                                                 ALU.add, ALU.max).then_inc(s_run, 1)
                    dve.wait_ge(s_cp, d + 1)
                    link(nc.vector.tensor_copy(carry[:, d, :], tps[2][0:ROWS, 0:C]))
                    for c in range(C):
                        link(nc.vector.tensor_tensor_scan(dst[:, c, way], cut[d][:, way], src[:, c, way],
                                                          carry[:, d, c:c + 1], ALU.add, ALU.max))
                nc.vector.memset(cutmin[:, :], 0.0).then_inc(s_most, 1)

                def leaky(q):
                    dve.wait_ge(s_ev, q + 1)
                    link(nc.vector.tensor_tensor(both[:, q, :], both[:, q, :], ed[:, :, q % C], ALU.add))
                    link(nc.vector.scalar_tensor_tensor(out=both[:, q, :], in0=both[:, q, :], scalar=0.2,
                                                        in1=both[:, q, :], op0=ALU.mult, op1=ALU.max))
                for c in range(C):
                    leaky(c)
                for c in range(C):
                    leaky(C + c)
                    nc.vector.tensor_tensor(both[:, c, :], both[:, c, :], both[:, C + c, :], ALU.subtract).then_inc(s_u, 1)
                    link(nc.vector.tensor_tensor(wx[:, :, C + c], both[:, C + c, :], k.first_step[:, :], ALU.mult))

            @block.tensor
            def _(pe):
                def expand(q):
                    row = es[:, q, :] if q < C else most[:, q - C, :]
                    after(pe, s_ev, q - 1)
                    for g in range(TPR):
                        for h in range(2):
                            last = nc.tensor.matmul(pair[q % 2][:, h, 0:HALF], row[:, g * P:(g + 1) * P],
                                                    k.steptile[:, g, h * HALF:(h + 1) * HALF],
                                                    start=(g == 0), stop=(g == TPR - 1))
                    last.then_inc(s_exp, 1)

                def hand_on(d):
                    pe.wait_ge(s_on, d + 1)
                    for m in range(2):
                        nc.tensor.transpose(tps[m][0:C, 0:ROWS], on[:, m * C:(m + 1) * C],
                                            k.ident[0:ROWS, 0:ROWS]).then_inc(s_tp, 1)
                    pe.wait_ge(s_run, d + 1)
                    o = run[:, d, 1:ROWS + 1] if d else run[:, d, 0:ROWS]
                    nc.tensor.transpose(tps[2][0:ROWS, 0:C], o, k.ident[0:C, 0:C]).then_inc(s_cp, 1)

                expand(0)
                hand_on(0)
                if C > 1:
                    expand(1)
                hand_on(1)
                for q in range(2, C):
                    expand(q)
                pe.wait_ge(s_most, 1)
                for q in range(C, 2 * C):
                    expand(q)

            @block.scalar
            def _(act):
                def read(q):
                    act.wait_ge(s_exp, q + 1)
                    nc.scalar.activation(both[:, q, :].rearrange("p (a s) -> p a s", a=2), pair[q % 2][:, :, 0:HALF],
                                         ACT.Copy).then_inc(s_ev, 1)

                def weight(c):
                    act.wait_ge(s_u, c + 1)
                    nc.scalar.activation(wx[:, :, c], both[:, c, :], ACT.Exp).then_inc(s_w, 1)

                for q in range(2 * C):
                    read(q)
                    if q > C:
                        weight(q - C - 1)
                weight(C - 1)


class Residual:

    def __init__(self, k, ctx):
        self.k = k
        self.x = k.sb(ctx, "x_all", [P, NB, D])
        self.b2 = k.sb(ctx, "b2_row", [P, D])

    def load(self, sp, s_zero, s_in):
        k = self.k
        sp.wait_ge(s_zero, 1)
        load_nodes(k, sp, k.a["x"], self.x, s_in)
        sp.dma_start(self.b2[:, :], k.a["L0_gnn_b2"].partition_broadcast(P)).then_inc(s_in, 16)
        sp.wait_ge(s_in, 16 * 3)


def gat_layer(k, ctx, C, rows_d, es_d, ends=False):
    W = D + 2 * C
    acc = k.sb(ctx, "acc", [P, NB, W])
    flat = acc[:, :, :].rearrange("p b w -> p (b w)")
    both = flat[:, 0:2 * C * STEPS].rearrange("p (c s) -> p c s", c=2 * C)
    ed = flat[:, 2 * C * STEPS:3 * C * STEPS].rearrange("p (s c) -> p s c", c=C)
    assert 3 * C * STEPS <= NB * W
    wx = k.sb(ctx, "wx", [P, STEPS, 2 * C])
    with ExitStack() as c2:
        es_row = k.sb(c2, "es_row", [ROWS, C, RW])
        most_row = k.sb(c2, "most_row", [ROWS, C, RW])
        lookups(k, C, k.node_s[:, 0:C, :], es_d, es_row, k.node_s[:, HEADS:HEADS + C, :], ed)
        softmax_weights(k, C, es_row, most_row, both, ed, wx)
    residual = Residual(k, ctx) if ends else None
    row_steps(k, C, rows_d, acc, wx, residual)
    return acc, residual


def indices(k, act, idx, s_idx, s_row, i, h):
    for u in range(h * H, (h + 1) * H):
        after(act, s_row[u], 16 * i)
    s = i * U + h * H
    settled(act, k.passed)
    k.nc.scalar.activation(idx[:, h * H:(h + 1) * H],
                           k.src_step[:, s:s + H] if isinstance(s, int) else k.src_step[:, bass.ds(s, H)],
                           ACT.Copy).then_inc(s_idx, 1)


def hand_indices(k, act, idx, s_idx, s_row, i, u):
    if u == 0:
        indices(k, act, idx, s_idx, s_row, i, 1)
    if u == H and not (isinstance(i, int) and i == TURNS - 1):
        indices(k, act, idx, s_idx, s_row, i + 1, 0)


def row_steps(k, C, rows_d, acc, wx, residual):
    k.phase()
    nc, sb, sem = k.nc, k.sb, k.sem
    W = D + 2 * C
    with ExitStack() as ctx:
        rows = sb(ctx, "rows", [P, U, D])
        weighed = sb(ctx, "weighed", [P, U, W])
        hot = sb(ctx, "hot", [P, U, P])
        idx = sb(ctx, "idx", [P, U], I32)
        ps = [k.psum(ctx, f"sum{i}", [P, 512]) for i in range(4)]
        s_idx = sem("indices")
        s_row = [sem(f"row_in{u}") for u in range(U)]
        s_hot, s_wt, s_wc, s_mm, s_acc, s_zero = (sem("hot"), sem("weighed"), sem("weights_copied"), sem("summed"),
                                                  sem("added"), sem("zeroed"))
        s_xzero, s_res = sem("residual_zeroed"), sem("residual_in")
        with nc.Block() as block:

            @block.sync
            def _(sp):
                if residual is not None:
                    residual.load(sp, s_xzero, s_res)

            @block.gpsimd
            def _(pool):
                if residual is not None:
                    nc.gpsimd.memset(residual.x[:, NFULL, :], 0.0).then_inc(s_xzero, 1)

                def body(i):
                    for u in range(U):
                        n = i * U + u
                        if u % H == 0:
                            pool.wait_ge(s_idx, 2 * i + u // H + 1)
                        after(pool, s_wt, n - U + 1)
                        settled(pool, k.passed)
                        pool.indirect_dma_start(
                            out=rows[:, u, :], out_offset=None, in_=rows_d,
                            in_offset=bass.IndirectOffsetOnAxis(ap=idx[:, u:u + 1], axis=0)).then_inc(s_row[u], 16)
                turns(pool, TURNS, body)

            @block.scalar
            def _(act):
                indices(k, act, idx, s_idx, s_row, 0, 0)

                def body(i):
                    for u in range(U):
                        n = i * U + u
                        hand_indices(k, act, idx, s_idx, s_row, i, u)
                        after(act, s_mm, n - U + 1)
                        w = wx[:, n, :] if isinstance(n, int) else wx[:, bass.ds(n, 1), :].rearrange("p o c -> p (o c)")
                        settled(act, k.passed)
                        nc.scalar.activation(weighed[:, u, D:W], w, ACT.Copy).then_inc(s_wc, 1)
                        if C == 1:
                            act.wait_ge(s_row[u], 16 * (i + 1))
                            settled(act, k.passed)
                            nc.scalar.activation(weighed[:, u, 0:D], rows[:, u, :], ACT.Copy,
                                                 scale=w[:, 0:1]).then_inc(s_wt, 1)
                turns(act, TURNS, body)

            @block.vector
            def _(dve):
                nc.vector.memset(acc[:, :, :], 0.0).then_inc(s_zero, 1)
                dve.wait_ge(s_zero, 1)

                def body(i):

                    def prepare(u):
                        n = i * U + u
                        after(dve, s_mm, n - U + 1)
                        d = k.dst_step[:, n:n + 1] if isinstance(n, int) else k.dst_step[:, bass.ds(n, 1)]
                        nc.vector.tensor_scalar(hot[:, u, :], k.iota_row[:, 0:P], d, None, ALU.is_equal).then_inc(s_hot, 1)
                        if C > 1:
                            dve.wait_ge(s_row[u], 16 * (i + 1))
                            w = wx[:, n:n + 1, 0:C] if isinstance(n, int) else wx[:, bass.ds(n, 1), 0:C]
                            nc.vector.tensor_tensor(
                                weighed[:, u, 0:D].rearrange("p (c e) -> p c e", c=C),
                                rows[:, u, :].rearrange("p (c e) -> p c e", c=C),
                                w.rearrange("p o c -> p c o").to_broadcast([P, C, D // C]), ALU.mult).then_inc(s_wt, 1)

                    def add(u, b):
                        n = i * U + u
                        dve.wait_ge(s_mm, n + 1)
                        after(dve, s_acc, n)
                        o = acc[:, bass.ds(b, 1), :].rearrange("p o w -> p (o w)")
                        nc.vector.tensor_tensor(o, o, ps[u % 4][:, 0:W],
                                                ALU.add).then_inc(s_acc, 1)

                    for u in range(U):
                        prepare(u)
                        if u == LAG - 1:
                            blocks = blocks_of(k, mybir.EngineType.DVE, i)
                        if u >= LAG:
                            add(u - LAG, blocks[u - LAG])
                    for u in range(U - LAG, U):
                        add(u, blocks[u])
                turns(dve, TURNS, body)

            @block.tensor
            def _(pe):
                def body(i):
                    for u in range(U):
                        n = i * U + u
                        pe.wait_ge(s_hot, n + 1)
                        pe.wait_ge(s_wt, n + 1)
                        pe.wait_ge(s_wc, n + 1)
                        after(pe, s_acc, n - 3)
                        nc.tensor.matmul(ps[u % 4][:, 0:W], hot[:, u, :], weighed[:, u, :],
                                         start=True, stop=True).then_inc(s_mm, 1)
                turns(pe, TURNS, body)



def softmax_end(k, C, acc, h_d, residual=None):
    k.phase()
    nc, sb, sem = k.nc, k.sb, k.sem
    with ExitStack() as ctx:
        hs = sb(ctx, "h_self", [P, SELFB, D])
        e, m, z, fe, fs = (sb(ctx, n, [P, C, SELFB]) for n in ("e_self", "e_most", "none", "f_edges", "f_self"))
        other = sb(ctx, "no_loop", [P, SELFB])
        loop = sb(ctx, "loop", [P, SELFB])
        coef = sb(ctx, "coef", [P, C, NB])
        s_b2 = sem("bias_added")
        s_dve, s_h, s_x, s_f = sem("dve"), sem("h_in"), sem("exponents"), sem("factors")
        first = slice(0, SELFB)
        with nc.Block() as block:

            @block.sync
            def _(sp):
                sp.dma_start(hs[:, :, :], h_d[0:SELFB * P, :].rearrange("(b p) d -> p b d", p=P)).then_inc(s_h, 16)

            @block.gpsimd
            def _(pool):
                if residual is not None:
                    nc.gpsimd.tensor_tensor(residual.x[:, :, :], residual.x[:, :, :],
                                            residual.b2[:, :].unsqueeze(1).to_broadcast([P, NB, D]), ALU.add).then_inc(s_b2, 1)

            @block.vector
            def _(dve):
                link = Chain(dve, s_dve)
                v = nc.vector
                den = acc[:, :, D:D + C].rearrange("p b c -> p c b")
                top = acc[:, first, D + C:D + 2 * C].rearrange("p b c -> p c b")
                link(v.memset(other[:, :], 0.0))
                link(v.tensor_scalar(other[:, SELFB - 1:SELFB], k.iota_part[:, :], SELF - (SELFB - 1) * P - 0.5, None, ALU.is_gt))
                link(v.tensor_scalar(loop[:, :], other[:, :], -1.0, 1.0, ALU.mult, ALU.add))
                link(v.tensor_tensor(e[:, :, :], k.node_s[:, 0:C, first], k.node_s[:, HEADS:HEADS + C, first], ALU.add))
                link(v.scalar_tensor_tensor(out=e[:, :, :], in0=e[:, :, :], scalar=0.2, in1=e[:, :, :], op0=ALU.mult, op1=ALU.max))
                for c in range(C):
                    link(v.scalar_tensor_tensor(out=e[:, c, :], in0=other[:, :], scalar=-BIG, in1=e[:, c, :],
                                                op0=ALU.mult, op1=ALU.add))
                link(v.tensor_scalar(z[:, :, :], den[:, :, first], 0.0, -BIG, ALU.is_equal, ALU.mult))
                link(v.tensor_tensor(m[:, :, :], top, z[:, :, :], ALU.add))
                link(v.tensor_tensor(z[:, :, :], m[:, :, :], e[:, :, :], ALU.max))
                link(v.tensor_tensor(m[:, :, :], m[:, :, :], z[:, :, :], ALU.subtract))
                v.tensor_tensor(e[:, :, :], e[:, :, :], z[:, :, :], ALU.subtract).then_inc(s_x, 1)
                link(v.tensor_copy(coef[:, :, :], den))
                dve.wait_ge(s_f, 2)
                for c in range(C):
                    link(v.tensor_tensor(fs[:, c, :], fs[:, c, :], loop[:, :], ALU.mult))
                link(v.tensor_tensor(coef[:, :, first], coef[:, :, first], fe[:, :, :], ALU.mult))
                link(v.tensor_tensor(coef[:, :, first], coef[:, :, first], fs[:, :, :], ALU.add))
                link(v.tensor_scalar(coef[:, :, :], coef[:, :, :], 1e-30, None, ALU.max))
                link(v.reciprocal(coef[:, :, :], coef[:, :, :]))
                link(v.tensor_tensor(fs[:, :, :], fs[:, :, :], coef[:, :, first], ALU.mult))
                link(v.tensor_tensor(coef[:, :, first], coef[:, :, first], fe[:, :, :], ALU.mult))
                dve.wait_ge(s_h, 16)
                for c in range(C):
                    o = slice(c * D // C, (c + 1) * D // C)
                    link(v.tensor_tensor(acc[:, :, o], acc[:, :, o], coef[:, c, :].unsqueeze(2).to_broadcast([P, NB, D // C]), ALU.mult))
                    link(v.tensor_tensor(hs[:, :, o], hs[:, :, o], fs[:, c, :].unsqueeze(2).to_broadcast([P, SELFB, D // C]), ALU.mult))
                link(v.tensor_tensor(acc[:, first, 0:D], acc[:, first, 0:D], hs[:, :, :], ALU.add))

            @block.scalar
            def _(act):
                act.wait_ge(s_x, 1)
                act.wait_ge(s_dve, 3 + 2 + C + 4)
                nc.scalar.activation(fe[:, :, :], m[:, :, :], ACT.Exp).then_inc(s_f, 1)
                nc.scalar.activation(fs[:, :, :], e[:, :, :], ACT.Exp).then_inc(s_f, 1)


def norm_factors(k, dve, link, x, stats, mean, rstd, s_var, s_root):
    v = k.nc.vector
    with dve.Fori(0, NODE_TURNS) as i:
        for u in range(NODE_U):
            n = i * NODE_U + u
            v.bn_stats(at(stats, n), at(x, n)).then_inc(s_var, 1)
    dve.wait_ge(s_var, NB)
    me, ve, mo, vo = (stats[:, :, q] for q in (1, 2, 4, 5))
    link(v.tensor_tensor(mean, me, mo, ALU.subtract))
    link(v.tensor_tensor(mean, mean, mean, ALU.mult))
    link(v.tensor_tensor(rstd, ve, vo, ALU.add))
    link(v.tensor_scalar(rstd, rstd, 1.0 / D, EPS, ALU.mult, ALU.add))
    link(v.scalar_tensor_tensor(out=rstd, in0=mean, scalar=0.25, in1=rstd, op0=ALU.mult, op1=ALU.add))
    link(v.tensor_tensor(mean, me, mo, ALU.add))
    v.tensor_scalar(mean, mean, 0.5, None, ALU.mult).then_inc(s_var, 1)
    dve.wait_ge(s_var, NB + 1)
    dve.wait_ge(s_root, 1)
    link(v.reciprocal(rstd, rstd))


def at(x, n):
    return x[:, n, :] if isinstance(n, int) else x[:, bass.ds(n, 1), :].rearrange("p o d -> p (o d)")


def col3(x, n):
    return x[:, :, n] if isinstance(n, int) else x[:, :, bass.ds(n, 1)].rearrange("p q o -> p (q o)")


def col(x, n):
    return x[:, n:n + 1] if isinstance(n, int) else x[:, bass.ds(n, 1)]


def gat_epilogue_1(k, acc):
    nc, sb, sem = k.nc, k.sb, k.sem
    softmax_end(k, HEADS, acc, k.h1_d)
    k.phase()
    W = D + 2
    with ExitStack() as ctx:
        w = sb(ctx, "w2x", [P, 2, W])
        av = sb(ctx, "a2_rows", [P, 2, D])
        wa = sb(ctx, "w2_times_a", [P, 2, D])
        vec = sb(ctx, "affine", [P, 3, D])
        stats, mean, var, rstd = sb(ctx, "stats", [P, NB, 6]), sb(ctx, "mean", [P, NB]), sb(ctx, "var", [P, NB]), sb(ctx, "rstd", [P, NB])
        eps = sb(ctx, "zero", [P, 1])
        y = sb(ctx, "normed", [P, NODE_U, D])
        xin = sb(ctx, "xin", [P, NODE_U, D])
        hout = sb(ctx, "hout", [P, NODE_U, D])
        eout = sb(ctx, "eout", [P, NB, 1])
        xt = [sb(ctx, f"xt{i}", [P, 2, P]) for i in range(2)]
        tps = [k.psum(ctx, f"tps{i}", [P, 2, P]) for i in range(2)]
        ops = [k.psum(ctx, f"ops{i}", [P, 512]) for i in range(2)]
        s_w, s_wx, s_dve, s_var, s_root = sem("weights_in"), sem("weights_ready"), sem("dve"), sem("statistics"), sem("root")
        s_y, s_x, s_es = sem("normed"), sem("relu"), sem("es_stored")
        s_st = [sem(f"h_stored{u}") for u in range(NODE_U)]
        s_tp, s_xt, s_mm, s_out, s_ev = sem("turned"), sem("turned_copied"), sem("product"), sem("product_read"), sem("h_ready")
        with nc.Block() as block:

            @block.sync
            def _(sp):
                sp.dma_start(w[:, :, 0:D], k.a["L0_gnn_W2"].rearrange("(c p) n -> p c n", p=P)).then_inc(s_w, 16)
                for m, n in enumerate(("L0_gnn_a2_src", "L0_gnn_a2_dst")):
                    sp.dma_start(av[:, m, :], k.a[n].rearrange("h c -> (h c)").partition_broadcast(P)).then_inc(s_w, 16)
                for m, n in enumerate(("L0_gnn_b1", "L0_gnn_ln_g", "L0_gnn_ln_b")):
                    sp.dma_start(vec[:, m, :], k.a[n].partition_broadcast(P)).then_inc(s_w, 16)

                def body(i):
                    for u in range(NODE_U):
                        n = i * NODE_U + u
                        sp.wait_ge(s_ev, 2 * n + 2)
                        sp.dma_start(rows_of(k.h2_d, n), hout[:, u, :]).then_inc(s_st[u], 16)
                    store_turn(k, sp, k.es2_d, eout, i, s_es)
                turns(sp, NODE_TURNS, body)
                sp.wait_ge(s_es, 16 * NODE_TURNS)
                for u in range(NODE_U):
                    sp.wait_ge(s_st[u], 16 * NODE_TURNS)

            @block.vector
            def _(dve):
                link = Chain(dve, s_dve)
                v = nc.vector
                dve.wait_ge(s_w, 16 * 6)
                for m in range(2):
                    link(v.tensor_tensor(wa[:, :, :], w[:, :, 0:D], av[:, m:m + 1, :].to_broadcast([P, 2, D]), ALU.mult))
                    v.tensor_reduce(w[:, :, D + m:D + m + 1], wa[:, :, :].unsqueeze(2), AX_X, ALU.add).then_inc(s_wx, 1)
                    dve.wait_ge(s_wx, m + 1)
                link(v.tensor_tensor(acc[:, :, 0:D], acc[:, :, 0:D], vec[:, 0:1, :].to_broadcast([P, NB, D]), ALU.add))
                norm_factors(k, dve, link, acc[:, :, 0:D], stats, mean[:, :], rstd[:, :], s_var, s_root)

                def norm(i, u):
                    n = i * NODE_U + u
                    after(dve, s_x, n - NODE_U + 1)
                    v.tensor_scalar(y[:, u, :], at(acc, n)[:, 0:D], col(mean, n), col(rstd, n),
                                    ALU.subtract, ALU.mult).then_inc(s_y, 1)
                    dve.wait_ge(s_y, 3 * n + 1)
                    v.tensor_tensor(y[:, u, :], y[:, u, :], vec[:, 1, :], ALU.mult).then_inc(s_y, 1)
                    dve.wait_ge(s_y, 3 * n + 2)
                    v.tensor_tensor(y[:, u, :], y[:, u, :], vec[:, 2, :], ALU.add).then_inc(s_y, 1)

                def copy(i, u):
                    n = i * NODE_U + u
                    dve.wait_ge(s_tp, n + 1)
                    after(dve, s_mm, n - 1 if u else n)
                    v.tensor_copy(xt[u % 2][:, :, :], tps[u % 2][:, :, :]).then_inc(s_xt, 1)

                node_turns(dve, [(2, norm)], copy)

            @block.tensor
            def _(pe):
                pe.wait_ge(s_wx, 2)
                pe_project(k, pe, xin, NODE_U, lambda e, i, u: e.wait_ge(s_x, i * NODE_U + u + 1), tps, s_tp, s_xt, xt,
                           [(0, [(c, w[:, c, :]) for c in range(2)])], ops, s_mm, s_out, [(0, P), (P, P)])

            @block.scalar
            def _(act):
                act.wait_ge(s_var, NB + 1)
                nc.scalar.activation(rstd[:, :], rstd[:, :], ACT.Sqrt).then_inc(s_root, 1)

                def relu(i, u):
                    n = i * NODE_U + u
                    act.wait_ge(s_y, 3 * n + 3)
                    after(act, s_tp, n - NODE_U + 1)
                    nc.scalar.activation(xin[:, u, :], y[:, u, :], ACT.Relu).then_inc(s_x, 1)

                def read(i, u):
                    n = i * NODE_U + u
                    act.wait_ge(s_mm, n + 1)
                    after(act, s_st[u], 16 * i)
                    nc.scalar.activation(hout[:, u, :], ops[u % 2][:, 0:D], ACT.Copy).then_inc(s_ev, 1)
                    nc.scalar.activation(at(eout, n), ops[u % 2][:, D:D + 1], ACT.Copy).then_inc(s_ev, 1)
                    o = k.node_s[:, 0:2 * HEADS:HEADS, n:n + 1] if isinstance(n, int) else k.node_s[:, 0:2 * HEADS:HEADS, bass.ds(n, 1)]
                    nc.scalar.activation(o, ops[u % 2][:, D:W].rearrange("p (c o) -> p c o", o=1), ACT.Copy).then_inc(s_out, 1)

                node_turns(act, [(2, relu)], read)


def load_nodes(k, sp, x_d, tile, s):
    sp.dma_start(tile[:, 0:NFULL, :], x_d[0:NFULL * P, :].rearrange("(b p) d -> p b d", p=P)).then_inc(s, 16)
    sp.dma_start(tile[0:NLAST, NFULL, :], x_d[NFULL * P:N, :]).then_inc(s, 16)


def gat_epilogue_2(k, acc, residual):
    nc, sb, sem = k.nc, k.sb, k.sem
    softmax_end(k, 1, acc, k.h2_d, residual)
    k.phase()
    with ExitStack() as ctx:
        x = residual.x
        w3 = sb(ctx, "w3", [P, 6, 3 * D])
        arow = sb(ctx, "a_row", [P, 3 * D])
        wv = sb(ctx, "w3_a", [P, 6])
        wb = sb(ctx, "w3_a_wide", [P, 2, P])
        rel = sb(ctx, "rel_rows", [P, 2, D])
        wl = sb(ctx, "loop_weights", [P, 2, 2 * D])
        some = sb(ctx, "has_edges", [P, 2, NB])
        mix = sb(ctx, "loop_messages", [P, 2, 2, D])
        wrow = sb(ctx, "w_rel_row", [P, D])
        w = sb(ctx, "w_cols", [P, 2, 2])
        stats, mean, rstd = sb(ctx, "stats", [P, NB, 6]), sb(ctx, "mean", [P, NB]), sb(ctx, "rstd", [P, NB])
        xin = sb(ctx, "xin", [P, NODE_U, D + 1])
        xt = [sb(ctx, f"xt{i}", [P, 2, P]) for i in range(2)]
        tps = [k.psum(ctx, f"tps{i}", [P, 2, P]) for i in range(2)]
        ops = [k.psum(ctx, f"ops{i}", [P, 1024]) for i in range(2)]
        wps = k.psum(ctx, "w_row_ps", [P, 2, P])
        s_in, s_zero, s_dve, s_var, s_root = sem("in"), sem("zeroed"), sem("dve"), sem("statistics"), sem("root")
        s_join, s_xl, s_mixed = sem("x1_and_loop"), sem("x1_and_loop_stored"), sem("loop_messages")
        s_wb, s_wp, s_x = sem("w_wide"), sem("w_row"), sem("normed")
        s_st = [sem(f"x1_stored{u}") for u in range(NODE_U)]
        s_tp, s_xt, s_mm, s_out, s_sc = (sem("turned"), sem("turned_copied"), sem("product"), sem("product_read"),
                                         sem("score_beside"))
        with nc.Block() as block:

            @block.gpsimd
            def _(pool):
                nc.gpsimd.memset(rel[:, :, :], 0.0).then_inc(s_zero, 1)

            @block.sync
            def _(sp):
                sp.dma_start(w3[:, :, :], k.a["L1_gnn_W3"].rearrange("(q p) n -> p q n", p=P)).then_inc(s_in, 16)
                sp.dma_start(arow[:, :], k.a["L1_gnn_a"].rearrange("n o -> (n o)").partition_broadcast(P)).then_inc(s_in, 16)
                sp.wait_ge(s_zero, 1)
                sp.dma_start(rel[:, 0, :], k.a["L1_gnn_rel_emb"][0:P, :]).then_inc(s_in, 16)
                sp.dma_start(rel[0:REL - P, 1, :], k.a["L1_gnn_rel_emb"][P:REL, :]).then_inc(s_in, 16)
                for m, n in enumerate(("L1_gnn_loop_weight", "L1_gnn_evolve_loop_weight")):
                    sp.dma_start(wl[:, :, m * D:(m + 1) * D], k.a[n].rearrange("(c p) n -> p c n", p=P)).then_inc(s_in, 16)

                def body(i):
                    for u in range(NODE_U):
                        n = i * NODE_U + u
                        sp.wait_ge(s_sc, n + 1)
                        sp.wait_ge(s_x, n + 1)
                        sp.dma_start(rows_of(k.x1_d, n), xin[:, u, :]).then_inc(s_st[u], 16)
                    sp.wait_ge(s_join, 2 * NODE_U * (i + 1))
                    store_turn(k, sp, k.xl_d, x, i, s_xl)
                turns(sp, NODE_TURNS, body)
                sp.wait_ge(s_xl, 16 * NODE_TURNS)
                for u in range(NODE_U):
                    sp.wait_ge(s_st[u], 16 * NODE_TURNS)

            @block.vector
            def _(dve):
                link = Chain(dve, s_dve)
                v = nc.vector
                link(v.tensor_scalar(some[:, 0, :], acc[:, :, D], 0.0, None, ALU.is_gt))
                link(v.tensor_scalar(some[:, 1, :], some[:, 0, :], -1.0, 1.0, ALU.mult, ALU.add))
                link(v.tensor_tensor(x[:, :, :], x[:, :, :], acc[:, :, 0:D], ALU.add))
                dve.wait_ge(s_in, 16 * 6)
                link(v.tensor_tensor(w3[:, :, :], w3[:, :, :], arow[:, :].unsqueeze(1).to_broadcast([P, 6, 3 * D]), ALU.mult))
                link(v.tensor_reduce(wv[:, :], w3[:, :, :], AX_X, ALU.add))
                for q in range(2):
                    v.tensor_copy(wb[:, q, :], wv[:, 4 + q:5 + q].to_broadcast([P, P])).then_inc(s_wb, 1)
                v.tensor_copy(w[:, :, :], wv[:, 0:4].rearrange("p (m c) -> p c m", m=2)).then_inc(s_wb, 1)
                dve.wait_ge(s_wp, 1)
                link(v.tensor_copy(wrow[:, :], wps[:, :, :].rearrange("p q n -> p (q n)")))
                link(v.tensor_tensor(rel[:, :, :], rel[:, :, :], wrow[:, :].unsqueeze(1).to_broadcast([P, 2, D]), ALU.mult))
                link(v.tensor_reduce(k.srel[:, :], rel[:, :, :], AX_X, ALU.add))
                norm_factors(k, dve, link, x, stats, mean[:, :], rstd[:, :], s_var, s_root)

                def norm(i, u):
                    n = i * NODE_U + u
                    after(dve, s_tp, n - NODE_U + 1)
                    after(dve, s_st[u], 16 * i)
                    v.tensor_scalar(xin[:, u, 0:D], at(x, n), col(mean, n), col(rstd, n),
                                    ALU.subtract, ALU.mult).then_inc(s_x, 1)

                def copy(i, u):
                    n = i * NODE_U + u
                    dve.wait_ge(s_tp, n + 1)
                    after(dve, s_mm, n - 1 if u else n)
                    v.tensor_copy(xt[u % 2][:, :, :], tps[u % 2][:, :, :]).then_inc(s_xt, 1)

                def join(i, u):
                    n = i * NODE_U + u
                    dve.wait_ge(s_mixed, 2 * n + 2)
                    xn = at(x, n)
                    v.tensor_tensor(xn, xin[:, u, 0:D], mix[:, u % 2, 0, :], ALU.add).then_inc(s_join, 1)
                    dve.wait_ge(s_join, 2 * n + 1)
                    v.tensor_tensor(xn, xn, mix[:, u % 2, 1, :], ALU.add).then_inc(s_join, 1)

                node_turns(dve, [(3, norm), (1, copy)], join)

            @block.tensor
            def _(pe):
                pe.wait_ge(s_wb, 3)
                pe.wait_ge(s_in, 16 * 6)
                for q in range(2):
                    last = nc.tensor.matmul(wps[:, q, :], wb[:, q, :], k.ident[:, :], start=True, stop=True)
                last.then_inc(s_wp, 1)
                pe_project(k, pe, xin, NODE_U, lambda e, i, u: e.wait_ge(s_x, i * NODE_U + u + 1), tps, s_tp, s_xt, xt,
                           [(0, [(c, wl[:, c, :]) for c in range(2)]), (512, [(c, w[:, c, :]) for c in range(2)])], ops, s_mm, s_out, [(0, P), (P, P)])

            @block.scalar
            def _(act):
                act.wait_ge(s_var, NB + 1)
                nc.scalar.activation(rstd[:, :], rstd[:, :], ACT.Sqrt).then_inc(s_root, 1)

                def body(i):
                    for u in range(NODE_U):
                        n = i * NODE_U + u
                        act.wait_ge(s_mm, n + 1)
                        after(act, s_st[u], 16 * i)
                        after(act, s_join, 2 * (n - 1 if u else n))
                        settled(act, k.passed)
                        for m in range(2):
                            nc.scalar.activation(mix[:, u % 2, m, :], ops[u % 2][:, m * D:(m + 1) * D], ACT.Copy,
                                                 scale=col(some[:, m, :], n)).then_inc(s_mixed, 1)
                        nc.scalar.activation(xin[:, u, D:D + 1], ops[u % 2][:, 512:513], ACT.Copy).then_inc(s_sc, 1)
                        nc.scalar.activation(col(k.node_s[:, HEADS, :], n), ops[u % 2][:, 513:514], ACT.Copy).then_inc(s_out, 1)
                turns(act, NODE_TURNS, body)


ONE_HOT = D + 1
ONES = ONE_HOT + REL
RW_COLS = ONES + 1


def relation_layer(k, ctx):
    acc = k.sb(ctx, "acc", [P, NB, RW_COLS])
    with ExitStack() as inner:
        rest_of_score = k.sb(inner, "rest_of_score", [P, STEPS])
        lookup_dst(k, k.node_s[:, HEADS, :], rest_of_score, k.srel[:, :])
        relation_steps(k, acc, rest_of_score)
    return acc


def relation_steps(k, acc, rest_of_score):
    k.phase()
    nc, sb, sem = k.nc, k.sb, k.sem
    W = RW_COLS
    with ExitStack() as ctx:
        rows = sb(ctx, "rows", [P, U, W])
        hot = sb(ctx, "hot", [P, U, P])
        idx = sb(ctx, "idx", [P, U], I32)
        part = sb(ctx, "score", [P, 4, QS])
        inv = sb(ctx, "inverse", [P, 4, QS])
        alpha = sb(ctx, "alpha", [P, 4, QS])
        away = sb(ctx, "distance", [P, 2, REL])
        ps = [k.psum(ctx, f"sum{i}", [P, 512]) for i in range(4)]
        s_idx = sem("indices")
        s_row = [sem(f"row_in{u}") for u in range(U)]
        s_hot, s_rel, s_mm, s_acc, s_zero = sem("hot"), sem("relation_hot"), sem("summed"), sem("added"), sem("zeroed")
        s_sum, s_score, s_exp, s_inv, s_alpha, s_away = (sem("score_sum"), sem("score"), sem("exp"), sem("inverse"),
                                                         sem("alpha"), sem("distance"))
        with nc.Block() as block:

            @block.gpsimd
            def _(pool):
                def body(i):
                    for u in range(U):
                        n = i * U + u
                        if u % H == 0:
                            pool.wait_ge(s_idx, 2 * i + u // H + 1)
                        after(pool, s_mm, n - U + 1)
                        settled(pool, k.passed)
                        pool.indirect_dma_start(
                            out=rows[:, u, 0:D + 1], out_offset=None, in_=k.x1_d,
                            in_offset=bass.IndirectOffsetOnAxis(ap=idx[:, u:u + 1], axis=0)).then_inc(s_row[u], 16)
                turns(pool, TURNS, body)

            @block.scalar
            def _(act):
                indices(k, act, idx, s_idx, s_row, 0, 0)
                indices(k, act, idx, s_idx, s_row, 0, 1)

                def body(i):
                    for u in range(U):
                        n = i * U + u
                        after(act, s_mm, n - U + 1)
                        settled(act, k.passed)
                        nc.scalar.activation(away[:, u % 2, :], k.iota_row[:, 0:REL], ACT.Abs, scale=-1.0,
                                             bias=col(k.et_step, n)).then_inc(s_away, 1)
                        act.wait_ge(s_away, n + 1)
                        nc.scalar.activation(rows[:, u, ONE_HOT:ONES], away[:, u % 2, :], ACT.Relu, scale=-1.0,
                                             bias=1.0).then_inc(s_rel, 1)
                        if u % QS == QS - 1:
                            g = u // QS
                            act.wait_ge(s_score, 4 * i + g + 1)
                            nc.scalar.activation(part[:, g, :], part[:, g, :], ACT.Exp).then_inc(s_exp, 1)
                        if u % H == H - 1 and not (isinstance(i, int) and i == TURNS - 1):
                            indices(k, act, idx, s_idx, s_row, i + 1, u // H)
                turns(act, TURNS, body)

            @block.vector
            def _(dve):
                nc.vector.memset(acc[:, :, :], 0.0).then_inc(s_zero, 1)
                nc.vector.memset(rows[:, :, ONES:W], 1.0).then_inc(s_zero, 1)
                dve.wait_ge(s_zero, 2)

                def score_sum(i, g):
                    s, us = i * U + g * QS, slice(g * QS, (g + 1) * QS)
                    for u in range(g * QS, (g + 1) * QS):
                        dve.wait_ge(s_row[u], 16 * (i + 1))
                    r = rest_of_score[:, s:s + QS] if isinstance(s, int) else rest_of_score[:, bass.ds(s, QS)]
                    nc.vector.tensor_tensor(part[:, g, :], rows[:, us, D], r, ALU.add).then_inc(s_sum, 1)

                def leaky(i, g):
                    dve.wait_ge(s_sum, 4 * i + g + 1)
                    nc.vector.scalar_tensor_tensor(out=part[:, g, :], in0=part[:, g, :], scalar=0.01,
                                                   in1=part[:, g, :], op0=ALU.mult, op1=ALU.max).then_inc(s_score, 1)

                def inverse(i, g):
                    dve.wait_ge(s_exp, 4 * i + g + 1)
                    nc.vector.reciprocal(inv[:, g, :], part[:, g, :]).then_inc(s_inv, 1)

                def weights(i, g):
                    t = 4 * i + g
                    dve.wait_ge(s_inv, t + 1)
                    after(dve, s_hot, (t - 3) * QS)
                    nc.vector.tensor_tensor(alpha[:, g, :], part[:, g, :], inv[:, g, :], ALU.mult).then_inc(s_alpha, 1)

                for stage in (score_sum, leaky, inverse, weights):
                    stage(0, 0)

                def body(i):

                    def prepare(u):
                        n = i * U + u
                        if u % QS == 0:
                            dve.wait_ge(s_alpha, 4 * i + u // QS + 1)
                        after(dve, s_mm, n - U + 1)
                        nc.vector.tensor_scalar(hot[:, u, :], k.iota_row[:, 0:P], col(k.dst_step, n),
                                                alpha[:, u // QS, u % QS:u % QS + 1],
                                                ALU.is_equal, ALU.mult).then_inc(s_hot, 1)

                    def add(u, b):
                        n = i * U + u
                        dve.wait_ge(s_mm, n + 1)
                        after(dve, s_acc, n)
                        o = at(acc, b)
                        nc.vector.tensor_tensor(o, o, ps[u % 4][:, 0:W], ALU.add).then_inc(s_acc, 1)

                    for u in range(U):
                        following = (i, u // QS + 1) if u + QS < U else (i + 1, 0)
                        more = u + QS < U or not (isinstance(i, int) and i == TURNS - 1)
                        prepare(u)
                        if u % QS == 1 and more:
                            score_sum(*following)
                        if u % QS == 3 and more:
                            weights(*following)
                        if u == LAG - 1:
                            blocks = blocks_of(k, mybir.EngineType.DVE, i)
                        if u >= LAG:
                            add(u - LAG, blocks[u - LAG])
                        if u % QS == 1 and more:
                            leaky(*following)
                        if u % QS == 2 and more:
                            inverse(*following)
                    for u in range(U - LAG, U):
                        add(u, blocks[u])
                turns(dve, TURNS, body)

            @block.tensor
            def _(pe):
                pe.wait_ge(s_zero, 2)

                def body(i):
                    for u in range(U):
                        n = i * U + u
                        pe.wait_ge(s_row[u], 16 * (i + 1))
                        pe.wait_ge(s_hot, n + 1)
                        pe.wait_ge(s_rel, n + 1)
                        after(pe, s_acc, n - 3)
                        nc.tensor.matmul(ps[u % 4][:, 0:W], hot[:, u, :], rows[:, u, :],
                                         start=True, stop=True).then_inc(s_mm, 1)
                turns(pe, TURNS, body)


def relation_epilogue(k, acc):
    k.phase()
    nc, sb, sem = k.nc, k.sb, k.sem
    chunks = [(0, P), (P, P), (ONE_HOT, P), (ONE_HOT + P, REL - P)]
    with ExitStack() as ctx:
        x = sb(ctx, "x1_and_loop", [P, NB, D])
        wn = sb(ctx, "w_neighbour", [P, 2, D])
        wr = sb(ctx, "rel_times_wn", [P, 2, D])
        stats, mean, rstd = sb(ctx, "stats", [P, NB, 6]), sb(ctx, "mean", [P, NB]), sb(ctx, "rstd", [P, NB])
        s_x1 = sem("x1_and_loop_in")
        s_in, s_dve, s_var, s_root = sem("in"), sem("dve"), sem("statistics"), sem("root")
        with ExitStack() as c2:
            rel = sb(c2, "rel_rows", [P, 2, D])
            relt = sb(c2, "rel_turned", [P, 2, 2 * P])
            rps = k.psum(c2, "rel_ps", [P, 2, 2, P])
            wps = [k.psum(c2, f"wr_ps{i}", [P, 512]) for i in range(2)]
            s_zero, s_rt, s_rc, s_wr = sem("zeroed"), sem("rel_turned"), sem("rel_copied"), sem("rel_product")
            with nc.Block() as block:

                @block.gpsimd
                def _(pool):
                    nc.gpsimd.memset(rel[:, :, :], 0.0).then_inc(s_zero, 1)

                @block.sync
                def _(sp):
                    sp.dma_start(wn[:, :, :], k.a["L1_gnn_weight_neighbor"].rearrange("(c p) n -> p c n", p=P)).then_inc(s_in, 16)
                    sp.wait_ge(s_zero, 1)
                    sp.dma_start(rel[:, 0, :], k.a["L1_gnn_rel_emb"][0:P, :]).then_inc(s_in, 16)
                    sp.dma_start(rel[0:REL - P, 1, :], k.a["L1_gnn_rel_emb"][P:REL, :]).then_inc(s_in, 16)
                    sp.wait_ge(s_in, 48)
                    sp.dma_start(x[:, :, :], k.xl_d.rearrange("(b p) d -> p b d", p=P)).then_inc(s_x1, 16)

                @block.tensor
                def _(pe):
                    pe.wait_ge(s_in, 48)
                    for r in range(2):
                        for c in range(2):
                            last = nc.tensor.transpose(rps[:, c, r, :], rel[:, r, c * P:(c + 1) * P], k.ident[:, :])
                    last.then_inc(s_rt, 1)
                    pe.wait_ge(s_rc, 1)
                    for r in range(2):
                        for c in range(2):
                            last = nc.tensor.matmul(wps[r][:, 0:D], relt[:, c, r * P:(r + 1) * P], wn[:, c, :],
                                                    start=(c == 0), stop=(c == 1))
                    last.then_inc(s_wr, 1)

                @block.vector
                def _(dve):
                    link = Chain(dve, s_dve)
                    dve.wait_ge(s_rt, 1)
                    nc.vector.tensor_copy(relt[:, :, :], rps[:, :, :, :].rearrange("p c r n -> p c (r n)")).then_inc(s_rc, 1)
                    dve.wait_ge(s_wr, 1)
                    for r in range(2):
                        link(nc.vector.tensor_copy(wr[:, r, :], wps[r][:, 0:D]))
        with ExitStack() as c2:
            xin = sb(c2, "xin", [P, 2, ONES])
            xt = [t[:, 0:4 * P].rearrange("p (c n) -> p c n", c=4) for t in (k.first_step, k.iota_row)]
            messages = [t[:, 0:D] for t in (k.dst_step, k.et_step)]
            s_x, s_tp, s_xt, s_mm, s_nb, s_lp, s_mix = (sem(n) for n in (
                "xin", "turned", "turned_copied", "product", "messages_read", "part_copied", "mixed"))
            with ExitStack() as c3:
                tps = [k.psum(c3, f"tps{i}", [P, 4, P]) for i in range(2)]
                ops = [k.psum(c3, f"ops{i}", [P, 512]) for i in range(2)]
                with nc.Block() as block:

                    @block.tensor
                    def _(pe):
                        ws = [wn[:, 0, :], wn[:, 1, :], wr[:, 0, :], wr[0:REL - P, 1, :]]
                        pe_project(k, pe, xin, 2, lambda e, i, u: e.wait_ge(s_x, i * NODE_U + u + 1), tps, s_tp, s_xt, xt,
                                   [(0, list(enumerate(ws)))], ops, s_mm, s_nb, chunks)

                    @block.scalar
                    def _(act):
                        def load(i, u):
                            n = i * NODE_U + u
                            after(act, s_tp, n - 1 if u else n)
                            settled(act, k.passed)
                            nc.scalar.activation(xin[:, u % 2, :], at(acc, n)[:, 0:ONES], ACT.Copy).then_inc(s_x, 1)

                        def read(i, u):
                            n = i * NODE_U + u
                            act.wait_ge(s_mm, n + 1)
                            after(act, s_mix, n - 1 if u else n)
                            nc.scalar.activation(messages[u % 2], ops[u % 2][:, 0:D], ACT.Relu).then_inc(s_nb, 1)

                        node_turns(act, [(2, load)], read)

                    @block.vector
                    def _(dve):
                        v = nc.vector

                        def copy(i, u):
                            n = i * NODE_U + u
                            dve.wait_ge(s_tp, n + 1)
                            after(dve, s_mm, n - 1 if u else n)
                            for lo, hi, p in ((0, 3, P), (3, 4, REL - P)):
                                last = v.tensor_copy(xt[u % 2][0:p, lo:hi, :], tps[u % 2][0:p, lo:hi, :])
                                if lo == 0:
                                    last.then_inc(s_lp, 1)
                            last.then_inc(s_xt, 1)

                        def join(i, u):
                            n = i * NODE_U + u
                            dve.wait_ge(s_nb, n + 1)
                            v.tensor_tensor(at(x, n), at(x, n), messages[u % 2], ALU.add).then_inc(s_mix, 1)

                        dve.wait_ge(s_x1, 16)
                        node_turns(dve, [(1, copy)], join)
        s_done, s_st = sem("normed"), sem("stored")
        y = acc[:, :, 0:D]
        with nc.Block() as block:

            @block.vector
            def _(dve):
                link = Chain(dve, s_dve, 2)
                norm_factors(k, dve, link, x, stats, mean[:, :], rstd[:, :], s_var, s_root)
                with dve.Fori(0, NODE_TURNS) as i:
                    for u in range(NODE_U):
                        n = i * NODE_U + u
                        nc.vector.tensor_scalar(at(y, n), at(x, n), col(mean, n), col(rstd, n),
                                                ALU.subtract, ALU.mult).then_inc(s_done, 1)

            @block.scalar
            def _(act):
                act.wait_ge(s_var, NB + 1)
                nc.scalar.activation(rstd[:, :], rstd[:, :], ACT.Sqrt).then_inc(s_root, 1)

            @block.sync
            def _(sp):
                for q in range(4):
                    lo, hi = q * 12, (q + 1) * 12
                    sp.wait_ge(s_done, hi)
                    sp.dma_start(k.out[lo * P:hi * P, :].rearrange("(b p) d -> p b d", p=P), y[:, lo:hi, :]).then_inc(s_st, 16)
                sp.wait_ge(s_done, NB)
                sp.dma_start(k.out[NFULL * P:N, :], y[0:NLAST, NFULL, :]).then_inc(s_st, 16)
                sp.wait_ge(s_st, 16 * 5)


_INS = ["x", "src", "dst", "edge_type_200", "L0_gnn_W1", "L0_gnn_a1_src", "L0_gnn_a1_dst", "L0_gnn_b1", "L0_gnn_ln_g",
        "L0_gnn_ln_b", "L0_gnn_W2", "L0_gnn_a2_src", "L0_gnn_a2_dst", "L0_gnn_b2", "L1_gnn_rel_emb",
        "L1_gnn_weight_neighbor", "L1_gnn_a", "L1_gnn_W3", "L1_gnn_loop_weight", "L1_gnn_evolve_loop_weight"]


def kernel(**inputs):
    import numpy as _np
    import concourse.bacc as _bacc
    from concourse import mybir as _mybir
    from concourse.bass_utils import run_bass_kernel_spmd as _run

    nc = _bacc.Bacc("TRN2", target_bir_lowering=False, num_devices=1)
    arrays, args = {}, {}
    for name in _INS:
        a = _np.ascontiguousarray(inputs[name])
        arrays[f"in_{name}_dram"] = a
        args[name] = nc.dram_tensor(f"in_{name}_dram", a.shape, _mybir.dt.from_np(a.dtype), kind="ExternalInput").ap()
    out = nc.dram_tensor("out_0_dram", (N, D), _mybir.dt.float32, kind="ExternalOutput").ap()
    program(nc, args, out)
    r = _run(nc, [arrays], core_ids=[0])
    return r.results[0]["out_0_dram"]
```
